# Optimizing a Trainium2 kernel written in Bass

```python
import numpy as np
import jax
import jax.numpy as jnp

def _softmax(x, axis=-1):
    return jax.nn.softmax(x, axis=axis)

def _gelu(x):
    return jax.nn.gelu(x, approximate=True)

def _silu(x):
    return jax.nn.silu(x)

def _sigmoid(x):
    return jax.nn.sigmoid(x)

def _layernorm(x, axis=-1, eps=1e-05):
    m = jnp.mean(x, axis=axis, keepdims=True)
    v = jnp.var(x, axis=axis, keepdims=True)
    return (x - m) / jnp.sqrt(v + eps)

def _scatter_add(tgt, idx, src, axis=0):
    return tgt.at[idx].add(src)

def _segment_sum(src, seg, n):
    return jax.ops.segment_sum(src, seg, n)
kernel_name = 'mk_metaformer_d4_conv_nchw128_r2_08458f'

def setup_inputs(seed: int=0):
    np.random.seed(seed)
    _w = jnp.asarray

    def _rec_inputs():
        import jax
        import jax.numpy as jnp
        _gk = jax.random.key(seed)
        x = -7.109e-05 + 0.9999 * jax.random.normal(jax.random.fold_in(_gk, 1), (4, 64, 128, 128), jnp.float32)
        return x
    x = _rec_inputs()

    def _L0_conv_setup():
        import jax, jax.numpy as jnp
        import numpy as np
        DIM = 64
        WS = 8
        NH = 4
        SHIFT = 4
        HD = DIM // NH
        SCALE = HD ** (-0.5)
        N = WS * WS

        def _rel_pos_index():
            coords = np.stack(np.meshgrid(np.arange(WS), np.arange(WS), indexing='ij'))
            cf = coords.reshape(2, -1)
            rel = (cf[:, :, None] - cf[:, None, :]).transpose(1, 2, 0)
            rel[:, :, 0] += WS - 1
            rel[:, :, 1] += WS - 1
            rel[:, :, 0] *= 2 * WS - 1
            return rel.sum(-1)

        def _shift_mask(H, W):
            img = np.zeros((H, W))
            cnt = 0
            for hs in (slice(0, -WS), slice(-WS, -SHIFT), slice(-SHIFT, None)):
                for ws in (slice(0, -WS), slice(-WS, -SHIFT), slice(-SHIFT, None)):
                    img[hs, ws] = cnt
                    cnt += 1
            mw = img.reshape(H // WS, WS, W // WS, WS).transpose(0, 2, 1, 3).reshape(-1, N)
            am = mw[:, None, :] - mw[:, :, None]
            return np.where(am != 0, -100.0, 0.0).astype(np.float32)
        key = jax.random.key(seed)
        ks = jax.random.split(key, 5)
        B, H, W = (8, 128, 128)
        x = jax.random.normal(ks[0], (B, DIM, H, W), dtype=jnp.float32)
        qkv_w = jax.random.normal(ks[1], (3 * DIM, DIM), dtype=jnp.float32) * DIM ** (-0.5)
        proj_w = jax.random.normal(ks[2], (DIM, DIM), dtype=jnp.float32) * DIM ** (-0.5)
        proj_b = jax.random.normal(ks[3], (DIM,), dtype=jnp.float32) * 0.01
        bias_table = jax.random.normal(ks[4], ((2 * WS - 1) ** 2, NH), dtype=jnp.float32) * 0.02
        return {'x': x, 'qkv_w': qkv_w, 'proj_w': proj_w, 'proj_b': proj_b, 'bias_table': bias_table}
    _L0_conv_all = _L0_conv_setup()
    _L0_conv_in = {k: v for k, v in _L0_conv_all.items() if k in ('qkv_w', 'proj_w', 'proj_b', 'bias_table')}
    del _L0_conv_all

    def _L0_ffn_setup():
        import jax, jax.numpy as jnp
        import numpy as np
        B, S, D, E, H, O, K = (256, 1024, 64, 32, 256, 64, 8)
        key = jax.random.key(seed)
        k0, k1, k2, k3 = jax.random.split(key, 4)
        x = jax.random.normal(k0, (B, S, D), dtype=jnp.float32)
        gate_w = jax.random.normal(k1, (E, D), dtype=jnp.float32) * (1.0 / np.sqrt(D))
        gate_b = jnp.zeros((E,), dtype=jnp.float32)
        weight1 = jax.random.uniform(k2, (E, D + 1, H), dtype=jnp.float32, minval=-1.0, maxval=1.0) * (1.0 / np.sqrt(D + 1))
        weight2 = jax.random.uniform(k3, (E, H + 1, O), dtype=jnp.float32, minval=-1.0, maxval=1.0) * (1.0 / np.sqrt(H + 1))
        return {'x': x, 'gate_w': gate_w, 'gate_b': gate_b, 'weight1': weight1, 'weight2': weight2}
    _L0_ffn_all = _L0_ffn_setup()
    _L0_ffn_in = {k: v for k, v in _L0_ffn_all.items() if k in ('gate_w', 'gate_b', 'weight1', 'weight2')}
    del _L0_ffn_all

    def _L1_conv_setup():
        import jax, jax.numpy as jnp
        import numpy as np
        BN_EPS = 1e-05

        def _ternary_weights(key, shape, sparsity):
            k1, k2 = jax.random.split(key)
            signs = jnp.where(jax.random.uniform(k1, shape) < 0.5, -1.0, 1.0)
            active = jax.random.uniform(k2, shape) <= 0.5
            return jnp.where(active, signs, 0.0).astype(jnp.float32)
        key = jax.random.key(seed)
        ks = jax.random.split(key, 5)
        B, C, H, W = (8, 64, 128, 128)
        Cout = 64
        x = jax.random.normal(ks[0], (B, C, H, W), dtype=jnp.float32)
        gamma = jnp.ones((C,), dtype=jnp.float32)
        beta = jnp.zeros((C,), dtype=jnp.float32)
        w_lbp = _ternary_weights(ks[1], (C, C, 3, 3), 0.5)
        fan_in = C * 1 * 1
        bound = 1.0 / np.sqrt(fan_in)
        w_1x1 = jax.random.uniform(ks[2], (Cout, C, 1, 1), minval=-bound, maxval=bound, dtype=jnp.float32)
        b_1x1 = jax.random.uniform(ks[3], (Cout,), minval=-bound, maxval=bound, dtype=jnp.float32)
        return {'x': x, 'gamma': gamma, 'beta': beta, 'w_lbp': w_lbp, 'w_1x1': w_1x1, 'b_1x1': b_1x1}
    _L1_conv_all = _L1_conv_setup()
    _L1_conv_in = {k: v for k, v in _L1_conv_all.items() if k in ('gamma', 'beta', 'w_lbp', 'w_1x1', 'b_1x1')}
    del _L1_conv_all

    def _L1_ffn_setup():
        import jax, jax.numpy as jnp
        import numpy as np
        B, N, D, C, E, K = (8, 4096, 64, 64, 8, 2)
        key = jax.random.key(seed)
        k0, k1, k2 = jax.random.split(key, 3)
        x = jax.random.normal(k0, (B, N, D), dtype=jnp.float32)
        router_w = jax.random.normal(k1, (D, E), dtype=jnp.float32) * 0.05
        router_b = jnp.zeros((E,), dtype=jnp.float32)
        expert_w = jax.random.normal(k2, (E, D, C), dtype=jnp.float32) * (1.0 / np.sqrt(D))
        expert_b = jnp.zeros((E, C), dtype=jnp.float32)
        return {'x': x, 'router_w': router_w, 'router_b': router_b, 'expert_w': expert_w, 'expert_b': expert_b}
    _L1_ffn_all = _L1_ffn_setup()
    _L1_ffn_in = {k: v for k, v in _L1_ffn_all.items() if k in ('router_w', 'router_b', 'expert_w', 'expert_b')}
    del _L1_ffn_all

    def _L2_conv_setup():
        import jax, jax.numpy as jnp
        import numpy as np
        from jax import lax
        B, C, H, W = (16, 64, 32, 80)
        KW, KH = (9, 9)
        PAD_W, PAD_H = ((KW - 1) // 2, (KH - 1) // 2)

        def _slice_conv(s, K, pad):
            kern = jnp.transpose(K[:, 0], (0, 2, 1))
            y = lax.conv_general_dilated(jnp.swapaxes(s, 1, 2), kern, (1,), [(pad, pad)])
            return jnp.swapaxes(y, 1, 2)

        def _sweep(x, K, pad, reverse):
            if reverse:
                x = x[:, ::-1]
            xs = jnp.swapaxes(x, 0, 1)

            def step(prev, xi):
                new = xi + jax.nn.relu(_slice_conv(prev, K, pad))
                return (new, new)
            _, rest = lax.scan(step, xs[0], xs[1:])
            out = jnp.swapaxes(jnp.concatenate([xs[:1], rest], axis=0), 0, 1)
            if reverse:
                out = out[:, ::-1]
            return out
        key = jax.random.key(seed)
        kx, k1, k2, k3, k4 = jax.random.split(key, 5)
        bw = 1.0 / float(np.sqrt(KW * C))
        bh = 1.0 / float(np.sqrt(KH * C))
        x = jax.random.normal(kx, (B, C, H, W), jnp.float32)
        kernel_td = jax.random.uniform(k1, (C, 1, KW, C), jnp.float32, -bw, bw)
        kernel_dt = jax.random.uniform(k2, (C, 1, KW, C), jnp.float32, -bw, bw)
        kernel_lr = jax.random.uniform(k3, (C, 1, KH, C), jnp.float32, -bh, bh)
        kernel_rl = jax.random.uniform(k4, (C, 1, KH, C), jnp.float32, -bh, bh)
        return {'x': x, 'kernel_td': kernel_td, 'kernel_dt': kernel_dt, 'kernel_lr': kernel_lr, 'kernel_rl': kernel_rl}
    _L2_conv_all = _L2_conv_setup()
    _L2_conv_in = {k: v for k, v in _L2_conv_all.items() if k in ('kernel_td', 'kernel_dt', 'kernel_lr', 'kernel_rl')}
    del _L2_conv_all

    def _L2_ffn_setup():
        import jax, jax.numpy as jnp
        import numpy as np
        B, S, D, E, H, O, K = (256, 1024, 64, 32, 256, 64, 8)
        key = jax.random.key(seed)
        k0, k1, k2, k3 = jax.random.split(key, 4)
        x = jax.random.normal(k0, (B, S, D), dtype=jnp.float32)
        gate_w = jax.random.normal(k1, (E, D), dtype=jnp.float32) * (1.0 / np.sqrt(D))
        gate_b = jnp.zeros((E,), dtype=jnp.float32)
        weight1 = jax.random.uniform(k2, (E, D + 1, H), dtype=jnp.float32, minval=-1.0, maxval=1.0) * (1.0 / np.sqrt(D + 1))
        weight2 = jax.random.uniform(k3, (E, H + 1, O), dtype=jnp.float32, minval=-1.0, maxval=1.0) * (1.0 / np.sqrt(H + 1))
        return {'x': x, 'gate_w': gate_w, 'gate_b': gate_b, 'weight1': weight1, 'weight2': weight2}
    _L2_ffn_all = _L2_ffn_setup()
    _L2_ffn_in = {k: v for k, v in _L2_ffn_all.items() if k in ('gate_w', 'gate_b', 'weight1', 'weight2')}
    del _L2_ffn_all

    def _L3_conv_setup():
        import jax, jax.numpy as jnp
        import numpy as np
        ITER = 4
        ALPHA = 2.0
        EPS = 0.001

        def _dwconv(x, w, dil, pad):
            return jax.lax.conv_general_dilated(x, w, window_strides=(1, 1), padding=((pad, pad), (pad, pad)), rhs_dilation=(dil, dil), dimension_numbers=('NCHW', 'OIHW', 'NCHW'), feature_group_count=x.shape[1])

        def _aspp(x, w, bn, dil):
            pad = 0 if dil == 1 else dil
            y = _dwconv(x, w, dil, pad)
            g, b, m, v = (bn[0], bn[1], bn[2], bn[3])
            scale = (g * jax.lax.rsqrt(v + EPS))[None, :, None, None]
            bias = (b - g * m * jax.lax.rsqrt(v + EPS))[None, :, None, None]
            return jax.nn.relu(y * scale + bias)
        key = jax.random.key(seed)
        ks = jax.random.split(key, 9)
        B, C, H, W = (32, 64, 36, 50)
        x = jax.random.normal(ks[0], (B, C, H, W), dtype=jnp.float32)
        w_d = 0.05 * jax.random.normal(ks[1], (ITER, C, 1, 1, 1), dtype=jnp.float32)
        w_u = 0.05 * jax.random.normal(ks[2], (ITER, C, 1, 3, 3), dtype=jnp.float32)
        w_r = 0.05 * jax.random.normal(ks[3], (ITER, C, 1, 3, 3), dtype=jnp.float32)
        w_l = 0.05 * jax.random.normal(ks[4], (ITER, C, 1, 3, 3), dtype=jnp.float32)

        def bn_params(k):
            k1, k2, k3, k4 = jax.random.split(k, 4)
            g = jax.random.uniform(k1, (ITER, C), minval=0.5, maxval=1.5)
            b = 0.1 * jax.random.normal(k2, (ITER, C))
            m = 0.1 * jax.random.normal(k3, (ITER, C))
            v = jax.random.uniform(k4, (ITER, C), minval=0.5, maxval=1.5)
            return jnp.stack([g, b, m, v], axis=1).astype(jnp.float32)
        return {'x': x, 'w_d': w_d, 'w_u': w_u, 'w_r': w_r, 'w_l': w_l, 'bn_d': bn_params(ks[5]), 'bn_u': bn_params(ks[6]), 'bn_r': bn_params(ks[7]), 'bn_l': bn_params(ks[8])}
    _L3_conv_all = _L3_conv_setup()
    _L3_conv_in = {k: v for k, v in _L3_conv_all.items() if k in ('w_d', 'w_u', 'w_r', 'w_l', 'bn_d', 'bn_u', 'bn_r', 'bn_l')}
    del _L3_conv_all

    def _L3_ffn_setup():
        import jax, jax.numpy as jnp
        import numpy as np
        B, N, D, C, E, K = (8, 4096, 64, 64, 8, 2)
        key = jax.random.key(seed)
        k0, k1, k2 = jax.random.split(key, 3)
        x = jax.random.normal(k0, (B, N, D), dtype=jnp.float32)
        router_w = jax.random.normal(k1, (D, E), dtype=jnp.float32) * 0.05
        router_b = jnp.zeros((E,), dtype=jnp.float32)
        expert_w = jax.random.normal(k2, (E, D, C), dtype=jnp.float32) * (1.0 / np.sqrt(D))
        expert_b = jnp.zeros((E, C), dtype=jnp.float32)
        return {'x': x, 'router_w': router_w, 'router_b': router_b, 'expert_w': expert_w, 'expert_b': expert_b}
    _L3_ffn_all = _L3_ffn_setup()
    _L3_ffn_in = {k: v for k, v in _L3_ffn_all.items() if k in ('router_w', 'router_b', 'expert_w', 'expert_b')}
    del _L3_ffn_all
    return {'x': x, 'L0_conv_qkv_w': _L0_conv_in['qkv_w'], 'L0_conv_proj_w': _L0_conv_in['proj_w'], 'L0_conv_proj_b': _L0_conv_in['proj_b'], 'L0_conv_bias_table': _L0_conv_in['bias_table'], 'L0_ffn_gate_w': _L0_ffn_in['gate_w'], 'L0_ffn_gate_b': _L0_ffn_in['gate_b'], 'L0_ffn_weight1': _L0_ffn_in['weight1'], 'L0_ffn_weight2': _L0_ffn_in['weight2'], 'L1_conv_gamma': _L1_conv_in['gamma'], 'L1_conv_beta': _L1_conv_in['beta'], 'L1_conv_w_lbp': _L1_conv_in['w_lbp'], 'L1_conv_w_1x1': _L1_conv_in['w_1x1'], 'L1_conv_b_1x1': _L1_conv_in['b_1x1'], 'L1_ffn_router_w': _L1_ffn_in['router_w'], 'L1_ffn_router_b': _L1_ffn_in['router_b'], 'L1_ffn_expert_w': _L1_ffn_in['expert_w'], 'L1_ffn_expert_b': _L1_ffn_in['expert_b'], 'L2_conv_kernel_td': _L2_conv_in['kernel_td'], 'L2_conv_kernel_dt': _L2_conv_in['kernel_dt'], 'L2_conv_kernel_lr': _L2_conv_in['kernel_lr'], 'L2_conv_kernel_rl': _L2_conv_in['kernel_rl'], 'L2_ffn_gate_w': _L2_ffn_in['gate_w'], 'L2_ffn_gate_b': _L2_ffn_in['gate_b'], 'L2_ffn_weight1': _L2_ffn_in['weight1'], 'L2_ffn_weight2': _L2_ffn_in['weight2'], 'L3_conv_w_d': _L3_conv_in['w_d'], 'L3_conv_w_u': _L3_conv_in['w_u'], 'L3_conv_w_r': _L3_conv_in['w_r'], 'L3_conv_w_l': _L3_conv_in['w_l'], 'L3_conv_bn_d': _L3_conv_in['bn_d'], 'L3_conv_bn_u': _L3_conv_in['bn_u'], 'L3_conv_bn_r': _L3_conv_in['bn_r'], 'L3_conv_bn_l': _L3_conv_in['bn_l'], 'L3_ffn_router_w': _L3_ffn_in['router_w'], 'L3_ffn_router_b': _L3_ffn_in['router_b'], 'L3_ffn_expert_w': _L3_ffn_in['expert_w'], 'L3_ffn_expert_b': _L3_ffn_in['expert_b']}

def reference(x, L0_conv_qkv_w, L0_conv_proj_w, L0_conv_proj_b, L0_conv_bias_table, L0_ffn_gate_w, L0_ffn_gate_b, L0_ffn_weight1, L0_ffn_weight2, L1_conv_gamma, L1_conv_beta, L1_conv_w_lbp, L1_conv_w_1x1, L1_conv_b_1x1, L1_ffn_router_w, L1_ffn_router_b, L1_ffn_expert_w, L1_ffn_expert_b, L2_conv_kernel_td, L2_conv_kernel_dt, L2_conv_kernel_lr, L2_conv_kernel_rl, L2_ffn_gate_w, L2_ffn_gate_b, L2_ffn_weight1, L2_ffn_weight2, L3_conv_w_d, L3_conv_w_u, L3_conv_w_r, L3_conv_w_l, L3_conv_bn_d, L3_conv_bn_u, L3_conv_bn_r, L3_conv_bn_l, L3_ffn_router_w, L3_ffn_router_b, L3_ffn_expert_w, L3_ffn_expert_b):
    import jax
    import jax.numpy as jnp

    def _L0_conv_ref(x, qkv_w, proj_w, proj_b, bias_table):
        import jax, jax.numpy as jnp
        import numpy as np
        DIM = 64
        WS = 8
        NH = 4
        SHIFT = 4
        HD = DIM // NH
        SCALE = HD ** (-0.5)
        N = WS * WS

        def _rel_pos_index():
            coords = np.stack(np.meshgrid(np.arange(WS), np.arange(WS), indexing='ij'))
            cf = coords.reshape(2, -1)
            rel = (cf[:, :, None] - cf[:, None, :]).transpose(1, 2, 0)
            rel[:, :, 0] += WS - 1
            rel[:, :, 1] += WS - 1
            rel[:, :, 0] *= 2 * WS - 1
            return rel.sum(-1)

        def _shift_mask(H, W):
            img = np.zeros((H, W))
            cnt = 0
            for hs in (slice(0, -WS), slice(-WS, -SHIFT), slice(-SHIFT, None)):
                for ws in (slice(0, -WS), slice(-WS, -SHIFT), slice(-SHIFT, None)):
                    img[hs, ws] = cnt
                    cnt += 1
            mw = img.reshape(H // WS, WS, W // WS, WS).transpose(0, 2, 1, 3).reshape(-1, N)
            am = mw[:, None, :] - mw[:, :, None]
            return np.where(am != 0, -100.0, 0.0).astype(np.float32)
        B, C, H, W = x.shape
        x = jnp.roll(x, (-SHIFT, -SHIFT), axis=(2, 3))
        qkv = jnp.einsum('bchw,oc->bohw', x, qkv_w)
        nWh, nWw = (H // WS, W // WS)
        nW = nWh * nWw
        qkv = qkv.reshape(B, 3, NH, HD, nWh, WS, nWw, WS)
        qkv = qkv.transpose(1, 0, 4, 6, 2, 5, 7, 3)
        qkv = qkv.reshape(3, B * nW, NH, N, HD)
        q, k, v = (qkv[0], qkv[1], qkv[2])
        attn = jnp.einsum('wnqd,wnkd->wnqk', q, k) * SCALE
        rpi = _rel_pos_index().reshape(-1)
        bias = bias_table[rpi].reshape(N, N, NH).transpose(2, 0, 1)
        attn = attn + bias[None]
        mask = jnp.asarray(_shift_mask(H, W))
        attn = attn.reshape(B, nW, NH, N, N) + mask[None, :, None]
        attn = jax.nn.softmax(attn, axis=-1).reshape(B * nW, NH, N, N)
        out = jnp.einsum('wnqk,wnkd->wnqd', attn, v)
        out = out.reshape(B, nWh, nWw, NH, WS, WS, HD)
        out = out.transpose(0, 3, 6, 1, 4, 2, 5).reshape(B, C, H, W)
        out = jnp.einsum('bchw,oc->bohw', out, proj_w) + proj_b[None, :, None, None]
        out = jnp.roll(out, (SHIFT, SHIFT), axis=(2, 3))
        return out

    def _L0_ffn_ref(x, gate_w, gate_b, weight1, weight2):
        import jax, jax.numpy as jnp
        import numpy as np
        B, S, D, E, H, O, K = (256, 1024, 64, 32, 256, 64, 8)
        Bn, Sn, Dn = x.shape
        logits = jnp.einsum('bsd,ed->bse', x, gate_w) + gate_b
        probs = jax.nn.softmax(logits, axis=1)
        vals, idx = jax.lax.top_k(probs.transpose(0, 2, 1), K)
        topv = vals.transpose(0, 2, 1)
        topi = idx.transpose(0, 2, 1)
        flat_idx = topi.reshape(Bn, K * E)
        gathered = jnp.take_along_axis(x, flat_idx[:, :, None], axis=1)
        gathered = gathered.reshape(Bn, K, E, Dn)
        pooled = jnp.einsum('bked,bke->bed', gathered, topv)
        ones = jnp.ones((E, Bn, 1), dtype=x.dtype)
        h = jnp.concatenate([pooled.transpose(1, 0, 2), ones], axis=-1)
        h = jax.nn.gelu(jnp.einsum('ebd,edh->ebh', h, weight1), approximate=False)
        h = jnp.concatenate([h, ones], axis=-1)
        out = jnp.einsum('ebh,eho->ebo', h, weight2)
        out = out.transpose(1, 0, 2)
        weighted = jnp.einsum('beo,bke->bkeo', out, topv).reshape(Bn, K * E, O)
        outputs = jnp.zeros((Bn, Sn, O), dtype=x.dtype)
        outputs = outputs.at[jnp.arange(Bn)[:, None], flat_idx].add(weighted)
        return outputs

    def _L1_conv_ref(x, gamma, beta, w_lbp, w_1x1, b_1x1):
        import jax, jax.numpy as jnp
        import numpy as np
        BN_EPS = 1e-05

        def _ternary_weights(key, shape, sparsity):
            k1, k2 = jax.random.split(key)
            signs = jnp.where(jax.random.uniform(k1, shape) < 0.5, -1.0, 1.0)
            active = jax.random.uniform(k2, shape) <= 0.5
            return jnp.where(active, signs, 0.0).astype(jnp.float32)
        mean = jnp.mean(x, axis=(0, 2, 3), keepdims=True)
        var = jnp.var(x, axis=(0, 2, 3), keepdims=True)
        xn = (x - mean) * jax.lax.rsqrt(var + BN_EPS)
        xn = xn * gamma[None, :, None, None] + beta[None, :, None, None]
        y = jax.lax.conv_general_dilated(xn, w_lbp, window_strides=(1, 1), padding=((1, 1), (1, 1)), dimension_numbers=('NCHW', 'OIHW', 'NCHW'))
        y = jax.nn.relu(y) + x
        out = jnp.einsum('bchw,oc->bohw', y, w_1x1[:, :, 0, 0]) + b_1x1[None, :, None, None]
        return out

    def _L1_ffn_ref(x, router_w, router_b, expert_w, expert_b):
        import jax, jax.numpy as jnp
        import numpy as np
        B, N, D, C, E, K = (8, 4096, 64, 64, 8, 2)
        router_probs = jax.nn.softmax(x @ router_w + router_b, axis=-1)
        top_p, top_i = jax.lax.top_k(router_probs, K)
        top_p = top_p / jnp.sum(top_p, axis=-1, keepdims=True)
        expert_out = jnp.einsum('bnd,edc->bnec', x, expert_w) + expert_b
        gathered = jnp.take_along_axis(expert_out, top_i[..., None], axis=2)
        return jnp.einsum('bnk,bnkc->bnc', top_p, gathered)

    def _L2_conv_ref(x, kernel_td, kernel_dt, kernel_lr, kernel_rl):
        import jax, jax.numpy as jnp
        import numpy as np
        from jax import lax
        B, C, H, W = (16, 64, 32, 80)
        KW, KH = (9, 9)
        PAD_W, PAD_H = ((KW - 1) // 2, (KH - 1) // 2)

        def _slice_conv(s, K, pad):
            kern = jnp.transpose(K[:, 0], (0, 2, 1))
            y = lax.conv_general_dilated(jnp.swapaxes(s, 1, 2), kern, (1,), [(pad, pad)])
            return jnp.swapaxes(y, 1, 2)

        def _sweep(x, K, pad, reverse):
            if reverse:
                x = x[:, ::-1]
            xs = jnp.swapaxes(x, 0, 1)

            def step(prev, xi):
                new = xi + jax.nn.relu(_slice_conv(prev, K, pad))
                return (new, new)
            _, rest = lax.scan(step, xs[0], xs[1:])
            out = jnp.swapaxes(jnp.concatenate([xs[:1], rest], axis=0), 0, 1)
            if reverse:
                out = out[:, ::-1]
            return out
        y = jnp.transpose(x, (0, 2, 3, 1))
        y = _sweep(y, kernel_td, PAD_W, False)
        y = _sweep(y, kernel_dt, PAD_W, True)
        y = jnp.swapaxes(y, 1, 2)
        y = _sweep(y, kernel_lr, PAD_H, False)
        y = _sweep(y, kernel_rl, PAD_H, True)
        y = jnp.swapaxes(y, 1, 2)
        return jnp.transpose(y, (0, 3, 1, 2))

    def _L2_ffn_ref(x, gate_w, gate_b, weight1, weight2):
        import jax, jax.numpy as jnp
        import numpy as np
        B, S, D, E, H, O, K = (256, 1024, 64, 32, 256, 64, 8)
        Bn, Sn, Dn = x.shape
        logits = jnp.einsum('bsd,ed->bse', x, gate_w) + gate_b
        probs = jax.nn.softmax(logits, axis=1)
        vals, idx = jax.lax.top_k(probs.transpose(0, 2, 1), K)
        topv = vals.transpose(0, 2, 1)
        topi = idx.transpose(0, 2, 1)
        flat_idx = topi.reshape(Bn, K * E)
        gathered = jnp.take_along_axis(x, flat_idx[:, :, None], axis=1)
        gathered = gathered.reshape(Bn, K, E, Dn)
        pooled = jnp.einsum('bked,bke->bed', gathered, topv)
        ones = jnp.ones((E, Bn, 1), dtype=x.dtype)
        h = jnp.concatenate([pooled.transpose(1, 0, 2), ones], axis=-1)
        h = jax.nn.gelu(jnp.einsum('ebd,edh->ebh', h, weight1), approximate=False)
        h = jnp.concatenate([h, ones], axis=-1)
        out = jnp.einsum('ebh,eho->ebo', h, weight2)
        out = out.transpose(1, 0, 2)
        weighted = jnp.einsum('beo,bke->bkeo', out, topv).reshape(Bn, K * E, O)
        outputs = jnp.zeros((Bn, Sn, O), dtype=x.dtype)
        outputs = outputs.at[jnp.arange(Bn)[:, None], flat_idx].add(weighted)
        return outputs

    def _L3_conv_ref(x, w_d, w_u, w_r, w_l, bn_d, bn_u, bn_r, bn_l):
        import jax, jax.numpy as jnp
        import numpy as np
        ITER = 4
        ALPHA = 2.0
        EPS = 0.001

        def _dwconv(x, w, dil, pad):
            return jax.lax.conv_general_dilated(x, w, window_strides=(1, 1), padding=((pad, pad), (pad, pad)), rhs_dilation=(dil, dil), dimension_numbers=('NCHW', 'OIHW', 'NCHW'), feature_group_count=x.shape[1])

        def _aspp(x, w, bn, dil):
            pad = 0 if dil == 1 else dil
            y = _dwconv(x, w, dil, pad)
            g, b, m, v = (bn[0], bn[1], bn[2], bn[3])
            scale = (g * jax.lax.rsqrt(v + EPS))[None, :, None, None]
            bias = (b - g * m * jax.lax.rsqrt(v + EPS))[None, :, None, None]
            return jax.nn.relu(y * scale + bias)
        H, W = (x.shape[2], x.shape[3])
        dirs = [(w_d, bn_d, 1, +1, 2), (w_u, bn_u, 2, -1, 2), (w_r, bn_r, 4, +1, 3), (w_l, bn_l, 8, -1, 3)]
        for w, bn, dil, sign, axis in dirs:
            dim = H if axis == 2 else W
            for i in range(ITER):
                shift = dim // 2 ** (ITER - i)
                idx = (np.arange(dim) + sign * shift) % dim
                xs = x[:, :, idx, :] if axis == 2 else x[:, :, :, idx]
                x = x + ALPHA * jax.nn.relu(_aspp(xs, w[i], bn[i], dil))
        return x

    def _L3_ffn_ref(x, router_w, router_b, expert_w, expert_b):
        import jax, jax.numpy as jnp
        import numpy as np
        B, N, D, C, E, K = (8, 4096, 64, 64, 8, 2)
        router_probs = jax.nn.softmax(x @ router_w + router_b, axis=-1)
        top_p, top_i = jax.lax.top_k(router_probs, K)
        top_p = top_p / jnp.sum(top_p, axis=-1, keepdims=True)
        expert_out = jnp.einsum('bnd,edc->bnec', x, expert_w) + expert_b
        gathered = jnp.take_along_axis(expert_out, top_i[..., None], axis=2)
        return jnp.einsum('bnk,bnkc->bnc', top_p, gathered)

    def _gn(v, G=32, eps=1e-05):
        B_, C_, H_, W_ = v.shape
        g = v.reshape(B_, G, C_ // G, H_, W_)
        m = jnp.mean(g, axis=(2, 3, 4), keepdims=True)
        s = jnp.var(g, axis=(2, 3, 4), keepdims=True)
        return ((g - m) / jnp.sqrt(s + eps)).reshape(v.shape)

    def _ln_c(v, eps=1e-06):
        m = jnp.mean(v, axis=1, keepdims=True)
        s = jnp.var(v, axis=1, keepdims=True)
        return (v - m) / jnp.sqrt(s + eps)

    def _ln_t(v, eps=1e-05):
        m = jnp.mean(v, axis=-1, keepdims=True)
        s = jnp.var(v, axis=-1, keepdims=True)
        return (v - m) / jnp.sqrt(s + eps)

    def _to_tokens(v):
        B_, C_, H_, W_ = v.shape
        return v.reshape(B_, C_, H_ * W_).transpose(0, 2, 1)

    def _from_tokens(t, like):
        B_, C_, H_, W_ = like.shape
        return t.transpose(0, 2, 1).reshape(B_, C_, H_, W_)
    x = x + _L0_conv_ref(_ln_c(x), L0_conv_qkv_w, L0_conv_proj_w, L0_conv_proj_b, L0_conv_bias_table)
    t = _to_tokens(x)
    t = t + _L0_ffn_ref(_ln_t(t), L0_ffn_gate_w, L0_ffn_gate_b, L0_ffn_weight1, L0_ffn_weight2)
    x = _from_tokens(t, x)
    x = x + _L1_conv_ref(_ln_c(x), L1_conv_gamma, L1_conv_beta, L1_conv_w_lbp, L1_conv_w_1x1, L1_conv_b_1x1)
    t = _to_tokens(x)
    t = t + _L1_ffn_ref(_ln_t(t), L1_ffn_router_w, L1_ffn_router_b, L1_ffn_expert_w, L1_ffn_expert_b)
    x = _from_tokens(t, x)
    x = x + _L2_conv_ref(_ln_c(x), L2_conv_kernel_td, L2_conv_kernel_dt, L2_conv_kernel_lr, L2_conv_kernel_rl)
    t = _to_tokens(x)
    t = t + _L2_ffn_ref(_ln_t(t), L2_ffn_gate_w, L2_ffn_gate_b, L2_ffn_weight1, L2_ffn_weight2)
    x = _from_tokens(t, x)
    x = x + _L3_conv_ref(_ln_c(x), L3_conv_w_d, L3_conv_w_u, L3_conv_w_r, L3_conv_w_l, L3_conv_bn_d, L3_conv_bn_u, L3_conv_bn_r, L3_conv_bn_l)
    t = _to_tokens(x)
    t = t + _L3_ffn_ref(_ln_t(t), L3_ffn_router_w, L3_ffn_router_b, L3_ffn_expert_w, L3_ffn_expert_b)
    x = _from_tokens(t, x)
    return x

_drawn_inputs = setup_inputs


def setup_inputs(seed=0):
    import zlib

    import numpy as np

    out = dict(_drawn_inputs(seed))
    spreads = {'L0_ffn_gate_b': (0.0, 0.8),
     'L1_conv_gamma': (1.0, 0.2),
     'L1_conv_beta': (0.0, 0.1),
     'L1_ffn_router_b': (0.0, 0.1),
     'L1_ffn_expert_b': (0.0, 0.758),
     'L2_ffn_gate_b': (0.0, 0.1),
     'L3_ffn_router_b': (0.0, 0.1),
     'L3_ffn_expert_b': (0.0, 0.8)}
    factors = {'L0_conv_proj_b': 8.0,
     'L0_conv_bias_table': 8.0,
     'L0_ffn_gate_w': 8.0,
     'L0_ffn_weight1': 8.0,
     'L0_ffn_weight2': 8.0,
     'L1_conv_b_1x1': 3.683,
     'L2_ffn_gate_w': 8.0,
     'L2_ffn_weight1': 8.0,
     'L2_ffn_weight2': 8.0}
    for name, (base, spread) in spreads.items():
        noise = np.random.default_rng([zlib.crc32(name.encode()), seed]).standard_normal(out[name].shape)
        drawn = base * np.exp(spread * noise) if base else spread * noise
        out[name] = jnp.asarray(drawn.astype(out[name].dtype))
    for name, factor in factors.items():
        out[name] = (out[name] * factor).astype(out[name].dtype)
    return out
```

```python
import numpy as np
import concourse.bass as bass
from concourse import mybir
from contextlib import ExitStack

FP32 = mybir.dt.float32
ALU = mybir.AluOpType
ACT = mybir.ActivationFunctionType
AX = mybir.AxisListType
B, C, H, W = 4, 64, 128, 128
S = H * W


class Link:

    def __init__(self, eng, sem):
        self.eng, self.sem, self.base, self.n = eng, sem, 0, 0

    def __call__(self, ins):
        ins.then_inc(self.sem, 1)
        self.n += 1
        self.eng.wait_ge(self.sem, self.base + self.n)

    def enter(self, i, per_iteration):
        self.start, self.per = self.base + self.n, per_iteration
        self.base, self.n = self.start + i * per_iteration, 0

    def leave(self, iterations):
        assert self.n == self.per, (self.n, self.per)
        self.base, self.n = self.start + iterations * self.per, 0


class Arena:

    def __init__(self, nc, ctx, stage):
        self.nc, self.ctx, self.stage, self.sems = nc, ctx, stage, []
        ctx.callback(self.clear)

    def clear(self):
        self.nc.clear_and_free_semaphores(self.sems)
        self.nc.all_engine_barrier()

    def sb(self, name, shape, dt=FP32):
        return self.ctx.enter_context(self.nc.sbuf_tensor(f"{self.stage}_{name}", shape, dt))

    def ps(self, name, shape, dt=FP32):
        return self.ctx.enter_context(self.nc.psum_tensor(f"{self.stage}_{name}", shape, dt))

    def sem(self, name):
        self.sems.append(self.nc.alloc_semaphore(name=f"{self.stage}_{name}"))
        return self.sems[-1]


def eye(pool, link, m):
    link(pool.memset(m, 0.0))
    link(pool.affine_select(out=m, in_=m, compare_op=ALU.not_equal, fill=1.0, base=0,
                            pattern=[[-1, 128]], channel_multiplier=1))


def bcast(v, n, m=C):
    return v.unsqueeze(2).to_broadcast([128, n, m])


def parity_blocks(taps, first):
    for m in range(-2, 3):
        for pi in range(2):
            for po in range(2):
                tap = 2 * m + pi - po + first
                if 0 <= tap < taps:
                    yield m, pi, po, tap


def stage_window_attention(nc, x, qkv_w, proj_w, proj_b, bias_table, tok):
    WS, NH, SHIFT = 8, 4, 4
    STEP = 4
    NSTEP = W // WS // STEP
    T = STEP * WS * WS
    STRIPS = H // WS
    SCALE = float(C // NH) ** -0.5
    EPS = 1e-6
    with ExitStack() as ctx:
        a = Arena(nc, ctx, "wa")
        ident = a.sb("ident", [128, 128])
        mean_w = a.sb("mean_w", [128, 128])
        w_rows = a.sb("w_rows", [128, 4, 128])
        w_cols = a.sb("w_cols", [128, 4, 128])
        pb = a.sb("pb", [128, 1])
        eps = a.sb("eps", [128, 1])
        iota_q = a.sb("iota_q", [128, 1], mybir.dt.int32)
        iota_k = a.sb("iota_k", [128, 64], mybir.dt.int32)
        bits_q = a.sb("bits_q", [128, 4], mybir.dt.int32)
        bits_k = a.sb("bits_k", [128, 2, 64], mybir.dt.int32)
        bits_qf = a.sb("bits_qf", [128, 4])
        bits_kf = a.sb("bits_kf", [128, 2, 64])
        gmask = a.sb("gmask", [128, 2])
        hmask = a.sb("hmask", [128, NH])
        half_mask = a.sb("half_mask", [128, 2, 16])
        table = a.sb("table", [128, 64, NH])
        bias = a.sb("bias", [128, 2, 2, NH, 64])
        cut = a.sb("cut", [128, 3, 64])
        xs = a.sb("xs", [128, 2, 8, 128])
        xc = a.sb("xc", [128, 8, 128])
        sq = a.sb("sq", [128, 8, 128])
        h = a.sb("h", [128, W // WS, 2, WS, WS])
        qs = a.sb("qs", [128, STEP, 2, 64])
        ks = a.sb("ks", [128, NH, T])
        vs = a.sb("vs", [128, 2, STEP, 128])
        sc = a.sb("sc", [128, 2, STEP, NH, 64])
        mx = a.sb("mx", [128, STEP, NH])
        sm = a.sb("sm", [128, 2, 2, STEP, NH])
        pt = a.sb("pt", [128, STEP, 2, 128])
        ov = a.sb("ov", [128, T])
        yr = a.sb("yr", [128, WS, W])
        x1 = a.sb("x1", [128, WS, W])
        xt = a.sb("xt", [128, 2, WS, 128])
        pL = a.ps("pL", [128, 512])
        pQK = a.ps("pQK", [128, 2, T])
        pV = a.ps("pV", [128, STEP, 128])
        pS = a.ps("pS", [128, STEP, NH, 64])
        pT = a.ps("pT", [128, STEP, 2, 128])
        pO = a.ps("pO", [128, 2, T])
        const_in = a.sem("const_in")
        pool_done = a.sem("pool_done")
        dve_done = a.sem("dve_done")
        const_ready = a.sem("const_ready")
        zeros_ready = a.sem("zeros_ready")
        w_turned = a.sem("w_turned")
        w_ready = a.sem("w_ready")
        x_in = [a.sem(f"x_in{i}") for i in range(2)]
        mean_ready = a.sem("mean_ready")
        centered = a.sem("centered")
        squared = a.sem("squared")
        var_ready = a.sem("var_ready")
        std_ready = a.sem("std_ready")
        h_ready = a.sem("h_ready")
        h_doubled = a.sem("h_doubled")
        qkv_ready = a.sem("qkv_ready")
        qk_saved = a.sem("qk_saved")
        v_saved = a.sem("v_saved")
        scores_ready = a.sem("scores_ready")
        scores_read = a.sem("scores_read")
        shifted = a.sem("shifted")
        exp_ready = a.sem("exp_ready")
        sum_ready = a.sem("sum_ready")
        probs_ready = a.sem("probs_ready")
        probs_turned = a.sem("probs_turned")
        pt_saved = a.sem("pt_saved")
        pv_ready = a.sem("pv_ready")
        ov_saved = a.sem("ov_saved")
        proj_ready = a.sem("proj_ready")
        yr_ready = a.sem("yr_ready")
        x1_ready = a.sem("x1_ready")
        x1_turned = a.sem("x1_turned")
        xt_saved = a.sem("xt_saved")
        stored = [a.sem(f"stored{i}") for i in range(2)]
        block = ctx.enter_context(nc.Block())

        N_CONST = 8 + 2 + 16

        def over_strips(eng, body, link=None, per=0):
            start = (link.base + link.n) if link else 0

            def strip(bp, i, n, par, last):
                if link:
                    link.base, link.n = start + n * per, 0
                body(bp, i, n, par, last)
                assert not link or link.n == per, link.n

            with eng.Fori(0, 2) as bp:
                with eng.Fori(0, STRIPS // 2 - 1) as t:
                    for par in range(2):
                        strip(bp, 2 * t + par, bp * STRIPS + 2 * t + par, par, False)
                for par in range(2):
                    i = STRIPS - 2 + par
                    strip(bp, i, bp * STRIPS + i, par, par == 1)
            if link:
                link.base, link.n = start + 2 * STRIPS * per, 0

        @block.sync
        def _(sp):
            sp.wait_ge(zeros_ready, 1)
            for g in range(2):
                part = slice(64 * g, 64 * g + 64)
                for m in range(4):
                    w = proj_w if m == 3 else qkv_w[64 * m:64 * m + 64, :]
                    sp.dma_start(w_rows[part, m, part], w).then_inc(const_in, 16)
                sp.dma_start(pb[part, :], proj_b.rearrange("(c a) -> c a", a=1)).then_inc(const_in, 16)
                for qr in range(WS):
                    src = bass.AP(bias_table.tensor, qr * 15 * NH, [[NH, 8], [15 * NH, 8], [1, 8 * NH]])
                    sp.dma_start(table[64 * g + 8 * qr:64 * g + 8 * qr + 8, :, :].rearrange(
                        "p (i j) h -> p i (j h)", i=8), src).then_inc(const_in, 16)

            def load(bp, i, n, par, last):
                sp.wait_ge(x1_ready, n + 1)
                for half in range(2):
                    r = (WS * i + SHIFT + 4 * half) % H if last else WS * i + SHIFT + 4 * half
                    src = x[bass.ds(2 * bp, 2), :, bass.ds(r, 4), :].rearrange("g c h w -> (g c) h w")
                    sp.dma_start(xs[:, par, 4 * half:4 * half + 4, :], src).then_inc(x_in[par], 16)

            over_strips(sp, load)

        @block.gpsimd
        def _(pool):
            link = Link(pool, pool_done)
            for s in (x1_turned, pv_ready, probs_turned, qkv_ready, scores_ready, v_saved, pt_saved, yr_ready):
                pool.sem_inc(s, 1)
            for s in stored:
                pool.sem_inc(s, 16)
            pool.memset(w_rows[:, :, :], 0.0).then_inc(zeros_ready, 1)
            pool.memset(eps[:, :], EPS)
            link(pool.memset(mean_w[:, :], 0.0))
            for g in range(2):
                link(pool.memset(mean_w[64 * g:64 * g + 64, 64 * g:64 * g + 64], 1.0 / C))
            eye(pool, link, ident[:, :])
            link(pool.iota(iota_q[:, :], pattern=[[0, 1]], base=0, channel_multiplier=1))
            pool.iota(iota_k[:, :], pattern=[[1, 64]], base=0, channel_multiplier=0).then_inc(const_ready, 1)
            pool.sem_inc(x1_ready, 2)

            def normalise(s, j):
                pool.wait_ge(sum_ready, s + 1)
                p = sc[:, j % 2, :, :, :]
                r = sm[:, j % 2, 1, :, :].unsqueeze(3).to_broadcast([128, STEP, NH, 64])
                pool.tensor_tensor(p, p, r, ALU.mult).then_inc(probs_ready, 1)

            def strip(bp, i, n, par, last):
                for j in range(NSTEP):
                    normalise(NSTEP * n + j, j)
                pool.wait_ge(yr_ready, NSTEP * (n + 1) + 1)
                pool.wait_ge(x1_turned, 2 * n + 1)
                pool.tensor_tensor(x1[:, :, SHIFT:W], xs[:, par, :, SHIFT:W], yr[:, :, 0:W - SHIFT], ALU.add)
                pool.tensor_tensor(x1[:, :, 0:SHIFT], xs[:, par, :, 0:SHIFT], yr[:, :, W - SHIFT:W],
                                   ALU.add).then_inc(x1_ready, 1)

            over_strips(pool, strip)

        @block.vector
        def _(dve):
            link = Link(dve, dve_done)
            SHR, AND = ALU.logical_shift_right, ALU.bitwise_and
            dve.wait_ge(const_ready, 1)
            for k, (bit, m) in enumerate([(5, 1), (2, 1), (4, 3), (6, 1)]):
                link(dve.tensor_scalar(bits_q[:, k:k + 1], iota_q[:, :], bit, m, SHR, AND))
                if k < 2:
                    link(dve.tensor_scalar(bits_k[:, k, :], iota_k[:, :], bit, m, SHR, AND))
            link(dve.tensor_copy(bits_qf[:, :], bits_q[:, :]))
            link(dve.tensor_copy(bits_kf[:, :, :], bits_k[:, :, :]))
            for g in range(2):
                link(dve.tensor_scalar(gmask[:, g:g + 1], bits_qf[:, 3:4], float(g), SCALE, ALU.is_equal, ALU.mult))
                link(dve.memset(half_mask[:, g, :], 0.0))
                link(dve.tensor_scalar(half_mask[:, g, :], half_mask[:, g, :], bits_qf[:, 3:4], float(g),
                                       ALU.add, ALU.is_equal))
            for k in range(NH):
                link(dve.tensor_scalar(hmask[:, k:k + 1], bits_qf[:, 2:3], float(k), None, ALU.is_equal))
            for k in range(2):
                link(dve.tensor_scalar(cut[:, k, :], bits_kf[:, k, :], bits_qf[:, k:k + 1], -100.0,
                                       ALU.not_equal, ALU.mult))
            link(dve.tensor_tensor(cut[:, 2, :], cut[:, 0, :], cut[:, 1, :], ALU.min))
            dve.wait_ge(const_in, 16 * N_CONST)
            link(dve.tensor_copy(bias[:, 0, 0, :, :], table[:, ::-1, :].rearrange("p k h -> p h k")))
            for row, col, which in ((0, 1, 1), (1, 0, 0), (1, 1, 2)):
                link(dve.tensor_tensor(bias[:, row, col, :, :], bias[:, 0, 0, :, :],
                                       cut[:, which, :].unsqueeze(1).to_broadcast([128, NH, 64]), ALU.add))
            dve.sem_inc(scores_read, 1)

            def save_v(s, j):
                dve.wait_ge(qkv_ready, s + 2)
                dve.wait_ge(pv_ready, s + 1)
                m = half_mask[:, :, :].rearrange("p a d -> p (a d)").unsqueeze(1).to_broadcast([128, STEP * 4, 32])
                dve.tensor_tensor(vs[:, j % 2, :, :].rearrange("p w (a d) -> p (w a) d", d=32),
                                  pV[:, :, :].rearrange("p w (a d) -> p (w a) d", d=32), m,
                                  ALU.mult).then_inc(v_saved, 1)

            def softmax_shift(s, j, last):
                dve.wait_ge(scores_ready, s + 2)
                dve.wait_ge(probs_turned, s + 1)
                e, f = sc[:, j % 2, :, :, :], pS[:, :, :, :]
                n = STEP - 1 if j == NSTEP - 1 else STEP
                if n < STEP:
                    dve.tensor_tensor(e[:, n, :, :], f[:, n, :, :], bias[:, int(last), 1, :, :], ALU.add)
                r = bias[:, int(last), 0, :, :].rearrange("p h k -> p (h k)").unsqueeze(1).to_broadcast([128, n, NH * 64])
                ins = dve.tensor_tensor(e[:, 0:n, :, :].rearrange("p w h k -> p w (h k)"),
                                        f[:, 0:n, :, :].rearrange("p w h k -> p w (h k)"), r, ALU.add)
                ins.then_inc(scores_read, 1)
                dve.wait_ge(scores_read, s + 2)
                link(dve.tensor_reduce(mx[:, :, :], e, AX.X, ALU.max))
                dve.tensor_tensor(e, e, mx[:, :, :].unsqueeze(3).to_broadcast([128, STEP, NH, 64]),
                                  ALU.subtract).then_inc(shifted, 1)

            def softmax_sum(s, j):
                dve.wait_ge(exp_ready, s + 1)
                link(dve.tensor_reduce(sm[:, j % 2, 0, :, :], sc[:, j % 2, :, :, :], AX.X, ALU.add))
                dve.reciprocal(sm[:, j % 2, 1, :, :], sm[:, j % 2, 0, :, :]).then_inc(sum_ready, 1)

            def strip(bp, i, n, par, last):
                dve.wait_ge(x_in[par], 16 * (n - par + 2))
                for k in range(2):
                    rows = slice(4 * k, 4 * k + 4)
                    dve.wait_ge(mean_ready, 2 * n + k + 1)
                    dve.tensor_tensor(xc[:, rows, :], xs[:, par, rows, :],
                                      pL[:, :].rearrange("p (r c) -> p r c", c=W), ALU.subtract).then_inc(centered, 1)
                for k in range(2):
                    rows = slice(4 * k, 4 * k + 4)
                    dve.wait_ge(std_ready, 2 * n + k + 1)
                    link(dve.reciprocal(sq[:, rows, :], sq[:, rows, :]))
                dve.wait_ge(qkv_ready, NSTEP * n + 1)
                for w0, w1, c0, c1, col in ((0, 15, 0, WS, SHIFT), (15, 16, 0, 4, W - 4), (15, 16, 4, 8, 0)):
                    def part(t):
                        return t[:, :, col:col + (w1 - w0) * (c1 - c0)].rearrange("p r (w c) -> p w r c", c=c1 - c0)
                    ins = dve.tensor_tensor(h[:, w0:w1, 0, :, c0:c1], part(xc), part(sq), ALU.mult)
                ins.then_inc(h_ready, 1)
                s = NSTEP * n
                for j in range(NSTEP + 1):
                    if j < NSTEP:
                        save_v(s + j, j)
                        softmax_shift(s + j, j, last)
                    if j > 0:
                        softmax_sum(s + j - 1, j - 1)

            over_strips(dve, strip, link, 2 + 2 * NSTEP)

        @block.scalar
        def _(act):
            for half in range(1):
                act.wait_ge(w_turned, 1)
                act.activation(w_cols[:, :, :].rearrange("p m c -> p (m c)"), pL[:, :], ACT.Copy).then_inc(w_ready, 1)
            act.sem_inc(xt_saved, 2)

            def save_qk(s, j):
                act.wait_ge(qkv_ready, s + 2)
                act.wait_ge(scores_ready, s + 1)
                for g in range(2):
                    act.activation(qs[:, :, g, :], pQK[:, 0, :].rearrange("p (w q) -> p w q", q=64), ACT.Copy,
                                   scale=gmask[:, g:g + 1])
                for k in range(NH):
                    ins = act.activation(ks[:, k, :], pQK[:, 1, :], ACT.Copy, scale=hmask[:, k:k + 1])
                ins.then_inc(qk_saved, 1)

            def exponential(s, j):
                act.wait_ge(shifted, s + 1)
                e = sc[:, j % 2, :, :, :]
                act.activation(e, e, ACT.Exp).then_inc(exp_ready, 1)

            def save_out(s, j):
                act.wait_ge(probs_turned, s + 3)
                act.activation(pt[:, :, :, :], pT[:, :, :, :], ACT.Copy).then_inc(pt_saved, 1)
                act.wait_ge(pv_ready, s + 3)
                act.activation(ov[:, :], pO[:, 0, :], ACT.Copy).then_inc(ov_saved, 1)
                act.wait_ge(proj_ready, s + 1)
                if j == 0:
                    act.wait_ge(x1_ready, s // NSTEP + 2)
                cols = yr[:, :, 4 * 8 * j:4 * 8 * j + 32].rearrange("p r (w c) -> p w r c", c=WS)
                act.activation(cols, pO[:, 1, :].rearrange("p (w r c) -> p w r c", w=STEP, r=WS), ACT.Identity,
                               bias=pb[:, 0:1]).then_inc(yr_ready, 1)

            def strip(bp, i, n, par, last):
                for k in range(2):
                    rows = slice(4 * k, 4 * k + 4)
                    act.wait_ge(centered, 2 * n + k + 1)
                    act.activation(sq[:, rows, :], xc[:, rows, :], ACT.Square).then_inc(squared, 1)
                for k in range(2):
                    rows = slice(4 * k, 4 * k + 4)
                    act.wait_ge(var_ready, 2 * n + k + 1)
                    act.activation(sq[:, rows, :].rearrange("p r c -> p (r c)"), pL[:, :], ACT.Sqrt,
                                   bias=eps[:, 0:1]).then_inc(std_ready, 1)
                act.wait_ge(h_ready, n + 1)
                act.activation(h[:, :, 1, :, :], h[:, :, 0, :, :], ACT.Copy).then_inc(h_doubled, 1)
                s = NSTEP * n
                for j in range(NSTEP + 1):
                    if j < NSTEP:
                        save_qk(s + j, j)
                        exponential(s + j, j)
                    if j > 0:
                        save_out(s + j - 1, j - 1)
                act.wait_ge(stored[par], 64 * ((n - par) // 2) + 16)
                for k in range(2):
                    act.wait_ge(x1_turned, 2 * n + k + 2)
                    act.activation(xt[:, par, 4 * k:4 * k + 4, :].rearrange("p r c -> p (r c)"), pL[:, :],
                                   ACT.Copy).then_inc(xt_saved, 1)
                act.wait_ge(xt_saved, 2 * n + 4)
                for half in range(2):
                    r = (WS * i + SHIFT + 4 * half) % H if last else WS * i + SHIFT + 4 * half
                    for g in range(2):
                        rows = tok[bass.ds((2 * bp + g) * S + r * W, 4 * W), :]
                        act.dma_start(rows.rearrange("(r w) c -> w r c", r=4),
                                      xt[:, par, 4 * half:4 * half + 4, 64 * g:64 * g + 64]).then_inc(stored[par], 16)

            over_strips(act, strip)
            for par in range(2):
                act.wait_ge(stored[par], 64 * STRIPS + 16)

        @block.tensor
        def _(pe):
            pe.wait_ge(const_ready, 1)
            pe.wait_ge(const_in, 16 * N_CONST)
            for m in range(4):
                ins = pe.transpose(pL[:, 128 * m:128 * m + 128], w_rows[:, m, :], ident[:, :])
            ins.then_inc(w_turned, 1)
            pe.wait_ge(w_ready, 1)
            pe.sem_inc(pv_ready, 1)
            pe.sem_inc(probs_turned, 1)

            def scores(s, j):
                ht = h[:, STEP * j:STEP * j + STEP, :, :, :].rearrange("p w t r c -> p w t (r c)")
                for m in range(2):
                    pe.matmul(pQK[:, m, :], w_cols[:, m, :], ht[:, :, 0, :], start=True, stop=True)
                pe.wait_ge(v_saved, s + 1)
                if j == 0:
                    pe.wait_ge(h_doubled, s // NSTEP + 1)
                for w in range(STEP):
                    keys = ht[:, w, :, :].rearrange("p t q -> p (t q)")
                    ins = pe.matmul(pV[:, w, :], keys, w_cols[:, 2, :], start=True, stop=True)
                ins.then_inc(qkv_ready, 1)
                pe.wait_ge(qk_saved, s + 1)
                pe.wait_ge(scores_read, s + 1)
                for w in range(STEP):
                    ins = pe.matmul(pS[:, w, :, :], qs[:, w, :, :].rearrange("p g q -> p (g q)"), ks[:, :, 64 * w:64 * w + 64],
                                    start=True, stop=True)
                ins.then_inc(scores_ready, 1)

            def outputs(s, j):
                pe.wait_ge(probs_ready, s + 1)
                pe.wait_ge(pt_saved, s + 1)
                for w in range(STEP):
                    for hp in range(2):
                        ins = pe.transpose(pT[:, w, hp, :], sc[:, j % 2, w, 2 * hp:2 * hp + 2, :], ident[:, :])
                ins.then_inc(probs_turned, 1)
                pe.wait_ge(pt_saved, s + 2)
                pe.wait_ge(yr_ready, s + 1)
                for w in range(STEP):
                    for g in range(2):
                        for hp in range(2):
                            o = 64 * g + 32 * hp
                            ins = pe.matmul(pO[o:o + 32, 0, 64 * w:64 * w + 64], vs[:, j % 2, w, o:o + 32],
                                            pt[:, w, hp, 64 * g:64 * g + 64], start=True, stop=True)
                ins.then_inc(pv_ready, 1)
                pe.wait_ge(ov_saved, s + 1)
                pe.matmul(pO[:, 1, :], w_cols[:, 3, :], ov[:, :], start=True, stop=True).then_inc(proj_ready, 1)

            def strip(bp, i, n, par, last):
                pe.wait_ge(x_in[par], 16 * (n - par + 2))
                for k in range(2):
                    if k == 0:
                        pe.wait_ge(xt_saved, 2 * n + 2)
                    else:
                        pe.wait_ge(centered, 2 * n + 1)
                    pe.matmul(pL[:, :], mean_w[:, :], xs[:, par, 4 * k:4 * k + 4, :], start=True,
                              stop=True).then_inc(mean_ready, 1)
                for k in range(2):
                    pe.wait_ge(squared, 2 * n + 1 + k)
                    if k == 0:
                        pe.wait_ge(centered, 2 * n + 2)
                    else:
                        pe.wait_ge(std_ready, 2 * n + 1)
                    pe.matmul(pL[:, :], mean_w[:, :], sq[:, 4 * k:4 * k + 4, :], start=True,
                              stop=True).then_inc(var_ready, 1)
                pe.wait_ge(h_ready, n + 1)
                s = NSTEP * n
                for j in range(NSTEP + 1):
                    if j < NSTEP:
                        scores(s + j, j)
                    if j > 0:
                        outputs(s + j - 1, j - 1)
                pe.wait_ge(x1_ready, n + 3)
                for k in range(2):
                    if k == 1:
                        pe.wait_ge(xt_saved, 2 * n + 3)
                    for r in range(4):
                        ins = pe.transpose(pL[:, 128 * r:128 * r + 128], x1[:, 4 * k + r, :], ident[:, :])
                    ins.then_inc(x1_turned, 1)

            over_strips(pe, strip)


def stage_choice_ffn(nc, stage, tok, gate_w, gate_b, weight1, weight2):
    E, K, HID = 32, 8, 256
    TS = 8
    TILE = 128 * TS
    NT = S // TILE
    EPS = 1e-5
    with ExitStack() as ctx:
        a = Arena(nc, ctx, stage)
        U32, I32 = mybir.dt.uint32, mybir.dt.int32
        ident = a.sb("ident", [128, 128])
        ones = a.sb("ones", [128, 128])
        tri = a.sb("tri", [128, 128])
        eps = a.sb("eps", [128, 1])
        gate_rows = a.sb("gate_rows", [E, 2, 128])
        gate_cols = a.sb("gate_cols", [128, 2, E])
        gb = a.sb("gb", [128, 1])
        w1 = a.sb("w1", [C + 1, E, HID])
        w2 = a.sb("w2", [128, 2, E, C])
        w2b = a.sb("w2b", [1, E, C])
        logits = a.sb("logits", [128, S])
        xs = a.sb("xs", [128, 2, TS, C])
        h = a.sb("h", [128, 2, TS, C])
        sq = a.sb("sq", [128, TS, C])
        st = a.sb("st", [128, 2, 2, TS])
        ht = a.sb("ht", [128, 2, 512])
        top = a.sb("top", [128, K])
        neg_max = a.sb("neg_max", [128, 1])
        at = a.sb("at", [128, K], U32)
        first = a.sb("first", [128, 1], I32)
        firstf = a.sb("firstf", [128, 1])
        idf = a.sb("idf", [128, K])
        rows_at = a.sb("rows_at", [128, K], U32)
        ex = a.sb("ex", [128, K])
        zsum = a.sb("zsum", [128, 2])
        val = a.sb("val", [128, K])
        rows = a.sb("rows", [128, K, C])
        rn = a.sb("rn", [128, K, C])
        rq = a.sb("rq", [128, K, C])
        rs = a.sb("rs", [128, 2, K])
        pooled = a.sb("pooled", [128, C + 1])
        pooled_t = a.sb("pooled_t", [C + 1, 128])
        hid = a.sb("hid", [128, 2, E, B])
        out_t = a.sb("out_t", [C, 128])
        wt = a.sb("wt", [128, K, C])
        dia = a.sb("dia", [128, K, 128])
        idr = a.sb("idr", [128, K, 128])
        same = a.sb("same", [128, 2, K, 128])
        same_before = a.sb("same_before", [128, 2, 128])
        trash = a.sb("trash", [128, K], I32)
        trashf = a.sb("trashf", [128, K])
        dup = a.sb("dup", [128, K])
        pH = [a.ps(f"pH{i}", [128, 512]) for i in range(2)]
        pG = [a.ps(f"pG{i}", [128, 512]) for i in range(2)]
        pA = a.ps("pA", [128, 512])
        pB = a.ps("pB", [128, 512])
        pC = a.ps("pC", [128, 512])
        pD = a.ps("pD", [128, 512])
        pool_done = a.sem("pool_done")
        dve_done = a.sem("dve_done")
        act_done = a.sem("act_done")
        zeros_ready = a.sem("zeros_ready")
        const_ready = a.sem("const_ready")
        gate_in = a.sem("gate_in")
        w_in = a.sem("w_in")
        gate_turned = a.sem("gate_turned")
        gate_ready = a.sem("gate_ready")
        x_in = [a.sem(f"x_in{i}") for i in range(2)]
        centered = a.sem("centered")
        squared = a.sem("squared")
        var_ready = a.sem("var_ready")
        std_ready = a.sem("std_ready")
        h_ready = a.sem("h_ready")
        h_turned = a.sem("h_turned")
        ht_saved = a.sem("ht_saved")
        gates_ready = a.sem("gates_ready")
        logits_saved = a.sem("logits_saved")
        top_ready = a.sem("top_ready")
        found = a.sem("found")
        exp_ready = a.sem("exp_ready")
        at_ready = a.sem("at_ready")
        rows_in = a.sem("rows_in")
        row_step = a.sem("row_step")
        row_act = a.sem("row_act")
        pooled_ready = a.sem("pooled_ready")
        pooled_turned = a.sem("pooled_turned")
        pooled_saved = a.sem("pooled_saved")
        hid_ready = a.sem("hid_ready")
        gelu_ready = a.sem("gelu_ready")
        out_ready = a.sem("out_ready")
        out_saved = a.sem("out_saved")
        out_turned = a.sem("out_turned")
        wt_ready = a.sem("wt_ready")
        dia_ready = a.sem("dia_ready")
        idr_ready = a.sem("idr_ready")
        same_ready = a.sem("same_ready")
        summed = a.sem("summed")
        new_rows = a.sem("new_rows")
        scattered = a.sem("scattered")
        block = ctx.enter_context(nc.Block())
        NGATE, NW = 6, 3

        @block.sync
        def _(sp):
            sp.wait_ge(zeros_ready, 1)
            for p in range(2):
                sp.dma_start(gate_rows[:, p, 64 * p:64 * p + 64], gate_w).then_inc(gate_in, 16)
            for b in range(B):
                sp.dma_start(gb[E * b:E * b + E, :], gate_b.rearrange("(e a) -> e a", a=1)).then_inc(gate_in, 16)
            with sp.Fori(0, NT) as t:
                for b in range(B):
                    sp.wait_ge(h_ready, B * t + b + 1)
                    sp.dma_start(xs[:, b % 2, :, :], tok[bass.ds(b * S + t * TILE, TILE), :].rearrange(
                        "(p j) c -> p j c", j=TS)).then_inc(x_in[b % 2], 16)
            sp.dma_start(w1[:, :, :], weight1.rearrange("e d h -> d e h")).then_inc(w_in, 16)
            for m in range(2):
                sp.dma_start(w2[:, m, :, :], weight2[:, 128 * m:128 * m + 128, :].rearrange(
                    "e h o -> h e o")).then_inc(w_in, 16)
            sp.dma_start(w2b[:, :, :], weight2[:, HID:HID + 1, :].rearrange("e a o -> a e o")).then_inc(w_in, 16)

        @block.gpsimd
        def _(pool):
            link = Link(pool, pool_done)
            for s in (var_ready, gates_ready, ht_saved, logits_saved):
                pool.sem_inc(s, 1)
            pool.memset(gate_rows[:, :, :], 0.0).then_inc(zeros_ready, 1)
            pool.memset(ones[:, :], 1.0)
            pool.memset(eps[:, :], EPS)
            pool.memset(pooled[:, C:C + 1], 1.0)
            link(pool.memset(tri[:, :], 1.0))
            link(pool.affine_select(out=tri[:, :], in_=tri[:, :], compare_op=ALU.is_gt, fill=0.0, base=0,
                                    pattern=[[1, 128]], channel_multiplier=-1))
            eye(pool, link, ident[:, :])
            link(pool.iota(trash[:, :], pattern=[[1, K]], base=B * S, channel_multiplier=K))
            pool.iota(first[:, :], pattern=[[0, 1]], base=0, channel_multiplier=1).then_inc(const_ready, 1)
            pool.sem_inc(h_ready, 2)
            pool.wait_ge(at_ready, 1)
            for k in range(K):
                pool.indirect_dma_start(rows[:, k, :], None, tok[0:B * S, :],
                                        bass.IndirectOffsetOnAxis(ap=rows_at[:, k:k + 1], axis=0)).then_inc(rows_in, 16)
            pool.wait_ge(new_rows, 1)
            for k in range(K):
                pool.indirect_dma_start(tok[:, :], bass.IndirectOffsetOnAxis(ap=rows_at[:, k:k + 1], axis=0),
                                        rows[:, k, :], None).then_inc(scattered, 16)
            pool.wait_ge(scattered, 16 * K)

        def bcast(v, n):
            return v.unsqueeze(2).to_broadcast([128, n, C])

        @block.vector
        def _(dve):
            link = Link(dve, dve_done)
            dve.wait_ge(const_ready, 1)
            link(dve.tensor_scalar(first[:, :], first[:, :], 5, 14, ALU.logical_shift_right, ALU.logical_shift_left))
            link(dve.tensor_copy(firstf[:, :], first[:, :]))
            link(dve.tensor_copy(trashf[:, :], trash[:, :]))
            dve.wait_ge(gate_turned, 1)
            dve.tensor_copy(gate_cols[:, :, :].rearrange("p m e -> p (m e)"), pA[:, 0:2 * E]).then_inc(gate_ready, 1)

            def center(t, n, b):
                par = b % 2
                dve.wait_ge(x_in[par], 16 * (2 * t + b // 2 + 1))
                s = st[:, par, 0, :]
                link(dve.tensor_reduce(s, xs[:, par, :, :], AX.X, ALU.add))
                link(dve.tensor_scalar(s, s, 1.0 / C, None, ALU.mult))
                dve.wait_ge(h_turned, n + 1)
                dve.tensor_tensor(h[:, par, :, :], xs[:, par, :, :], bcast(s, TS), ALU.subtract).then_inc(centered, 1)

            def scale(t, n, b):
                par = b % 2
                s = st[:, par, 1, :]
                dve.wait_ge(squared, n + 1)
                dve.tensor_reduce(s, sq[:, :, :], AX.X, ALU.add).then_inc(var_ready, 1)
                dve.wait_ge(std_ready, n + 1)
                link(dve.reciprocal(s, s))
                dve.tensor_tensor(h[:, par, :, :], h[:, par, :, :], bcast(s, TS), ALU.mult).then_inc(h_ready, 1)

            PER = 3 * B
            start = link.base + link.n
            with dve.Fori(0, NT) as t:
                link.base, link.n = start + t * PER, 0
                for b in range(B + 1):
                    if b < B:
                        center(t, B * t + b, b)
                    if b > 0:
                        scale(t, B * t + b - 1, b - 1)
                assert link.n == PER
            link.base, link.n = start + NT * PER, 0

            dve.wait_ge(logits_saved, 2 * NT + 1)
            link(dve.max(top[:, :], logits[:, :]))
            dve.tensor_scalar(neg_max[:, :], top[:, 0:1], -1.0, None, ALU.mult).then_inc(top_ready, 1)
            link(dve.max_index(at[:, :], top[:, :], logits[:, :]))
            dve.sem_inc(found, 1)
            link(dve.tensor_copy(idf[:, :], at[:, :]))
            link(dve.tensor_scalar(idf[:, :], idf[:, :], firstf[:, 0:1], None, ALU.add))
            dve.tensor_copy(rows_at[:, :], idf[:, :]).then_inc(at_ready, 1)
            for k in range(K):
                ins = dve.tensor_scalar(dia[:, k, :], ident[:, :], idf[:, k:k + 1], None, ALU.mult)
            ins.then_inc(dia_ready, 1)
            dve.wait_ge(exp_ready, 1)
            link(dve.reciprocal(zsum[:, 1:2], zsum[:, 0:1]))
            link(dve.tensor_scalar(val[:, :], ex[:, :], zsum[:, 1:2], None, ALU.mult))
            dve.wait_ge(idr_ready, 1)
            dve.wait_ge(rows_in, 16 * K)
            link(dve.tensor_reduce(rs[:, 0, :], rows[:, :, :], AX.X, ALU.add))
            link(dve.tensor_scalar(rs[:, 0, :], rs[:, 0, :], 1.0 / C, None, ALU.mult))
            link(dve.tensor_tensor(rn[:, :, :], rows[:, :, :], bcast(rs[:, 0, :], K), ALU.subtract))
            link(dve.tensor_tensor(rq[:, :, :], rn[:, :, :], rn[:, :, :], ALU.mult))
            dve.tensor_reduce(rs[:, 1, :], rq[:, :, :], AX.X, ALU.add).then_inc(row_step, 1)
            dve.wait_ge(row_act, 1)
            link(dve.reciprocal(rs[:, 1, :], rs[:, 1, :]))
            link(dve.tensor_tensor(rs[:, 1, :], rs[:, 1, :], val[:, :], ALU.mult))
            link(dve.tensor_tensor(rn[:, :, :], rn[:, :, :], bcast(rs[:, 1, :], K), ALU.mult))
            dve.tensor_reduce(pooled[:, 0:C], rn[:, :, :].rearrange("p k c -> p c k"), AX.X,
                              ALU.add).then_inc(pooled_ready, 1)
            dve.wait_ge(out_turned, 1)
            v = val[:, :].unsqueeze(2).to_broadcast([128, K, C])
            dve.tensor_tensor(wt[:, :, :], v, pD[:, 0:C].unsqueeze(1).to_broadcast([128, K, C]),
                              ALU.mult).then_inc(wt_ready, 1)
            for k in range(K):
                if k >= 2:
                    dve.wait_ge(summed, k - 1)
                link(dve.tensor_scalar(same[:, k % 2, :, :], idr[:, :, :], idf[:, k:k + 1], None, ALU.is_equal))
                dve.tensor_tensor(same_before[:, k % 2, :], same[:, k % 2, k, :], tri[:, :],
                                  ALU.mult).then_inc(same_ready, 1)
            dve.wait_ge(summed, K)
            link(dve.tensor_scalar(dup[:, :], pB[:, 0:K], 0.5, None, ALU.is_gt))
            link(dve.tensor_tensor(trashf[:, :], trashf[:, :], idf[:, :], ALU.subtract))
            link(dve.tensor_tensor(dup[:, :], dup[:, :], trashf[:, :], ALU.mult))
            link(dve.tensor_tensor(dup[:, :], dup[:, :], idf[:, :], ALU.add))
            dve.tensor_copy(rows_at[:, :], dup[:, :])
            dve.tensor_tensor(rows[:, :, :].rearrange("p k c -> p (k c)"), rows[:, :, :].rearrange("p k c -> p (k c)"),
                              pA[:, :], ALU.add).then_inc(new_rows, 1)

        @block.scalar
        def _(act):
            act.wait_ge(const_ready, 1)
            act.wait_ge(gate_in, 16 * NGATE)

            def square(n, b):
                act.wait_ge(centered, n + 1)
                act.wait_ge(var_ready, n + 1)
                act.activation(sq[:, :, :], h[:, b % 2, :, :], ACT.Square).then_inc(squared, 1)

            def root(n, b):
                s = st[:, b % 2, 1, :]
                act.wait_ge(var_ready, n + 2)
                act.activation(s, s, ACT.Sqrt, bias=eps[:, 0:1], scale=1.0 / C).then_inc(std_ready, 1)

            def save(n, b):
                act.wait_ge(h_turned, n + 3)
                act.wait_ge(gates_ready, n + 1)
                act.activation(ht[:, b % 2, :], pH[b % 2][:, :], ACT.Copy).then_inc(ht_saved, 1)

            with act.Fori(0, NT) as t:
                for b in range(B + 1):
                    if b < B:
                        square(B * t + b, b)
                        root(B * t + b, b)
                    if b > 0:
                        save(B * t + b - 1, b - 1)
                act.wait_ge(gates_ready, B * t + B + 2)
                out = logits[:, bass.ds(t * TILE, TILE)].rearrange("q (p j m) -> q m j p", j=TS // 2, m=2)
                for m in range(2):
                    act.activation(out[:, m, :, :], pG[m][:, :].rearrange("q (j p) -> q j p", p=128), ACT.Identity,
                                   bias=gb[:, 0:1]).then_inc(logits_saved, 1)
            act.wait_ge(top_ready, 1)
            act.activation(ex[:, :], top[:, :], ACT.Exp, bias=neg_max[:, 0:1])
            act.wait_ge(at_ready, 1)
            act.activation(logits[:, :], logits[:, :], ACT.Exp, bias=neg_max[:, 0:1],
                           accum_out=zsum[:, 0:1]).then_inc(exp_ready, 1)
            act.wait_ge(dia_ready, 2)
            act.activation(idr[:, 0:4, :].rearrange("p k i -> p (k i)"), pB[:, :], ACT.Copy)
            act.activation(idr[:, 4:8, :].rearrange("p k i -> p (k i)"), pC[:, :], ACT.Copy).then_inc(idr_ready, 1)
            act.wait_ge(row_step, 1)
            act.activation(rs[:, 1, :], rs[:, 1, :], ACT.Sqrt, bias=eps[:, 0:1], scale=1.0 / C).then_inc(row_act, 1)
            act.wait_ge(pooled_turned, 1)
            act.activation(pooled_t[:, :], pD[0:C + 1, 0:128], ACT.Copy).then_inc(pooled_saved, 1)
            act.wait_ge(hid_ready, 1)
            act.activation(hid[:, :, :, :].rearrange("p m e b -> p (m e b)"), pH[0][:, 0:2 * E * B],
                           ACT.Gelu).then_inc(gelu_ready, 1)
            act.wait_ge(out_ready, 1)
            act.activation(out_t[:, :], pH[1][0:C, 0:128], ACT.Copy).then_inc(out_saved, 1)

        @block.tensor
        def _(pe):
            pe.wait_ge(const_ready, 1)
            pe.wait_ge(gate_in, 16 * NGATE)
            for m in range(2):
                ins = pe.transpose(pA[:, E * m:E * m + E], gate_rows[:, m, :], ident[0:E, 0:E])
            ins.then_inc(gate_turned, 1)
            pe.wait_ge(gate_ready, 1)
            pe.sem_inc(h_turned, 2)
            pe.sem_inc(gates_ready, 1)
            pe.sem_inc(ht_saved, 1)

            def turn(n, b):
                pe.wait_ge(h_ready, n + 3)
                pe.wait_ge(ht_saved, n + 1)
                for j in range(TS // 2):
                    ins = pe.transpose(pH[b % 2][:, 128 * j:128 * j + 128],
                                       h[:, b % 2, 2 * j:2 * j + 2, :].rearrange("p j c -> p (j c)"), ident[:, :])
                ins.then_inc(h_turned, 1)

            def gates(n, b, t):
                pe.wait_ge(ht_saved, n + 3)
                if b == 0:
                    pe.wait_ge(logits_saved, 2 * t + 1)
                for m in range(2):
                    ins = pe.matmul(pG[m][E * b:E * b + E, :], gate_cols[:, m, :], ht[:, b % 2, :],
                                    start=True, stop=True)
                ins.then_inc(gates_ready, 1)

            with pe.Fori(0, NT) as t:
                for b in range(B):
                    turn(B * t + b, b)
                    gates(B * t + b, b, t)
            pe.wait_ge(dia_ready, 1)
            for k in range(K):
                ins = pe.matmul([pB, pC][k // 4][:, 128 * (k % 4):128 * (k % 4) + 128], ones[:, :], dia[:, k, :],
                                start=True, stop=True)
            ins.then_inc(dia_ready, 1)
            pe.wait_ge(pooled_ready, 1)
            pe.transpose(pD[0:C + 1, 0:128], pooled[:, :], ident[:, :]).then_inc(pooled_turned, 1)
            pe.wait_ge(pooled_saved, 1)
            pe.wait_ge(w_in, 16 * (NW + 1))
            for e in range(E):
                for m in range(2):
                    o = (m * E + e) * B
                    ins = pe.matmul(pH[0][:, o:o + B], w1[:, e, 128 * m:128 * m + 128],
                                    pooled_t[:, e:128:E], start=True, stop=True)
            ins.then_inc(hid_ready, 1)
            pe.wait_ge(gelu_ready, 1)
            for e in range(E):
                o = pH[1][0:C, e:128:E]
                for m in range(2):
                    pe.matmul(o, w2[:, m, e, :], hid[:, m, e, :], start=(m == 0), stop=False)
                ins = pe.matmul(o, w2b[0:1, e, :], ones[0:1, 0:B], start=False, stop=True)
            ins.then_inc(out_ready, 1)
            pe.wait_ge(out_saved, 1)
            pe.transpose(pD[:, 0:C], out_t[:, :], ident[0:C, 0:C]).then_inc(out_turned, 1)
            pe.wait_ge(wt_ready, 1)
            for j in range(K):
                pe.wait_ge(same_ready, j + 1)
                for k in range(K):
                    pe.matmul(pA[:, C * k:C * k + C], same[:, j % 2, k, :], wt[:, j, :], start=(j == 0 and k == 0),
                              stop=(j == K - 1), skip_group_check=True)
                for k in range(j, K):
                    m = same_before[:, j % 2, :] if k == j else same[:, j % 2, k, :]
                    ins = pe.matmul(pB[:, k:k + 1], m, ones[:, 0:1], start=(j == 0 and k == 0), stop=(k == j),
                                    skip_group_check=True)
                ins.then_inc(summed, 1)


def stage_conv_bn(nc, tok, gamma, beta, w_lbp, w_1x1, b_1x1):
    TS = 8
    TILE = 128 * TS
    R, P2 = TILE // W, W // 2
    NT = S // TILE
    EPS_LN, EPS_BN = 1e-6, 1e-5
    with ExitStack() as ctx:
        a = Arena(nc, ctx, "cb")
        ident = a.sb("ident", [128, 128])
        halves = a.sb("halves", [128, 128])
        ones = a.sb("ones", [1, 128])
        brow = a.sb("brow", [1, 2, C])
        bias = a.sb("bias", [128, 1, 2, C])
        eps = a.sb("eps", [128, 2])
        gam = a.sb("gam", [128, 2])
        w_in_rows = a.sb("w_in_rows", [C, C, 9])
        w_rows = a.sb("w_rows", [C, 9, 2, C])
        w_tap = a.sb("w_tap", [128, 9, C])
        wc = a.sb("wc", [128, 3, 2, 128])
        w1_rows = a.sb("w1_rows", [128, 128])
        w1 = a.sb("w1", [128, 128])
        u = a.sb("u", [128, B, H, P2])
        xs = a.sb("xs", [128, 2, TS, C])
        h = a.sb("h", [128, 2, TS, C])
        sq = a.sb("sq", [128, TS, C])
        st = a.sb("st", [128, 2, 2, TS])
        stats = a.sb("stats", [128, B * NT, 6])
        mv = a.sb("mv", [128, 8])
        zero = a.sb("zero", [128, P2 + 2])
        xn = a.sb("xn", [128, 2, R + 2, P2])
        xb = a.sb("xb", [128, 2, R + 2, P2])
        y = a.sb("y", [128, 2, R, P2])
        pH = [a.ps(f"pH{i}", [128, 512]) for i in range(2)]
        pC = [a.ps(f"pC{i}", [128, 512]) for i in range(2)]
        pY = [a.ps(f"pY{i}", [128, 512]) for i in range(2)]
        pool_done = a.sem("pool_done")
        dve_done = a.sem("dve_done")
        zeros_ready = a.sem("zeros_ready")
        const_ready = a.sem("const_ready")
        w_in = a.sem("w_in")
        w_dup = a.sem("w_dup")
        w_turned = a.sem("w_turned")
        w_ready = a.sem("w_ready")
        x_in = [a.sem(f"x_in{i}") for i in range(2)]
        centered = a.sem("centered")
        squared = a.sem("squared")
        var_ready = a.sem("var_ready")
        std_ready = a.sem("std_ready")
        h_ready = a.sem("h_ready")
        h_turned = a.sem("h_turned")
        u_saved = a.sem("u_saved")
        stats_ready = a.sem("stats_ready")
        mean_in = a.sem("mean_in")
        mean_out = a.sem("mean_out")
        bn_std = a.sem("bn_std")
        bn_ready = a.sem("bn_ready")
        r_in = [a.sem(f"r_in{i}") for i in range(2)]
        r_biased = a.sem("r_biased")
        xn_ready = a.sem("xn_ready")
        conv_ready = a.sem("conv_ready")
        y_ready = a.sem("y_ready")
        mixed = a.sem("mixed")
        sum_ready = a.sem("sum_ready")
        stored = [a.sem(f"stored{i}") for i in range(2)]
        block = ctx.enter_context(nc.Block())
        NW = 2 + 1 + 4 + 1
        BN_LINKS = 12

        def over_strips(eng, body, link=None, per=0):
            start = (link.base + link.n) if link else 0

            def strip(b, i, n, par, top, bottom):
                if link:
                    link.base, link.n = start + n * per, 0
                body(b, i, n, par, top, bottom)
                assert not link or link.n == per, link.n

            with eng.Fori(0, B) as b:
                strip(b, 0, b * NT, 0, True, False)
                with eng.Fori(0, NT // 2 - 1) as t:
                    for k in range(2):
                        strip(b, 2 * t + 1 + k, b * NT + 2 * t + 1 + k, (1 + k) % 2, False, False)
                strip(b, NT - 1, b * NT + NT - 1, 1, False, True)
            if link:
                link.base, link.n = start + B * NT * per, 0

        def tokens_by_pair(n):
            return tok[bass.ds(n * TILE, TILE), :].rearrange("(q p j) c -> p q (j c)", p=128, j=2)

        @block.sync
        def _(sp):
            sp.dma_start(w_in_rows[:, :, :], w_lbp.rearrange("o i a b -> o i (a b)")).then_inc(w_in, 16)
            sp.dma_start(brow[:, 0, :], b_1x1.rearrange("(a c) -> a c", a=1)).then_inc(w_in, 16)
            sp.wait_ge(zeros_ready, 1)
            for p in range(2):
                part = slice(64 * p, 64 * p + 64)
                sp.dma_start(w1_rows[part, part], w_1x1.rearrange("o i a b -> o (i a b)")).then_inc(w_in, 16)
                sp.dma_start(gam[part, 0:1], gamma.rearrange("(c a) -> c a", a=1)).then_inc(w_in, 16)
                sp.dma_start(gam[part, 1:2], beta.rearrange("(c a) -> c a", a=1)).then_inc(w_in, 16)
            with sp.Fori(0, NT) as t:
                for b in range(B):
                    sp.wait_ge(h_ready, B * t + b + 1)
                    sp.dma_start(xs[:, b % 2, :, :], tok[bass.ds(b * S + t * TILE, TILE), :].rearrange(
                        "(p j) c -> p j c", j=TS)).then_inc(x_in[b % 2], 16)
            sp.wait_ge(h_ready, B * NT + 2)

            def load(n, par):
                sp.wait_ge(sum_ready, n + 1)
                sp.dma_start(xs[:, par, :, :].rearrange("p (q j) c -> p q (j c)", j=2),
                             tokens_by_pair(n)).then_inc(r_in[par], 16)

            def store(n, par):
                sp.wait_ge(sum_ready, n + 3)
                sp.dma_start(tokens_by_pair(n), h[:, par, :, :].rearrange(
                    "p (q j) c -> p q (j c)", j=2)).then_inc(stored[par], 16)

            load(0, 0)
            with sp.Fori(0, B * NT // 2 - 1) as t:
                for par in range(2):
                    load(2 * t + par + 1, 1 - par)
                    store(2 * t + par, par)
            load(B * NT - 1, 1)
            for par in range(2):
                store(B * NT - 2 + par, par)
            for par in range(2):
                sp.wait_ge(stored[par], 16 * B * NT // 2 + 16)

        @block.gpsimd
        def _(pool):
            link = Link(pool, pool_done)
            for s in (var_ready, conv_ready, u_saved, y_ready):
                pool.sem_inc(s, 1)
            for s in stored:
                pool.sem_inc(s, 16)
            pool.memset(w1_rows[:, :], 0.0).then_inc(zeros_ready, 1)
            pool.memset(zero[:, :], 0.0)
            pool.memset(xb[:, :, :, :], 0.0)
            pool.memset(wc[:, :, :, :], 0.0)
            pool.memset(eps[:, 0:1], EPS_LN)
            pool.memset(eps[:, 1:2], EPS_BN)
            pool.memset(ones[:, :], 1.0)
            pool.memset(halves[:, :], 0.0)
            eye(pool, link, ident[:, :])
            for k in (0, 64, -64):
                link(pool.affine_select(out=halves[:, :], in_=halves[:, :], compare_op=ALU.not_equal, fill=0.5,
                                        base=k, pattern=[[-1, 128]], channel_multiplier=1))
            pool.sem_inc(const_ready, 1)
            pool.sem_inc(h_ready, 2)
            pool.sem_inc(sum_ready, 2)
            pool.wait_ge(bn_ready, 1)

            def add_bias(b, i, n, par, top, bottom):
                pool.wait_ge(r_in[par], 8 * (n - par) + 16)
                v = xs[:, par, :, :].rearrange("p (q j) c -> p q (j c)", j=2)
                pool.tensor_tensor(v, v, bias[:, :, :, :].rearrange("p a j c -> p a (j c)").to_broadcast([128, 4, 128]),
                                   ALU.add).then_inc(r_biased, 1)

            over_strips(pool, add_bias)

        @block.vector
        def _(dve):
            link = Link(dve, dve_done)
            dve.wait_ge(w_in, 16 * NW)
            dve.wait_ge(const_ready, 1)
            for d in range(2):
                ins = dve.tensor_copy(w_rows[:, :, d, :], w_in_rows[:, :, :].rearrange("o i k -> o k i"))
            link(dve.tensor_copy(brow[:, 1, :], brow[:, 0, :]))
            dve.sem_inc(w_dup, 1)
            dve.wait_ge(w_turned, 1)
            link(dve.tensor_copy(w_tap[:, 0:8, :].rearrange("p k o -> p (k o)"), pH[0][:, :]))
            link(dve.tensor_copy(w_tap[:, 8, :], pH[1][:, 0:64]))
            dve.tensor_copy(bias[:, 0, :, :].rearrange("p j c -> p (j c)"), pH[1][:, 64:192])
            dve.tensor_copy(w1[:, :], pC[0][:, 0:128])
            for m, pi, po, tap in parity_blocks(3, 1):
                rows, cols = slice(64 * pi, 64 * pi + 64), slice(64 * po, 64 * po + 64)
                ins = dve.tensor_copy(wc[rows, :, abs(m), cols], w_tap[rows, tap:9:3, :])
            ins.then_inc(w_ready, 1)

            def center(t, n, b):
                par = b % 2
                dve.wait_ge(x_in[par], 16 * (2 * t + b // 2 + 1))
                s = st[:, par, 0, :]
                link(dve.tensor_reduce(s, xs[:, par, :, :], AX.X, ALU.add))
                link(dve.tensor_scalar(s, s, 1.0 / C, None, ALU.mult))
                dve.wait_ge(h_turned, n + 1)
                dve.tensor_tensor(h[:, par, :, :], xs[:, par, :, :], bcast(s, TS), ALU.subtract).then_inc(centered, 1)

            def scale(t, n, b):
                par = b % 2
                s = st[:, par, 1, :]
                dve.wait_ge(squared, n + 1)
                dve.tensor_reduce(s, sq[:, :, :], AX.X, ALU.add).then_inc(var_ready, 1)
                dve.wait_ge(std_ready, n + 1)
                link(dve.reciprocal(s, s))
                dve.tensor_tensor(h[:, par, :, :], h[:, par, :, :], bcast(s, TS), ALU.mult).then_inc(h_ready, 1)

            def gather_stats(t, n, b):
                dve.wait_ge(u_saved, n + 3)
                dve.bn_stats(stats[:, n, :], u[:, b, bass.ds(t * R, R), :]).then_inc(stats_ready, 1)

            PER = 3 * B
            start = link.base + link.n
            with dve.Fori(0, NT) as t:
                link.base, link.n = start + t * PER, 0
                for b in range(B + 2):
                    if b < B:
                        center(t, B * t + b, b)
                    if 0 < b <= B:
                        scale(t, B * t + b - 1, b - 1)
                    if b > 1:
                        gather_stats(t, B * t + b - 2, b - 2)
                assert link.n == PER
            link.base, link.n = start + NT * PER, 0
            dve.wait_ge(stats_ready, B * NT)
            mean, var, avg, dev, sc, sh = (mv[:, k:k + 1] for k in range(6))
            link(dve.bn_aggr(mv[:, 0:2], stats[:, :, :].rearrange("p n s -> p (n s)")))
            dve.sem_inc(mean_in, 1)
            dve.wait_ge(mean_out, 1)
            link(dve.tensor_copy(avg, pC[0][:, 0:1]))
            link(dve.tensor_tensor(dev, mean, avg, ALU.subtract))
            link(dve.tensor_tensor(dev, dev, dev, ALU.mult))
            link(dve.tensor_tensor(var, var, dev, ALU.add))
            dve.sem_inc(mean_in, 1)
            dve.wait_ge(bn_std, 1)
            link(dve.reciprocal(sc, sc))
            link(dve.tensor_tensor(sc, sc, gam[:, 0:1], ALU.mult))
            link(dve.tensor_tensor(sh, avg, sc, ALU.mult))
            dve.tensor_tensor(sh, gam[:, 1:2], sh, ALU.subtract).then_inc(bn_ready, 1)

            def add_relu(b, i, n, par):
                dve.wait_ge(conv_ready, n + 3)
                dve.wait_ge(mixed, n + 1)
                dve.scalar_tensor_tensor(y[:, par, :, :].rearrange("p r w -> p (r w)"), pC[par][:, :], 0.0,
                                         u_flat(b, i), ALU.max, ALU.add).then_inc(y_ready, 1)

            def u_flat(b, i):
                return u[:, :, :, :].rearrange("p b r w -> p (b r w)")[:, bass.ds((b * H + i * R) * P2, R * P2)]

            def add_rest(n, par):
                dve.wait_ge(mixed, n + 3)
                dve.wait_ge(r_biased, n + 1)
                dve.wait_ge(stored[par], 8 * (n - par) + 16)
                dve.tensor_tensor(h[:, par, :, :].rearrange("p t c -> p (t c)"),
                                  xs[:, par, :, :].rearrange("p t c -> p (t c)"), pY[par][:, :], ALU.add).then_inc(sum_ready, 1)

            def strip(b, i, n, par, top, bottom):
                add_relu(b, i, n, par)
                add_rest(n, par)

            over_strips(dve, strip)

        @block.scalar
        def _(act):
            act.wait_ge(const_ready, 1)

            def square(n, b):
                act.wait_ge(centered, n + 1)
                act.wait_ge(var_ready, n + 1)
                act.activation(sq[:, :, :], h[:, b % 2, :, :], ACT.Square).then_inc(squared, 1)

            def root(n, b):
                s = st[:, b % 2, 1, :]
                act.wait_ge(var_ready, n + 2)
                act.activation(s, s, ACT.Sqrt, bias=eps[:, 0:1], scale=1.0 / C).then_inc(std_ready, 1)

            def save(t, n, b):
                act.wait_ge(h_turned, n + 3)
                dst = u[:, b, bass.ds(t * R, R), :].rearrange("q r (a j) -> q j r a", j=TS // 2)
                act.activation(dst, pH[b % 2][:, :].rearrange("q (j r a) -> q j r a", j=TS // 2, r=R),
                               ACT.Copy).then_inc(u_saved, 1)

            with act.Fori(0, NT) as t:
                for b in range(B + 1):
                    if b < B:
                        square(B * t + b, b)
                        root(B * t + b, b)
                    if b > 0:
                        save(t, B * t + b - 1, b - 1)
            act.wait_ge(mean_out, 2)
            act.activation(mv[:, 4:5], pC[1][:, 0:1], ACT.Sqrt, bias=eps[:, 1:2]).then_inc(bn_std, 1)
            act.wait_ge(bn_ready, 1)

            def normalise(b, i, n, par, top, bottom):
                act.wait_ge(conv_ready, n + 1)
                r0, r1 = int(top), R + 2 - int(bottom)
                kw = dict(bias=mv[:, 5:6], scale=mv[:, 4:5])
                if top or bottom:
                    z = 0 if top else R + 1
                    act.activation(xn[:, par, z, :], zero[:, 0:P2], ACT.Copy)
                    act.activation(xb[:, par, z, :], zero[:, 0:P2], ACT.Copy)
                src = u[:, b, bass.ds(i * R + r0 - 1, r1 - r0), :]
                act.activation(xn[:, par, r0:r1, :], src, ACT.Identity, **kw)
                for p in range(2):
                    rows = slice(64 * p, 64 * p + 64)
                    ins = act.activation(xb[rows, par, r0:r1, p:P2 - 1 + p], u[rows, b, bass.ds(i * R + r0 - 1, r1 - r0),
                                         1 - p:P2 - p], ACT.Identity, bias=mv[rows, 5:6], scale=mv[rows, 4:5])
                ins.then_inc(xn_ready, 1)

            def strip(b, i, n, par, top, bottom):
                normalise(b, i, n, par, top, bottom)

            over_strips(act, strip)

        @block.tensor
        def _(pe):
            pe.wait_ge(const_ready, 1)
            pe.wait_ge(w_dup, 1)
            for k in range(9):
                pe.transpose(pH[k // 8][:, 64 * (k % 8):64 * (k % 8) + 64],
                             w_rows[:, k, :, :].rearrange("o d i -> o (d i)"), ident[0:C, 0:C])
            pe.matmul(pH[1][:, 64:192], ones[:, :], brow[:, :, :].rearrange("a j c -> a (j c)"), start=True, stop=True)
            pe.transpose(pC[0][:, 0:128], w1_rows[:, :], ident[:, :]).then_inc(w_turned, 1)
            pe.wait_ge(w_ready, 1)
            pe.sem_inc(h_turned, 2)
            pe.sem_inc(u_saved, 1)
            pe.sem_inc(y_ready, 1)
            pe.sem_inc(mixed, 2)
            pe.sem_inc(conv_ready, 1)

            def turn(n, b):
                pe.wait_ge(h_ready, n + 3)
                pe.wait_ge(u_saved, n + 1)
                for j in range(TS // 2):
                    ins = pe.transpose(pH[b % 2][:, 128 * j:128 * j + 128],
                                       h[:, b % 2, 2 * j:2 * j + 2, :].rearrange("p j c -> p (j c)"), ident[:, :])
                ins.then_inc(h_turned, 1)

            with pe.Fori(0, NT) as t:
                for b in range(B):
                    turn(B * t + b, b)
            for k in range(2):
                pe.wait_ge(mean_in, k + 1)
                pe.matmul(pC[k][:, 0:1], halves[:, :], mv[:, k:k + 1], start=True, stop=True).then_inc(mean_out, 1)

            def strip(b, i, n, par, top, bottom):
                pe.wait_ge(xn_ready, n + 1)
                pe.wait_ge(y_ready, n + 1)
                for k in range(3):
                    for beside, src in enumerate((xn, xb)):
                        ins = pe.matmul(pC[par][:, :], wc[:, k, beside, :], src[:, par, k:k + R, :],
                                        start=(k == 0 and not beside), stop=(k == 2 and beside == 1))
                ins.then_inc(conv_ready, 1)
                pe.wait_ge(y_ready, n + 3)
                pe.wait_ge(sum_ready, n + 1)
                yt = y[:, par, :, :].rearrange("p r w -> p (r w)")
                for q in range(4):
                    ins = pe.matmul(pY[par][:, 128 * q:128 * q + 128], yt[:, 128 * q:128 * q + 128], w1[:, :],
                                    start=True, stop=True)
                ins.then_inc(mixed, 1)

            over_strips(pe, strip)


def stage_top2_ffn(nc, stage, tok, router_w, router_b, expert_w, expert_b, image=None):
    E = 8
    TS = 8
    TILE = 128 * TS
    N = B * S // TILE
    EPS = 1e-5
    BIG = 1e30
    with ExitStack() as ctx:
        a = Arena(nc, ctx, stage)
        ident = a.sb("ident", [128, 128])
        eps = a.sb("eps", [128, 1])
        order = a.sb("order", [128, E])
        order_i = a.sb("order_i", [128, E], mybir.dt.int32)
        rw = a.sb("rw", [C + 1, E])
        ew = a.sb("ew", [C + 1, E, C])
        xs = a.sb("xs", [128, 3, TS, C])
        h = a.sb("h", [128, 2, TS, C + 1])
        sq = a.sb("sq", [128, TS, C])
        st = a.sb("st", [128, 2, 2, TS])
        ht = a.sb("ht", [C + 1, 2, TS, 128])
        lg = a.sb("lg", [128, TS, E])
        eq = a.sb("eq", [128, TS, E])
        one = a.sb("one", [128, 2, TS, E])
        mx = a.sb("mx", [128, 4, TS])
        ex = a.sb("ex", [128, 2, TS])
        gt = a.sb("gt", [128, 2, TS])
        gates = a.sb("gates", [128, 2, TS, E])
        prod = a.sb("prod", [128, 4, E, C])
        part = a.sb("part", [128, 2, 2, 4, C])
        y = a.sb("y", [128, 2, TS, C])
        yt = a.sb("yt", [128, 2, TS // 2, 128])
        pT = [a.ps(f"pT{i}", [128, 512]) for i in range(2)]
        pL = a.ps("pL", [128, 512])
        pE = [a.ps(f"pE{i}", [128, 512]) for i in range(4)]
        pY = a.ps("pY", [128, 512])
        pool_done = a.sem("pool_done")
        pool_step = a.sem("pool_step")
        dve_done = a.sem("dve_done")
        const_ready = a.sem("const_ready")
        w_in = a.sem("w_in")
        x_in = [a.sem(f"x_in{i}") for i in range(3)]
        centered = a.sem("centered")
        squared = a.sem("squared")
        var_ready = a.sem("var_ready")
        std_ready = a.sem("std_ready")
        h_ready = a.sem("h_ready")
        h_turned = a.sem("h_turned")
        ht_saved = a.sem("ht_saved")
        logits_ready = a.sem("logits_ready")
        gap_ready = a.sem("gap_ready")
        gap_exp = a.sem("gap_exp")
        experts_ready = a.sem("experts_ready")
        weighted = a.sem("weighted")
        summed = a.sem("summed")
        y_ready = a.sem("y_ready")
        y_turned = a.sem("y_turned")
        yt_saved = a.sem("yt_saved")
        stored = [a.sem(f"stored{i}") for i in range(2)]
        block = ctx.enter_context(nc.Block())
        UN = 6

        def over_tiles(eng, body, link=None, per=0, tiles=N):
            loops, rest = divmod(tiles, UN)
            start = (link.base + link.n) if link else 0

            def tile(n, k):
                if link:
                    link.base, link.n = start + n * per, 0
                body(n, k)
                assert not link or link.n == per, link.n

            with eng.Fori(0, loops) as t:
                for k in range(UN):
                    tile(UN * t + k, k)
            for k in range(rest):
                tile(UN * loops + k, k)

        def tokens(n):
            rows = tok[bass.ds(n * TILE, TILE), :]
            return rows.rearrange("(p j) c -> p j c", j=TS) if image is None else rows.rearrange("(r w) c -> w r c", w=W)

        def image_rows(n):
            b, i = n // (H // TS), n % (H // TS)
            v = image[bass.ds(b, 1), :, bass.ds(i * TS, TS), :].rearrange("a c (q r) w -> r (a c) q w", r=2)
            return [v[r] for r in range(2)]

        @block.sync
        def _(sp):
            sp.dma_start(rw[0:C, :], router_w).then_inc(w_in, 16)
            sp.dma_start(rw[C:C + 1, :], router_b.rearrange("(a e) -> a e", a=1)).then_inc(w_in, 16)
            sp.dma_start(ew[0:C, :, :], expert_w.rearrange("e d c -> d e c")).then_inc(w_in, 16)
            sp.dma_start(ew[C:C + 1, :, :], expert_b.rearrange("(a e) c -> a e c", a=1)).then_inc(w_in, 16)

            def load(n, k):
                sp.wait_ge(y_ready, n + 1)
                sp.dma_start(xs[:, k % 3, :, :], tokens(n)).then_inc(x_in[k % 3], 16)

            def store(n, k):
                if image is None:
                    sp.wait_ge(y_ready, n + 4)
                    sp.dma_start(tokens(n), y[:, k % 2, :, :]).then_inc(stored[k % 2], 16)
                else:
                    sp.wait_ge(yt_saved, n + 2)
                    for r in range(2):
                        dst = image_rows(n)[r]
                        sp.dma_start(dst, yt[64 * r:64 * r + 64, k % 2, :, :]).then_inc(stored[k % 2], 16)

            def tile(n, k):
                load(n + 2, k + 2)
                store(n, k)

            load(0, 0)
            load(1, 1)
            over_tiles(sp, tile, tiles=N - 2)
            for n in (N - 2, N - 1):
                store(n, n)
            for k in range(2):
                sp.wait_ge(stored[k], 16 * (1 if image is None else 2) * N // 2 + 16)

        @block.gpsimd
        def _(pool):
            link = Link(pool, pool_done)
            for s in (ht_saved, gap_ready, yt_saved):
                pool.sem_inc(s, 1)
            for s in stored:
                pool.sem_inc(s, 16)
            pool.memset(eps[:, :], EPS)
            pool.memset(h[:, :, :, :], 1.0)
            eye(pool, link, ident[:, :])
            pool.iota(order_i[:, :], pattern=[[-1, E]], base=E, channel_multiplier=0).then_inc(const_ready, 1)
            pool.sem_inc(y_ready, 3)
            step = Link(pool, pool_step)

            def combine(n, k):
                for q in range(4):
                    pool.wait_ge(weighted, 8 * n + 2 * q + 6)
                    pq = part[:, q % 2, :, :, :]
                    pr = prod[:, 2 * (q % 2):2 * (q % 2) + 2, :, :]
                    pool.tensor_tensor(pq, pr[:, :, 0:4, :], pr[:, :, 4:8, :], ALU.add).then_inc(summed, 1)
                    pool.wait_ge(summed, 4 * n + q + 3)
                    step(pool.tensor_tensor(pq[:, :, 0:2, :], pq[:, :, 0:2, :], pq[:, :, 2:4, :], ALU.add))
                    step(pool.tensor_tensor(pq[:, :, 0, :], pq[:, :, 0, :], pq[:, :, 1, :], ALU.add))
                    if q == 0:
                        if image is None:
                            pool.wait_ge(stored[k % 2], 8 * (n - k % 2) + 16)
                        else:
                            pool.wait_ge(y_turned, n + 1)
                    ins = pool.tensor_tensor(y[:, k % 2, 2 * q:2 * q + 2, :], pq[:, :, 0, :],
                                             xs[:, k % 3, 2 * q:2 * q + 2, :], ALU.add)
                ins.then_inc(y_ready, 1)

            over_tiles(pool, combine, step, 8)

        @block.vector
        def _(dve):
            link = Link(dve, dve_done)
            dve.wait_ge(const_ready, 1)
            link(dve.tensor_copy(order[:, :], order_i[:, :]))

            def center(n, k):
                x, s = xs[:, k % 3, :, :], st[:, k % 2, 0, :]
                dve.wait_ge(x_in[k % 3], 16 * ((n - k % 3) // 3 + 1))
                link(dve.tensor_reduce(s, x, AX.X, ALU.add))
                link(dve.tensor_scalar(s, s, 1.0 / C, None, ALU.mult))
                dve.wait_ge(h_turned, n + 1)
                dve.tensor_tensor(h[:, k % 2, :, 0:C], x, bcast(s, TS), ALU.subtract).then_inc(centered, 1)

            def scale(n, k):
                s = st[:, k % 2, 1, :]
                dve.wait_ge(squared, n + 1)
                dve.tensor_reduce(s, sq[:, :, :], AX.X, ALU.add).then_inc(var_ready, 1)
                dve.wait_ge(std_ready, n + 1)
                link(dve.reciprocal(s, s))
                v = h[:, k % 2, :, 0:C]
                dve.tensor_tensor(v, v, bcast(s, TS), ALU.mult).then_inc(h_ready, 1)

            def pick(which, n):
                m, o = mx[:, which, :], one[:, which, :, :]
                link(dve.tensor_reduce(m, lg[:, :, :], AX.X, ALU.max))
                link(dve.tensor_tensor(eq[:, :, :], lg[:, :, :], bcast(m, TS, E), ALU.is_equal))
                link(dve.tensor_tensor(eq[:, :, :], eq[:, :, :], order[:, :].unsqueeze(1).to_broadcast([128, TS, E]),
                                       ALU.mult))
                link(dve.tensor_reduce(mx[:, 2 + which, :], eq[:, :, :], AX.X, ALU.max))
                link(dve.tensor_tensor(o, eq[:, :, :], bcast(mx[:, 2 + which, :], TS, E), ALU.is_equal))

            def route(n, k):
                dve.wait_ge(logits_ready, n + 1)
                link(dve.tensor_copy(lg[:, :, :].rearrange("p t e -> p (t e)"), pL[:, 0:TS * E]))
                pick(0, n)
                link(dve.scalar_tensor_tensor(lg[:, :, :].rearrange("p t e -> p (t e)"),
                                              one[:, 0, :, :].rearrange("p t e -> p (t e)"), -BIG,
                                              lg[:, :, :].rearrange("p t e -> p (t e)"), ALU.mult, ALU.add))
                pick(1, n)
                dve.tensor_tensor(ex[:, k % 2, :], mx[:, 1, :], mx[:, 0, :], ALU.subtract).then_inc(gap_ready, 1)
                dve.wait_ge(gap_exp, n + 1)
                link(dve.tensor_scalar(gt[:, 0, :], ex[:, k % 2, :], 1.0, None, ALU.add))
                link(dve.reciprocal(gt[:, 0, :], gt[:, 0, :]))
                link(dve.tensor_tensor(gt[:, 1, :], ex[:, k % 2, :], gt[:, 0, :], ALU.mult))
                link(dve.tensor_tensor(one[:, 0, :, :], one[:, 0, :, :], bcast(gt[:, 0, :], TS, E), ALU.mult))
                link(dve.tensor_tensor(one[:, 1, :, :], one[:, 1, :, :], bcast(gt[:, 1, :], TS, E), ALU.mult))
                link(dve.tensor_tensor(gates[:, k % 2, :, :], one[:, 0, :, :], one[:, 1, :, :], ALU.add))

            def weigh(n, k):
                for j in range(TS):
                    dve.wait_ge(experts_ready, 8 * n + j + 1)
                    if j % 2 == 0:
                        dve.wait_ge(summed, 4 * n + j // 2 + 1)
                    dve.tensor_tensor(prod[:, j % 4, :, :], pE[j % 4][:, :].rearrange("p (e c) -> p e c", e=E),
                                      bcast(gates[:, k % 2, j, :], E), ALU.mult).then_inc(weighted, 1)

            def tile(n, k):
                center(n, k)
                scale(n, k)
                route(n, k)
                weigh(n, k)

            over_tiles(dve, tile, link, 3 + 1 + 5 + 1 + 5 + 6)

        @block.scalar
        def _(act):
            act.wait_ge(const_ready, 1)

            def tile(n, k):
                act.wait_ge(centered, n + 1)
                act.activation(sq[:, :, :], h[:, k % 2, :, 0:C], ACT.Square).then_inc(squared, 1)
                s = st[:, k % 2, 1, :]
                act.wait_ge(var_ready, n + 1)
                act.activation(s, s, ACT.Sqrt, bias=eps[:, 0:1], scale=1.0 / C).then_inc(std_ready, 1)
                for m in range(2):
                    act.wait_ge(h_turned, n + 3)
                    act.activation(ht[:, k % 2, 4 * m:4 * m + 4, :].rearrange("c t p -> c (t p)"), pT[m][0:C + 1, :],
                                   ACT.Copy).then_inc(ht_saved, 1)
                act.wait_ge(gap_ready, n + 2)
                act.activation(ex[:, k % 2, :], ex[:, k % 2, :], ACT.Exp).then_inc(gap_exp, 1)
                if image is not None:
                    act.wait_ge(y_turned, n + 3)
                    act.wait_ge(stored[k % 2], 8 * 2 * (n - k % 2) + 16)
                    act.activation(yt[:, k % 2, :, :].rearrange("p q w -> p (q w)"), pY[:, :],
                                   ACT.Copy).then_inc(yt_saved, 1)

            over_tiles(act, tile)

        @block.tensor
        def _(pe):
            pe.wait_ge(const_ready, 1)
            pe.wait_ge(w_in, 16 * 4)
            pe.sem_inc(h_turned, 2)
            pe.sem_inc(y_turned, 2)
            pe.sem_inc(summed, 2)
            pe.sem_inc(weighted, 4)

            def tile(n, k):
                pe.wait_ge(h_ready, n + 1)
                pe.wait_ge(ht_saved, 2 * n + 1)
                for j in range(TS):
                    ins = pe.transpose(pT[j // 4][0:C + 1, 128 * (j % 4):128 * (j % 4) + 128], h[:, k % 2, j, :],
                                       ident[:, :])
                ins.then_inc(h_turned, 1)
                pe.wait_ge(ht_saved, 2 * n + 3)
                pe.wait_ge(gap_ready, n + 1)
                for j in range(TS):
                    ins = pe.matmul(pL[:, E * j:E * j + E], ht[:, k % 2, j, :], rw[:, :], start=True, stop=True)
                ins.then_inc(logits_ready, 1)
                for j in range(TS):
                    pe.wait_ge(weighted, 8 * n + j + 1)
                    pe.matmul(pE[j % 4][:, :], ht[:, k % 2, j, :], ew[:, :, :].rearrange("d e c -> d (e c)"),
                              start=True, stop=True).then_inc(experts_ready, 1)
                if image is not None:
                    pe.wait_ge(y_ready, n + 4)
                    pe.wait_ge(yt_saved, n + 1)
                    for q in range(4):
                        ins = pe.transpose(pY[:, 128 * q:128 * q + 128],
                                           y[:, k % 2, 2 * q:2 * q + 2, :].rearrange("w r c -> w (r c)"), ident[:, :])
                    ins.then_inc(y_turned, 1)

            over_tiles(pe, tile)


def stage_sweeps(nc, tok, kernels):
    TS = 8
    TILE = 128 * TS
    R, P2 = TILE // W, W // 2
    NT = S // TILE
    KW = 9
    PAD = 2
    EPS = 1e-6
    STEPS = H - 1
    BL = 8
    NB = W // BL
    with ExitStack() as ctx:
        a = Arena(nc, ctx, "sw")
        ident = a.sb("ident", [128, 128])
        eps = a.sb("eps", [128, 1])
        k_in = a.sb("k_in", [C, 2, KW, C])
        k_dup = a.sb("k_dup", [C, KW, 2, C])
        k_tap = a.sb("k_tap", [128, KW, C])
        wc = a.sb("wc", [128, 4, 5, 128])
        xs = a.sb("xs", [128, 2, TS, C])
        h = a.sb("h", [128, 2, TS, C])
        sq = a.sb("sq", [128, TS, C])
        st = a.sb("st", [128, 2, 2, TS])
        y = a.sb("y", [128, B, H, P2])
        row = [[a.sb(f"row{p}{c}", [128, 2, P2 + 2 * PAD]) for c in range(2)] for p in range(2)]
        packed = [[a.sb(f"packed{p}{c}", [128, 2, P2]) for c in range(2)] for p in range(2)]
        swap = a.sb("swap", [64, 2, 8, P2])
        xw = a.sb("xw", [128, 2, 2, 2, BL, C])
        pH = [a.ps(f"pH{i}", [128, 512]) for i in range(2)]
        pC = [a.ps(f"pC{i}", [128, 512]) for i in range(2)]
        pT = [a.ps(f"pT{i}", [128, 512]) for i in range(2)]
        pool_done = a.sem("pool_done")
        dve_done = a.sem("dve_done")
        const_ready = a.sem("const_ready")
        k_loaded = [a.sem(f"k_loaded{i}") for i in range(2)]
        k_doubled = a.sem("k_doubled")
        k_turned = a.sem("k_turned")
        k_ready = a.sem("k_ready")
        x_in = [a.sem(f"x_in{i}") for i in range(2)]
        centered = a.sem("centered")
        squared = a.sem("squared")
        var_ready = a.sem("var_ready")
        std_ready = a.sem("std_ready")
        h_ready = a.sem("h_ready")
        h_turned = a.sem("h_turned")
        u_saved = a.sem("u_saved")
        row_ready = [a.sem(f"row_ready{c}") for c in range(2)]
        conv_ready = [a.sem(f"conv_ready{c}") for c in range(2)]
        saved = [a.sem(f"saved{c}") for c in range(2)]
        taken = a.sem("taken")
        moved = a.sem("moved")
        put_back = a.sem("put_back")
        pack_ready = [a.sem(f"pack_ready{c}") for c in range(2)]
        turned = [a.sem(f"turned{c}") for c in range(2)]
        added = [a.sem(f"added{c}") for c in range(2)]
        w_loaded = [a.sem(f"w_loaded{i}") for i in range(2)]
        stored = [a.sem(f"stored{i}") for i in range(2)]
        block = ctx.enter_context(nc.Block())
        CHUNKS = B * H // 2 // 8

        def images(c):
            return slice(2 * c, 2 * c + 2)

        def line(sweep, c, i):
            if sweep < 2:
                return y[:, images(c), bass.ds(i, 1), :].rearrange("p b a w -> p b (a w)")
            v = y[:, images(c), :, bass.ds(i[0], 1)].rearrange("p b (h m) a -> p b m (h a)", m=2)
            return v[:, :, i[1], :]

        def over_steps(eng, sweep, body):
            g0 = sweep * STEPS
            par0 = FIRST[sweep]

            def at(t, k):
                if sweep == 1:
                    return t * -2 + (H - 1 - k)
                return 2 * t + k if sweep == 0 else (t + k // 2, k % 2)

            with eng.Fori(0, (STEPS - 1) // 2) as t:
                for k in (1, 2):
                    body(at(t, k), g0 + 2 * t + k, (par0 + k) % 2)
            body(at(STEPS // 2, 1), g0 + STEPS, (par0 + STEPS) % 2)

        FIRST = [0, 1, 0, 1]

        def block_rows(c, w0):
            v = tok[2 * c * S:(2 * c + 2) * S, :].rearrange("(q m w) c -> q m w c", m=2, w=W)
            return v[:, :, bass.ds(w0, BL), :]

        def exchange(n, half, odd):
            b, q = n // (CHUNKS // B), n % (CHUNKS // B)
            v = y[64 * half:64 * half + 64, bass.ds(b, 1), bass.ds(16 * q, 16), :]
            return v.rearrange("p a (r m) w -> p m (a r) w", m=2)[:, odd, :, :]

        def over_chunks(eng, body):
            with eng.Fori(0, CHUNKS // 2) as t:
                for k in range(2):
                    body(2 * t + k, k)

        def over_blocks(eng, body):
            body(0, 0, True)
            with eng.Fori(0, NB // 2 - 1) as t:
                for k in range(2):
                    body(2 * t + 1 + k, (1 + k) % 2, False)
            body(NB - 1, 1, False)

        @block.sync
        def _(sp):
            for k in range(2):
                sp.dma_start(k_in[:, k, :, :], kernels[k].rearrange("o a k i -> o (a k) i")).then_inc(k_loaded[k], 16)
            for k in range(2, 4):
                sp.wait_ge(k_doubled, k - 1)
                sp.dma_start(k_in[:, k % 2, :, :], kernels[k].rearrange("o a k i -> o (a k) i")).then_inc(k_loaded[k % 2], 16)
            with sp.Fori(0, NT) as t:
                for b in range(B):
                    sp.wait_ge(h_ready, B * t + b + 1)
                    sp.dma_start(xs[:, b % 2, :, :], tok[bass.ds(b * S + t * TILE, TILE), :].rearrange(
                        "(p j) c -> p j c", j=TS)).then_inc(x_in[b % 2], 16)

            def load(w0, buf):
                for c in range(2):
                    for m in range(2):
                        sp.dma_start(xw[:, buf, c, m, :, :], block_rows(c, w0)[:, m, :, :]).then_inc(w_loaded[buf], 16)

            def store(i, w0, buf):
                for c in range(2):
                    sp.wait_ge(added[c], BL * (i + 1) + 1)
                    for m in range(2):
                        sp.dma_start(block_rows(c, w0)[:, m, :, :], xw[:, buf, c, m, :, :]).then_inc(stored[buf], 16)

            load(W - BL, 0)
            load(W - 2 * BL, 1)
            with sp.Fori(0, NB // 2 - 1) as t:
                for buf in range(2):
                    w0 = t * (-2 * BL) + (W - BL * (1 + buf))
                    w2 = t * (-2 * BL) + (W - BL * (3 + buf))
                    store(2 * t + buf, w0, buf)
                    sp.wait_ge(stored[buf], 64 * (t + 1))
                    load(w2, buf)
            for buf in range(2):
                store(NB - 2 + buf, BL * (1 - buf), buf)
            for buf in range(2):
                sp.wait_ge(stored[buf], 64 * NB // 2)

        @block.gpsimd
        def _(pool):
            link = Link(pool, pool_done)
            for s in (var_ready, put_back, u_saved):
                pool.sem_inc(s, 1)
            for s in pack_ready:
                pool.sem_inc(s, 1)
            for s in added:
                pool.sem_inc(s, 1)
            pool.memset(eps[:, :], EPS)
            pool.memset(wc[:, :, :, :], 0.0)
            for p in range(2):
                for c in range(2):
                    pool.memset(row[p][c][:, :, :], 0.0)
            eye(pool, link, ident[:, :])
            pool.sem_inc(const_ready, 1)
            pool.sem_inc(h_ready, 2)

        @block.vector
        def _(dve):
            link = Link(dve, dve_done)
            dve.wait_ge(const_ready, 1)
            for s in range(4):
                dve.wait_ge(k_loaded[s % 2], 16 * (s // 2 + 1))
                if s > 0:
                    dve.wait_ge(k_turned, s)
                dve.tensor_copy(k_dup[:, :, 0, :], k_in[:, s % 2, :, :])
                dve.tensor_copy(k_dup[:, :, 1, :], k_in[:, s % 2, :, :]).then_inc(k_doubled, 1)
                dve.wait_ge(k_turned, s + 1)
                link(dve.tensor_copy(k_tap[:, 0:8, :].rearrange("p k o -> p (k o)"), pH[0][:, :]))
                link(dve.tensor_copy(k_tap[:, 8, :], pH[1][:, 0:C]))
                for m, pi, po, tap in parity_blocks(KW, KW // 2):
                    rows, cols = slice(64 * pi, 64 * pi + 64), slice(64 * po, 64 * po + 64)
                    ins = dve.tensor_copy(wc[rows, s, m + 2, cols], k_tap[rows, tap, :])
                ins.then_inc(k_ready, 1)
                dve.wait_ge(k_ready, s + 1)

            def center(t, n, b):
                par = b % 2
                dve.wait_ge(x_in[par], 16 * (2 * t + b // 2 + 1))
                s = st[:, par, 0, :]
                link(dve.tensor_reduce(s, xs[:, par, :, :], AX.X, ALU.add))
                link(dve.tensor_scalar(s, s, 1.0 / C, None, ALU.mult))
                dve.wait_ge(h_turned, n + 1)
                dve.tensor_tensor(h[:, par, :, :], xs[:, par, :, :], bcast(s, TS), ALU.subtract).then_inc(centered, 1)

            def scale(t, n, b):
                par = b % 2
                s = st[:, par, 1, :]
                dve.wait_ge(squared, n + 1)
                dve.tensor_reduce(s, sq[:, :, :], AX.X, ALU.add).then_inc(var_ready, 1)
                dve.wait_ge(std_ready, n + 1)
                link(dve.reciprocal(s, s))
                dve.tensor_tensor(h[:, par, :, :], h[:, par, :, :], bcast(s, TS), ALU.mult).then_inc(h_ready, 1)

            PER = 3 * B
            start = link.base + link.n
            with dve.Fori(0, NT) as t:
                link.base, link.n = start + t * PER, 0
                for b in range(B + 1):
                    if b < B:
                        center(t, B * t + b, b)
                    if b > 0:
                        scale(t, B * t + b - 1, b - 1)
                assert link.n == PER
            link.base, link.n = start + NT * PER, 0

            def make(sweep, c, i, g, par, r=None):
                dve.wait_ge(conv_ready[c], g)
                if r is None:
                    dve.wait_ge(saved[c], g)
                else:
                    dve.wait_ge(pack_ready[c], r)
                dve.scalar_tensor_tensor(row[par][c][:, :, PAD:PAD + P2],
                                         pC[c][:, 0:2 * P2].rearrange("p (b w) -> p b w", b=2), 0.0,
                                         line(sweep, c, i), ALU.max, ALU.add).then_inc(row_ready[c], 1)

            dve.wait_ge(u_saved, B * NT + 2)
            for sweep in range(3):
                if sweep != 1:
                    for c in range(2):
                        if sweep == 2:
                            dve.wait_ge(put_back, CHUNKS + 1)
                            dve.wait_ge(moved, CHUNKS)
                        dve.tensor_copy(row[0][c][:, :, PAD:PAD + P2], line(sweep, c, 0 if sweep == 0 else (0, 0))).then_inc(row_ready[c], 1)
                over_steps(dve, sweep, lambda i, g, par: [make(sweep, c, i, g, par) for c in range(2)])
                if sweep == 1:
                    for c in range(2):
                        dve.wait_ge(saved[c], 2 * STEPS + 2)
                    def move(n, k):
                        dve.wait_ge(taken, n + 1)
                        lo = exchange(n, 0, 1)
                        dve.tensor_copy(exchange(n, 1, 0), lo).then_inc(moved, 1)
                    over_chunks(dve, move)
            for c in range(2):
                dve.wait_ge(saved[c], 3 * STEPS + 2)

            def add(c, r, s, buf):
                dve.wait_ge(turned[c], r + 1)
                dve.tensor_tensor(xw[:, buf, c, :, BL - 1 - s, :], xw[:, buf, c, :, BL - 1 - s, :],
                                  pT[c][:, 0:128].rearrange("q (m c) -> q m c", m=2), ALU.add).then_inc(added[c], 1)

            def last(i, buf, first):
                pair0 = i * (-BL // 2) + (NB - 1) * (BL // 2)
                dve.wait_ge(w_loaded[buf], 64 * ((i - buf) // 2 + 1))
                for s in range(BL + 1):
                    if s < BL and not (first and s == 0):
                        for c in range(2):
                            make(3, c, (pair0 + (BL - 1 - s) // 2, (BL - 1 - s) % 2), 3 * STEPS + BL * i + s, (FIRST[3] + s) % 2, BL * i + s)
                    if s > 0:
                        for c in range(2):
                            add(c, BL * i + s - 1, s - 1, buf)

            over_blocks(dve, last)

        @block.scalar
        def _(act):
            act.wait_ge(const_ready, 1)

            def square(n, b):
                act.wait_ge(centered, n + 1)
                act.wait_ge(var_ready, n + 1)
                act.activation(sq[:, :, :], h[:, b % 2, :, :], ACT.Square).then_inc(squared, 1)

            def root(n, b):
                s = st[:, b % 2, 1, :]
                act.wait_ge(var_ready, n + 2)
                act.activation(s, s, ACT.Sqrt, bias=eps[:, 0:1], scale=1.0 / C).then_inc(std_ready, 1)

            def save(t, n, b):
                act.wait_ge(h_turned, n + 3)
                dst = y[:, b, bass.ds(t * R, R), :].rearrange("q r (a j) -> q j r a", j=TS // 2)
                act.activation(dst, pH[b % 2][:, :].rearrange("q (j r a) -> q j r a", j=TS // 2, r=R),
                               ACT.Copy).then_inc(u_saved, 1)

            with act.Fori(0, NT) as t:
                for b in range(B + 1):
                    if b < B:
                        square(B * t + b, b)
                        root(B * t + b, b)
                    if b > 0:
                        save(t, B * t + b - 1, b - 1)

            def save_row(sweep, c, i, g, par, firsts):
                act.wait_ge(row_ready[c], g + firsts)
                act.activation(line(sweep, c, i), row[par][c][:, :, PAD:PAD + P2], ACT.Copy).then_inc(saved[c], 1)

            for sweep in range(3):
                firsts = 2 if sweep == 2 else 1
                over_steps(act, sweep, lambda i, g, par: [save_row(sweep, c, i, g, par, firsts) for c in range(2)])
                if sweep == 1:
                    for c in range(2):
                        act.wait_ge(saved[c], 2 * STEPS + 2)
                    def take(n, k):
                        act.wait_ge(put_back, n + 1)
                        act.activation(swap[:, k, :, :], exchange(n, 1, 0), ACT.Copy).then_inc(taken, 1)
                        act.wait_ge(moved, n + 1)
                        act.activation(exchange(n, 0, 1), swap[:, k, :, :], ACT.Copy).then_inc(put_back, 1)
                    over_chunks(act, take)

            def pack(i, buf, first):
                for s in range(BL):
                    r, par = BL * i + s, (FIRST[3] + s) % 2
                    for c in range(2):
                        act.wait_ge(row_ready[c], 3 * STEPS + 2 + r)
                        if not (first and s < 2):
                            act.wait_ge(turned[c], r - 1)
                        act.activation(packed[par][c][:, :, :], row[par][c][:, :, PAD:PAD + P2],
                                       ACT.Copy).then_inc(pack_ready[c], 1)

            over_blocks(act, pack)

        @block.tensor
        def _(pe):
            pe.wait_ge(const_ready, 1)
            for s in range(4):
                pe.wait_ge(k_doubled, s + 1)
                if s > 0:
                    pe.wait_ge(k_ready, s)
                for k in range(KW):
                    ins = pe.transpose(pH[k // 8][:, C * (k % 8):C * (k % 8) + C],
                                       k_dup[:, k, :, :].rearrange("o d i -> o (d i)"), ident[0:C, 0:C])
                ins.then_inc(k_turned, 1)
            pe.wait_ge(k_ready, 4)
            pe.sem_inc(h_turned, 2)
            pe.sem_inc(u_saved, 1)
            for c in range(2):
                pe.sem_inc(saved[c], 2)

            def turn(n, b):
                pe.wait_ge(h_ready, n + 3)
                pe.wait_ge(u_saved, n + 1)
                for j in range(TS // 2):
                    ins = pe.transpose(pH[b % 2][:, 128 * j:128 * j + 128],
                                       h[:, b % 2, 2 * j:2 * j + 2, :].rearrange("p j c -> p (j c)"), ident[:, :])
                ins.then_inc(h_turned, 1)

            with pe.Fori(0, NT) as t:
                for b in range(B):
                    turn(B * t + b, b)

            def conv(sweep, c, g, par, firsts):
                pe.wait_ge(row_ready[c], g - 1 + firsts)
                for m in range(5):
                    ins = pe.matmul(pC[c][:, 0:2 * P2], wc[:, sweep, m, :], row[1 - par][c][:, :, m:m + P2],
                                    start=(m == 0), stop=(m == 4))
                ins.then_inc(conv_ready[c], 1)

            for sweep in range(3):
                firsts = 2 if sweep == 2 else 1
                over_steps(pe, sweep, lambda i, g, par: [conv(sweep, c, g, par, firsts) for c in range(2)])

            def turn_out(c, r, par):
                pe.wait_ge(pack_ready[c], r + 2)
                pe.wait_ge(added[c], r + 1)
                pe.transpose(pT[c][:, 0:128], packed[par][c][:, :, :].rearrange("p b h -> p (b h)"),
                             ident[:, :]).then_inc(turned[c], 1)

            def last(i, buf, first):
                for s in range(BL + 1):
                    if s < BL and not (first and s == 0):
                        for c in range(2):
                            conv(3, c, 3 * STEPS + BL * i + s, (FIRST[3] + s) % 2, 2)
                    if s > 0:
                        for c in range(2):
                            turn_out(c, BL * i + s - 1, (FIRST[3] + s - 1) % 2)

            over_blocks(pe, last)


def stage_spread(nc, tok, w_d, w_dirs, bns):
    IT = 4
    NC = 4
    TS = 8
    NT = W // TS
    EPS_LN, EPS_BN = 1e-6, 1e-3
    SHIFTS = [H // 2 ** (IT - i) for i in range(IT)]
    UP = [(2, -s, 0) for s in SHIFTS]
    RIGHT = [(4, 0, s) for s in SHIFTS]
    LEFT = [(8, 0, -s) for s in SHIFTS]
    CONVS = UP + RIGHT + LEFT
    NP = 9 * len(CONVS) + 8 * IT
    SC, BI = 9 * len(CONVS), 9 * len(CONVS) + 4 * IT
    with ExitStack() as ctx:
        a = Arena(nc, ctx, "sp")
        eps = a.sb("eps", [128, 2])
        y = a.sb("y", [128, C, B, W])
        par = a.sb("par", [128, C, NP])
        roll = a.sb("roll", [128, IT, 128])
        diag = a.sb("diag", [128, IT + 2, 3, 128])
        cur = a.sb("cur", [128, NC, NP])
        work = a.sb("work", [128, 7168])
        st = a.sb("st", [128, 2, 2, TS])
        xs = work[:, 0:1536].rearrange("p (n t c) -> p n t c", n=3, t=TS)
        h = work[:, 2048:3072].rearrange("p (n t c) -> p n t c", n=2, t=TS)
        sq = work[:, 3072:3584].rearrange("p (t c) -> p t c", t=TS)
        x = work[:, 0:2048].rearrange("p (q n) -> p q n", q=NC)
        rel = work[:, 2048:4096].rearrange("p (q n) -> p q n", q=NC)
        band = work[:, 4096:7168].rearrange("p (q n k m) -> p q n k m", q=NC, n=2, k=3)
        raw = y[:, :, :, :].rearrange("p c b w -> p (c b w)")
        NW9 = IT * C * 9
        raw_w = [raw[:, NW9 * d:NW9 * (d + 1)] for d in range(3)]
        raw_bn = raw[:, 3 * NW9:3 * NW9 + 4 * IT * 4 * C].rearrange("p (d i k c) -> p d i k c", d=4, i=IT, k=4)
        raw_d = raw[:, 3 * NW9 + 16 * IT * C:3 * NW9 + 17 * IT * C].rearrange("p (i c) -> p i c", i=IT)
        pC = [a.ps(f"pC{i}", [128, 512]) for i in range(NC)]
        pool_done = a.sem("pool_done")
        dve_done = a.sem("dve_done")
        const_ready = a.sem("const_ready")
        p_in = a.sem("p_in")
        bn_var = a.sem("bn_var")
        bn_std = a.sem("bn_std")
        par_ready = a.sem("par_ready")
        x_in = [a.sem(f"x_in{i}") for i in range(2)]
        centered = a.sem("centered")
        squared = a.sem("squared")
        var_ready = a.sem("var_ready")
        std_ready = a.sem("std_ready")
        y_ready = a.sem("y_ready")
        cur_ready = a.sem("cur_ready")
        band_ready = [a.sem(f"band_ready{i}") for i in range(NC)]
        x_ready = [a.sem(f"x_ready{i}") for i in range(NC)]
        conv_ready = [a.sem(f"conv_ready{i}") for i in range(NC)]
        relu_ready = [a.sem(f"relu_ready{i}") for i in range(NC)]
        r_in = [a.sem(f"r_in{i}") for i in range(2)]
        sum_ready = a.sem("sum_ready")
        stored = [a.sem(f"stored{i}") for i in range(2)]
        block = ctx.enter_context(nc.Block())
        ITS = 4 * IT
        GROUPS = C // NC

        def tokens(n):
            v = tok[bass.ds(n // NT * S, S), :].rearrange("(h w) c -> h w c", h=H)
            return v[:, bass.ds(n % NT * TS, TS), :].rearrange("h t c -> h (t c)")

        def columns(n, b, t):
            v = y[:, :, bass.ds(b, 1), bass.ds(TS * t, TS)]
            return v.rearrange("p c a w -> p (a w) c")

        def channel(g, q):
            return y[:, bass.ds(NC * g + q, 1), :, :].rearrange("p a b w -> p (a b w)")

        def over_tiles(eng, body, link=None, per=0):
            start = (link.base + link.n) if link else 0
            with eng.Fori(0, B) as b:
                with eng.Fori(0, NT // 2) as t:
                    for k in range(2):
                        n = NT * b + 2 * t + k
                        if link:
                            link.base, link.n = start + n * per, 0
                        body(n, b, 2 * t + k, k)
                        assert not link or link.n == per, link.n
            if link:
                link.base, link.n = start + B * NT * per, 0

        def spans(dil, kw, roll_w):
            d, s = dil * (kw - 1), roll_w % W
            lo, hi, cut = max(0, -d), min(W, W - d), W - d - s
            return [(p, q, (p + d + s) % W) for p, q in ((lo, min(hi, cut)), (max(lo, cut), hi)) if p < q]

        @block.sync
        def _(sp):
            for d in range(3):
                sp.dma_start(raw_w[d], w_dirs[d].rearrange("i c a k m -> (i c a k m)").partition_broadcast(128)).then_inc(p_in, 16)
            for d in range(4):
                sp.dma_start(raw_bn[:, d, :, :, :].rearrange("p i k c -> p (i k c)"),
                             bns[d].rearrange("i k c -> (i k c)").partition_broadcast(128)).then_inc(p_in, 16)
            sp.dma_start(raw_d[:, :, :].rearrange("p i c -> p (i c)"),
                         w_d.rearrange("i c a k m -> (i c a k m)").partition_broadcast(128)).then_inc(p_in, 16)

            def load(n, b, t, k):
                sp.wait_ge(centered, n + 1)
                sp.dma_start(xs[:, k, :, :].rearrange("p t c -> p (t c)"), tokens(n)).then_inc(x_in[k], 16)

            over_tiles(sp, load)
            for q in range(NC):
                sp.wait_ge(x_ready[q], 17 * GROUPS + 1)

            def load_rest(n, k):
                sp.wait_ge(sum_ready, n + 1)
                sp.dma_start(xs[:, k, :, :].rearrange("p t c -> p (t c)"), tokens(n)).then_inc(r_in[k], 16)

            def store(n, k):
                sp.wait_ge(sum_ready, n + 3)
                sp.dma_start(tokens(n), h[:, k, :, :].rearrange("p t c -> p (t c)")).then_inc(stored[k], 16)

            load_rest(0, 0)
            with sp.Fori(0, B * NT // 2 - 1) as t:
                for k in range(2):
                    load_rest(2 * t + k + 1, 1 - k)
                    store(2 * t + k, k)
            load_rest(B * NT - 1, 1)
            for k in range(2):
                store(B * NT - 2 + k, k)
            for k in range(2):
                sp.wait_ge(stored[k], 16 * B * NT // 2 + 16)

        @block.gpsimd
        def _(pool):
            link = Link(pool, pool_done)
            for s in relu_ready:
                pool.sem_inc(s, 1)
            for s in stored:
                pool.sem_inc(s, 16)
            for s in x_ready:
                pool.sem_inc(s, 1)
            pool.memset(eps[:, 0:1], EPS_LN)
            pool.memset(eps[:, 1:2], EPS_BN)
            link(pool.memset(roll[:, :, :], 0.0))
            link(pool.memset(diag[:, :, :, :], 0.0))

            def set_diagonal(m, c0, c1, k):
                link(pool.affine_select(out=m[:, c0:c1], in_=m[:, c0:c1], compare_op=ALU.not_equal, fill=1.0,
                                        base=-c0 - k, pattern=[[-1, c1 - c0]], channel_multiplier=1))

            for i, s in enumerate(SHIFTS):
                for k in (s, s - H):
                    set_diagonal(roll[:, i, :], 0, H, k)
            for i, (dil, s) in enumerate([(d, s) for d, s, _ in UP] + [(RIGHT[0][0], 0), (LEFT[0][0], 0)]):
                for kh in range(3):
                    e = dil * (kh - 1)
                    for k in {e + s, e + s + H if s else e}:
                        set_diagonal(diag[:, i, kh, :], max(0, -e), min(H, H - e), k)
            pool.sem_inc(const_ready, 1)
            pool.sem_inc(centered, 2)
            pool.sem_inc(sum_ready, 2)
            with pool.Fori(0, GROUPS) as g:
                for i in range(ITS):
                    for q in range(NC):
                        pool.wait_ge(relu_ready[q], ITS * g + i + 2)
                        out = x[:, q, :] if i < ITS - 1 else channel(g, q)
                        pool.tensor_tensor(out, x[:, q, :], rel[:, q, :], ALU.add).then_inc(x_ready[q], 1)

        @block.vector
        def _(dve):
            link = Link(dve, dve_done)
            dve.wait_ge(p_in, 16 * 8)
            taps = par[:, :, 0:SC].rearrange("p c (d i k) -> p d i c k", d=3, i=IT)
            for d in range(3):
                w = raw_w[d].rearrange("p (i c k) -> p i c k", i=IT, c=C)
                for i in range(IT):
                    dve.tensor_copy(taps[:, d, i, :, :], w[:, i, :, :])
            scale_v = par[:, :, SC:BI].rearrange("p c (d i) -> p d i c", d=4)
            bias_v = par[:, :, BI:NP].rearrange("p c (d i) -> p d i c", d=4)
            gam, bet, mean, var = (raw_bn[:, :, :, k, :] for k in range(4))
            dve.wait_ge(bn_std, 1)
            link(dve.reciprocal(var, var))
            link(dve.tensor_tensor(gam, gam, var, ALU.mult))
            link(dve.tensor_tensor(mean, mean, gam, ALU.mult))
            link(dve.tensor_tensor(bet, bet, mean, ALU.subtract))
            link(dve.tensor_scalar(bias_v, bet, 2.0, None, ALU.mult))
            link(dve.tensor_scalar(scale_v, gam, 2.0, None, ALU.mult))
            link(dve.tensor_tensor(scale_v[:, 0, :, :], scale_v[:, 0, :, :], raw_d, ALU.mult))

            def normalise(n, b, t, k):
                xt, s = xs[:, k, :, :], st[:, k, :, :]
                dve.wait_ge(x_in[k], 16 * ((n - k) // 2 + 1))
                link(dve.tensor_reduce(s[:, 0, :], xt, AX.X, ALU.add))
                link(dve.tensor_scalar(s[:, 0, :], s[:, 0, :], 1.0 / C, None, ALU.mult))
                dve.tensor_tensor(h[:, k, :, :], xt, bcast(s[:, 0, :], TS), ALU.subtract).then_inc(centered, 1)
                dve.wait_ge(squared, n + 1)
                dve.tensor_reduce(s[:, 1, :], sq, AX.X, ALU.add).then_inc(var_ready, 1)
                dve.wait_ge(std_ready, n + 1)
                link(dve.reciprocal(s[:, 1, :], s[:, 1, :]))
                dve.tensor_tensor(columns(n, b, t), h[:, k, :, :], bcast(s[:, 1, :], TS), ALU.mult).then_inc(y_ready, 1)

            over_tiles(dve, normalise, link, 3)
            dve.wait_ge(y_ready, B * NT)

            def build(q, i, g):
                conv = i - IT
                d, n = (conv if conv < IT else IT + (conv - IT) // IT), i % 2
                dve.wait_ge(conv_ready[q], ITS * g + i - 1)
                for kw in range(3):
                    m = band[:, q, n, kw, :]
                    w = [cur[:, q, 9 * conv + 3 * kh + kw:9 * conv + 3 * kh + kw + 1] for kh in range(3)]
                    link(dve.tensor_scalar(m, diag[:, d, 0, :], w[0], None, ALU.mult))
                    link(dve.scalar_tensor_tensor(m, diag[:, d, 1, :], w[1], m, ALU.mult, ALU.add))
                    ins = dve.scalar_tensor_tensor(m, diag[:, d, 2, :], w[2], m, ALU.mult, ALU.add)
                ins.then_inc(band_ready[q], 1)

            PER = 6 * NC * 3 * IT
            start = link.base + link.n
            with dve.Fori(0, GROUPS) as g:
                link.base, link.n = start + g * PER, 0
                for q in range(NC):
                    dve.wait_ge(relu_ready[q], ITS * g + 1)
                    dve.tensor_copy(cur[:, q, :], par[:, bass.ds(NC * g + q, 1), :].rearrange(
                        "p a n -> p (a n)")).then_inc(cur_ready, 1)
                dve.wait_ge(cur_ready, NC * g + NC)
                for i in range(IT, ITS):
                    for q in range(NC):
                        build(q, i, g)
                assert link.n == PER
            link.base, link.n = start + GROUPS * PER, 0

            def add_rest(n, b, t, k):
                dve.wait_ge(r_in[k], 16 * ((n - k) // 2 + 1))
                dve.wait_ge(stored[k], 8 * (n - k) + 16)
                dve.tensor_tensor(h[:, k, :, :], columns(n, b, t), xs[:, k, :, :], ALU.add).then_inc(sum_ready, 1)

            over_tiles(dve, add_rest)

        @block.scalar
        def _(act):
            act.wait_ge(const_ready, 1)
            act.wait_ge(p_in, 16 * 8)
            var = raw_bn[:, :, :, 3, :]
            act.activation(var, var, ACT.Sqrt, bias=eps[:, 1:2]).then_inc(bn_std, 1)

            def spread(n, b, t, k):
                act.wait_ge(centered, n + 3)
                act.activation(sq, h[:, k, :, :], ACT.Square).then_inc(squared, 1)
                act.wait_ge(var_ready, n + 1)
                s = st[:, k, 1, :]
                act.activation(s, s, ACT.Sqrt, bias=eps[:, 0:1], scale=1.0 / C).then_inc(std_ready, 1)

            over_tiles(act, spread)
            act.wait_ge(y_ready, B * NT)
            with act.Fori(0, GROUPS) as g:
                for q in range(NC):
                    act.wait_ge(x_ready[q], 17 * g + 1)
                    act.activation(x[:, q, :], channel(g, q), ACT.Copy).then_inc(x_ready[q], 1)
                act.wait_ge(cur_ready, NC * g + NC)
                for i in range(ITS):
                    for q in range(NC):
                        act.wait_ge(conv_ready[q], ITS * g + i + 1)
                        act.activation(rel[:, q, :], pC[q][:, :], ACT.Relu, bias=cur[:, q, BI + i:BI + i + 1],
                                       scale=cur[:, q, SC + i:SC + i + 1]).then_inc(relu_ready[q], 1)

        @block.tensor
        def _(pe):
            pe.wait_ge(const_ready, 1)
            with pe.Fori(0, GROUPS) as g:
                for i in range(ITS):
                    for q in range(NC):
                        pe.wait_ge(x_ready[q], 17 * g + i + 2)
                        if i < IT:
                            pe.matmul(pC[q][:, :], roll[:, i, :], x[:, q, :], start=True,
                                      stop=True).then_inc(conv_ready[q], 1)
                            continue
                        pe.wait_ge(band_ready[q], 3 * IT * g + i - IT + 1)
                        dil, _, s = CONVS[i - IT]
                        xq = x[:, q, :].rearrange("p (b w) -> p b w", b=B)
                        out = pC[q][:, :].rearrange("p (b w) -> p b w", b=B)
                        jobs = [(kw, *piece) for kw in (1, 0, 2) for piece in spans(dil, kw, s)]
                        for n, (kw, lo, hi, at) in enumerate(jobs):
                            ins = pe.matmul(out[:, :, lo:hi], band[:, q, i % 2, kw, :], xq[:, :, at:at + hi - lo],
                                            start=(n == 0), stop=(n == len(jobs) - 1), skip_group_check=True)
                        ins.then_inc(conv_ready[q], 1)


def build_program(nc, p, out):
    PICKS = 4 * 32 * 8
    tok = nc.dram_tensor("tokens", (B * S + PICKS, C), FP32, kind="Internal").ap()
    stage_window_attention(nc, p["x"], p["L0_conv_qkv_w"], p["L0_conv_proj_w"], p["L0_conv_proj_b"],
                           p["L0_conv_bias_table"], tok)
    stage_choice_ffn(nc, "c0", tok, *(p["L0_ffn_" + n] for n in ("gate_w", "gate_b", "weight1", "weight2")))
    stage_conv_bn(nc, tok, *(p["L1_conv_" + n] for n in ("gamma", "beta", "w_lbp", "w_1x1", "b_1x1")))
    stage_top2_ffn(nc, "t1", tok, *(p["L1_ffn_" + n] for n in ("router_w", "router_b", "expert_w", "expert_b")))
    stage_sweeps(nc, tok, [p["L2_conv_kernel_" + n] for n in ("td", "dt", "lr", "rl")])
    stage_choice_ffn(nc, "c2", tok, *(p["L2_ffn_" + n] for n in ("gate_w", "gate_b", "weight1", "weight2")))
    stage_spread(nc, tok, p["L3_conv_w_d"], [p["L3_conv_w_" + n] for n in "url"],
                 [p["L3_conv_bn_" + n] for n in "durl"])
    stage_top2_ffn(nc, "t3", tok, *(p["L3_ffn_" + n] for n in ("router_w", "router_b", "expert_w", "expert_b")),
                   image=out)


def kernel(**inputs):
    import numpy as _np
    import concourse.bacc as _bacc
    from concourse import mybir as _mybir
    from concourse.bass_utils import run_bass_kernel_spmd as _run

    nc = _bacc.Bacc("TRN2", target_bir_lowering=False, num_devices=1)
    arrays, params = {}, {}
    for name, value in inputs.items():
        a = _np.ascontiguousarray(value)
        arrays[f"in_{name}"] = a
        params[name] = nc.dram_tensor(f"in_{name}", a.shape, _mybir.dt.from_np(a.dtype), kind="ExternalInput").ap()
    out = nc.dram_tensor("out", (B, C, H, W), _mybir.dt.float32, kind="ExternalOutput").ap()
    build_program(nc, params, out)
    r = _run(nc, [arrays], core_ids=[0])
    return r.results[0]["out"]
```

```python
import numpy as np
import concourse.bass as bass
from concourse import mybir
from contextlib import ExitStack

FP32 = mybir.dt.float32
ALU = mybir.AluOpType
ACT = mybir.ActivationFunctionType
AX = mybir.AxisListType
B, C, H, W = 4, 64, 128, 128
S = H * W


class Link:

    def __init__(self, eng, sem):
        self.eng, self.sem, self.base, self.n = eng, sem, 0, 0

    def __call__(self, ins):
        ins.then_inc(self.sem, 1)
        self.n += 1
        self.eng.wait_ge(self.sem, self.base + self.n)

    def enter(self, i, per_iteration):
        self.start, self.per = self.base + self.n, per_iteration
        self.base, self.n = self.start + i * per_iteration, 0

    def leave(self, iterations):
        assert self.n == self.per, (self.n, self.per)
        self.base, self.n = self.start + iterations * self.per, 0


class Arena:

    def __init__(self, nc, ctx, stage):
        self.nc, self.ctx, self.stage, self.sems = nc, ctx, stage, []
        ctx.callback(self.clear)

    def clear(self):
        self.nc.clear_and_free_semaphores(self.sems)
        self.nc.all_engine_barrier()

    def sb(self, name, shape, dt=FP32):
        return self.ctx.enter_context(self.nc.sbuf_tensor(f"{self.stage}_{name}", shape, dt))

    def ps(self, name, shape, dt=FP32):
        return self.ctx.enter_context(self.nc.psum_tensor(f"{self.stage}_{name}", shape, dt))

    def sem(self, name):
        self.sems.append(self.nc.alloc_semaphore(name=f"{self.stage}_{name}"))
        return self.sems[-1]


def eye(pool, link, m):
    link(pool.memset(m, 0.0))
    link(pool.affine_select(out=m, in_=m, compare_op=ALU.not_equal, fill=1.0, base=0,
                            pattern=[[-1, 128]], channel_multiplier=1))


def bcast(v, n, m=C):
    return v.unsqueeze(2).to_broadcast([128, n, m])


def parity_blocks(taps, first):
    for m in range(-2, 3):
        for pi in range(2):
            for po in range(2):
                tap = 2 * m + pi - po + first
                if 0 <= tap < taps:
                    yield m, pi, po, tap


def stage_window_attention(nc, x, qkv_w, proj_w, proj_b, bias_table, tok):
    WS, NH, SHIFT = 8, 4, 4
    STEP = 4
    NSTEP = W // WS // STEP
    T = STEP * WS * WS
    STRIPS = H // WS
    NX = 4
    SCALE = float(C // NH) ** -0.5
    EPS = 1e-6
    with ExitStack() as ctx:
        a = Arena(nc, ctx, "wa")
        ident = a.sb("ident", [128, 128])
        mean_w = a.sb("mean_w", [128, 128])
        w_rows = a.sb("w_rows", [128, 4, 128])
        w_cols = a.sb("w_cols", [128, 4, 128])
        pb = a.sb("pb", [128, 1])
        eps = a.sb("eps", [128, 1])
        iota_q = a.sb("iota_q", [128, 1], mybir.dt.int32)
        iota_k = a.sb("iota_k", [128, 64], mybir.dt.int32)
        bits_q = a.sb("bits_q", [128, 4], mybir.dt.int32)
        bits_k = a.sb("bits_k", [128, 2, 64], mybir.dt.int32)
        bits_qf = a.sb("bits_qf", [128, 4])
        bits_kf = a.sb("bits_kf", [128, 2, 64])
        gmask = a.sb("gmask", [128, 2])
        hmask = a.sb("hmask", [128, NH])
        half_mask = a.sb("half_mask", [128, 2, 16])
        table = a.sb("table", [128, 64, NH])
        bias = a.sb("bias", [128, 2, 2, NH, 64])
        cut = a.sb("cut", [128, 3, 64])
        xs = a.sb("xs", [128, NX, 8, 128])
        xc = a.sb("xc", [128, 8, 128])
        sq = a.sb("sq", [128, 8, 128])
        h = a.sb("h", [128, 2, W // WS, 2, WS, WS])
        qs = a.sb("qs", [128, STEP, 2, 64])
        ks = a.sb("ks", [128, NH, T])
        vs = a.sb("vs", [128, NSTEP, STEP, 128])
        sc = a.sb("sc", [128, 2, STEP, NH, 64])
        mx = a.sb("mx", [128, STEP, NH])
        sm = a.sb("sm", [128, 2, 2, STEP, NH])
        pt = a.sb("pt", [128, STEP, 2, 128])
        ov = a.sb("ov", [128, T])
        yr = a.sb("yr", [128, 2, WS, W])
        x1 = a.sb("x1", [128, WS, W])
        xt = a.sb("xt", [128, 2, WS, 128])
        pL = a.ps("pL", [128, 512])
        pQK = a.ps("pQK", [128, 2, T])
        pV = a.ps("pV", [128, STEP, 128])
        pS = a.ps("pS", [128, STEP, NH, 64])
        pT = a.ps("pT", [128, STEP, 2, 128])
        pO = a.ps("pO", [128, 2, T])
        const_in = a.sem("const_in")
        pool_done = a.sem("pool_done")
        dve_done = a.sem("dve_done")
        const_ready = a.sem("const_ready")
        zeros_ready = a.sem("zeros_ready")
        w_turned = a.sem("w_turned")
        w_ready = a.sem("w_ready")
        x_in = [a.sem(f"x_in{i}") for i in range(NX)]
        mean_ready = a.sem("mean_ready")
        centered = a.sem("centered")
        squared = a.sem("squared")
        var_ready = a.sem("var_ready")
        log_ready = a.sem("log_ready")
        rstd_ready = a.sem("rstd_ready")
        h_ready = a.sem("h_ready")
        h_doubled = a.sem("h_doubled")
        qkv_ready = a.sem("qkv_ready")
        qk_saved = a.sem("qk_saved")
        v_saved = a.sem("v_saved")
        scores_ready = a.sem("scores_ready")
        bias_ready = a.sem("bias_ready")
        scores_read = a.sem("scores_read")
        max_ready = a.sem("max_ready")
        shifted = a.sem("shifted")
        exp_ready = a.sem("exp_ready")
        row_sums = a.sem("row_sums")
        sum_ready = a.sem("sum_ready")
        probs_ready = a.sem("probs_ready")
        probs_turned = a.sem("probs_turned")
        pt_saved = a.sem("pt_saved")
        pv_ready = a.sem("pv_ready")
        ov_saved = a.sem("ov_saved")
        proj_ready = a.sem("proj_ready")
        yr_ready = a.sem("yr_ready")
        x1_ready = a.sem("x1_ready")
        x1_turned = a.sem("x1_turned")
        xt_saved = a.sem("xt_saved")
        stored = [a.sem(f"stored{i}") for i in range(2)]
        block = ctx.enter_context(nc.Block())

        N_CONST = 8 + 2 + 16

        def over_strips(eng, begin, strip, end):
            with eng.Fori(0, 2) as bp:
                n0 = bp * STRIPS
                begin(bp, n0)
                strip(bp, 0, n0, 0, True, False)
                with eng.Fori(0, STRIPS // NX - 1) as t:
                    for k in range(1, NX + 1):
                        strip(bp, NX * t + k, bp * STRIPS + NX * t + k, k % NX, False, False)
                for i in range(STRIPS - NX + 1, STRIPS):
                    strip(bp, i, bp * STRIPS + i, i % NX, False, i == STRIPS - 1)
                end(bp, bp * STRIPS + STRIPS)

        def normalised(eng, par, copy):
            for w0, w1, c0, c1, col in ((0, 15, 0, WS, SHIFT), (15, 16, 0, 4, W - 4), (15, 16, 4, 8, 0)):
                def part(t):
                    return t[:, :, col:col + (w1 - w0) * (c1 - c0)].rearrange("p r (w c) -> p w r c", c=c1 - c0)
                ins = eng.tensor_tensor(h[:, par, w0:w1, copy, :, c0:c1], part(xc), part(sq), ALU.mult)
            return ins

        def steps(n, k, first, last, body):
            for j in range(NSTEP):
                s = NSTEP * n + j
                def at(d):
                    up = (j + d) // NSTEP
                    return s + d, (j + d) % NSTEP, n + up, (k + up) % 2
                body(s, j, None if last and j == NSTEP - 1 else at(1),
                     None if first and j < 1 else at(-1), None if first and j < 2 else at(-2))

        @block.sync
        def _(sp):
            sp.wait_ge(zeros_ready, 1)
            for g in range(2):
                part = slice(64 * g, 64 * g + 64)
                for m in range(4):
                    w = proj_w if m == 3 else qkv_w[64 * m:64 * m + 64, :]
                    sp.dma_start(w_rows[part, m, part], w).then_inc(const_in, 16)
                sp.dma_start(pb[part, :], proj_b.rearrange("(c a) -> c a", a=1)).then_inc(const_in, 16)
                for qr in range(WS):
                    src = bass.AP(bias_table.tensor, qr * 15 * NH, [[NH, 8], [15 * NH, 8], [1, 8 * NH]])
                    sp.dma_start(table[64 * g + 8 * qr:64 * g + 8 * qr + 8, :, :].rearrange(
                        "p (i j) h -> p i (j h)", i=8), src).then_inc(const_in, 16)

            def halves(i):
                return [(WS * i + SHIFT + 4 * half) % H if isinstance(i, int) else WS * i + SHIFT + 4 * half
                        for half in range(2)]

            def load(bp, i, n, k):
                sp.wait_ge(x1_ready, n + 1)
                for half, r in enumerate(halves(i)):
                    src = x[bass.ds(2 * bp, 2), :, bass.ds(r, 4), :].rearrange("g c h w -> (g c) h w")
                    sp.dma_start(xs[:, k, 4 * half:4 * half + 4, :], src).then_inc(x_in[k], 16)

            def store(bp, i, n, par):
                sp.wait_ge(xt_saved, 2 * n + 4)
                for half, r in enumerate(halves(i)):
                    for g in range(2):
                        rows = tok[bass.ds((2 * bp + g) * S + r * W, 4 * W), :]
                        sp.dma_start(rows.rearrange("(r w) c -> w r c", r=4),
                                     xt[:, par, 4 * half:4 * half + 4, 64 * g:64 * g + 64]).then_inc(stored[par], 16)

            with sp.Fori(0, 2) as bp:
                for i in range(NX):
                    load(bp, i, bp * STRIPS + i, i)
                with sp.Fori(1, STRIPS // NX - 1) as t:
                    for k in range(NX):
                        load(bp, NX * t + k, bp * STRIPS + NX * t + k, k)
                        store(bp, NX * t + (k - NX), bp * STRIPS + NX * t + (k - NX), k % 2)
                for i in range(STRIPS - NX, STRIPS):
                    load(bp, i, bp * STRIPS + i, i % NX)
                    store(bp, i - NX, bp * STRIPS + (i - NX), i % 2)
                for i in range(STRIPS - NX, STRIPS):
                    store(bp, i, bp * STRIPS + i, i % 2)
            for par in range(2):
                sp.wait_ge(stored[par], 64 * STRIPS + 16)

        @block.gpsimd
        def _(pool):
            link = Link(pool, pool_done)
            for s, k in ((x1_turned, 1), (yr_ready, 1), (qkv_ready, 1), (scores_ready, 1), (v_saved, 1), (pt_saved, 1),
                         (proj_ready, 1), (scores_read, 1), (h_doubled, 1), (probs_turned, 2), (xt_saved, 2),
                         (pv_ready, NSTEP), (x1_ready, NX), (stored[0], 16), (stored[1], 16)):
                pool.sem_inc(s, k)
            pool.memset(w_rows[:, :, :], 0.0).then_inc(zeros_ready, 1)
            pool.memset(eps[:, :], EPS)
            link(pool.memset(mean_w[:, :], 0.0))
            for g in range(2):
                link(pool.memset(mean_w[64 * g:64 * g + 64, 64 * g:64 * g + 64], 1.0 / C))
            eye(pool, link, ident[:, :])
            link(pool.iota(iota_q[:, :], pattern=[[0, 1]], base=0, channel_multiplier=1))
            pool.iota(iota_k[:, :], pattern=[[1, 64]], base=0, channel_multiplier=0).then_inc(const_ready, 1)

            def normalise(u, j):
                pool.wait_ge(sum_ready, u + 1)
                p = sc[:, j % 2, :, :, :]
                r = sm[:, j % 2, 1, :, :].unsqueeze(3).to_broadcast([128, STEP, NH, 64])
                pool.tensor_tensor(p, p, r, ALU.mult).then_inc(probs_ready, 1)

            def write_h(m, par, done):
                pool.wait_ge(rstd_ready, m + 1)
                pool.wait_ge(qkv_ready, done + 1)
                normalised(pool, par, 1).then_inc(h_doubled, 1)

            def residual(q, k):
                pool.wait_ge(yr_ready, NSTEP * q + NSTEP + 1)
                pool.wait_ge(x1_turned, 2 * q + 1)
                o, p = x1[:, :, :], yr[:, k % 2, :, :]
                pool.tensor_tensor(o[:, :, SHIFT:W], xs[:, k, :, SHIFT:W], p[:, :, 0:W - SHIFT], ALU.add)
                pool.tensor_tensor(o[:, :, 0:SHIFT], xs[:, k, :, 0:SHIFT], p[:, :, W - SHIFT:W],
                                   ALU.add).then_inc(x1_ready, 1)

            def begin(bp, n):
                write_h(n, 0, NSTEP * n)

            def strip(bp, i, n, k, first, last):
                def body(s, j, after, back1, back2):
                    if back1:
                        normalise(*back1[0:2])
                    if j == 2 and not last:
                        write_h(n + 1, (k + 1) % 2, NSTEP * n)
                    if j == 2 and not first:
                        residual(n - 1, (k - 1) % NX)
                steps(n, k, first, last, body)

            def end(bp, n):
                normalise(NSTEP * n - 1, NSTEP - 1)
                residual(n - 1, NX - 1)

            over_strips(pool, begin, strip, end)

        @block.vector
        def _(dve):
            link = Link(dve, dve_done)
            SHR, AND = ALU.logical_shift_right, ALU.bitwise_and
            dve.wait_ge(const_ready, 1)
            for k, (bit, m) in enumerate([(5, 1), (2, 1), (4, 3), (6, 1)]):
                link(dve.tensor_scalar(bits_q[:, k:k + 1], iota_q[:, :], bit, m, SHR, AND))
                if k < 2:
                    link(dve.tensor_scalar(bits_k[:, k, :], iota_k[:, :], bit, m, SHR, AND))
            link(dve.tensor_copy(bits_qf[:, :], bits_q[:, :]))
            link(dve.tensor_copy(bits_kf[:, :, :], bits_k[:, :, :]))
            for g in range(2):
                link(dve.tensor_scalar(gmask[:, g:g + 1], bits_qf[:, 3:4], float(g), SCALE, ALU.is_equal, ALU.mult))
                link(dve.memset(half_mask[:, g, :], 0.0))
                link(dve.tensor_scalar(half_mask[:, g, :], half_mask[:, g, :], bits_qf[:, 3:4], float(g),
                                       ALU.add, ALU.is_equal))
            for k in range(NH):
                link(dve.tensor_scalar(hmask[:, k:k + 1], bits_qf[:, 2:3], float(k), None, ALU.is_equal))
            for k in range(2):
                link(dve.tensor_scalar(cut[:, k, :], bits_kf[:, k, :], bits_qf[:, k:k + 1], -100.0,
                                       ALU.not_equal, ALU.mult))
            link(dve.tensor_tensor(cut[:, 2, :], cut[:, 0, :], cut[:, 1, :], ALU.min))
            dve.wait_ge(const_in, 16 * N_CONST)
            link(dve.tensor_copy(bias[:, 0, 0, :, :], table[:, ::-1, :].rearrange("p k h -> p h k")))
            for row, col, which in ((0, 1, 1), (1, 0, 0), (1, 1, 2)):
                link(dve.tensor_tensor(bias[:, row, col, :, :], bias[:, 0, 0, :, :],
                                       cut[:, which, :].unsqueeze(1).to_broadcast([128, NH, 64]), ALU.add))
            dve.sem_inc(bias_ready, 1)

            dve.wait_ge(bias_ready, 1)

            def save_v(s, j):
                dve.wait_ge(qkv_ready, s + 2)
                dve.wait_ge(pv_ready, s + 1)
                m = half_mask[:, :, :].rearrange("p a d -> p (a d)").unsqueeze(1).to_broadcast([128, STEP * 4, 32])
                dve.tensor_tensor(vs[:, j, :, :].rearrange("p w (a d) -> p (w a) d", d=32),
                                  pV[:, :, :].rearrange("p w (a d) -> p (w a) d", d=32), m,
                                  ALU.mult).then_inc(v_saved, 1)

            def softmax_shift(s, j, last):
                dve.wait_ge(scores_ready, s + 2)
                dve.wait_ge(probs_turned, s + 1)
                e, f = sc[:, j % 2, :, :, :], pS[:, :, :, :]
                n = STEP - 1 if j == NSTEP - 1 else STEP
                if n < STEP:
                    dve.tensor_tensor(e[:, n, :, :], f[:, n, :, :], bias[:, int(last), 1, :, :], ALU.add)
                r = bias[:, int(last), 0, :, :].rearrange("p h k -> p (h k)").unsqueeze(1).to_broadcast([128, n, NH * 64])
                dve.tensor_tensor(e[:, 0:n, :, :].rearrange("p w h k -> p w (h k)"),
                                  f[:, 0:n, :, :].rearrange("p w h k -> p w (h k)"), r,
                                  ALU.add).then_inc(scores_read, 1)
                dve.wait_ge(scores_read, s + 2)
                dve.tensor_reduce(mx[:, :, :], e, AX.X, ALU.max).then_inc(max_ready, 1)
                dve.wait_ge(max_ready, s + 1)
                dve.tensor_tensor(e, e, mx[:, :, :].unsqueeze(3).to_broadcast([128, STEP, NH, 64]),
                                  ALU.subtract).then_inc(shifted, 1)

            def softmax_sum(u, j):
                dve.wait_ge(exp_ready, u + 1)
                dve.tensor_reduce(sm[:, j % 2, 0, :, :], sc[:, j % 2, :, :, :], AX.X, ALU.add).then_inc(row_sums, 1)
                dve.wait_ge(row_sums, u + 1)
                dve.reciprocal(sm[:, j % 2, 1, :, :], sm[:, j % 2, 0, :, :]).then_inc(sum_ready, 1)

            def center(m, half, k):
                rows = slice(4 * half, 4 * half + 4)
                dve.wait_ge(mean_ready, 2 * m + half + 1)
                dve.wait_ge(h_doubled, m + 1)
                dve.tensor_tensor(xc[:, rows, :], xs[:, k, rows, :],
                                  pL[:, :].rearrange("p (r c) -> p r c", c=W), ALU.subtract).then_inc(centered, 1)

            def write_h(m, par, done):
                dve.wait_ge(rstd_ready, m + 1)
                dve.wait_ge(qkv_ready, done + 1)
                normalised(dve, par, 0).then_inc(h_ready, 1)

            def begin(bp, n):
                for half in range(2):
                    center(n, half, 0)
                write_h(n, 0, NSTEP * n)
                save_v(NSTEP * n, 0)

            def strip(bp, i, n, k, first, last):
                def body(s, j, after, back1, back2):
                    if back1:
                        softmax_sum(*back1[0:2])
                    if j == 1 and not last:
                        center(n + 1, 1, (k + 1) % NX)
                    softmax_shift(s, j, last)
                    if j == 2 and not last:
                        write_h(n + 1, (k + 1) % 2, NSTEP * n)
                    if after:
                        save_v(*after[0:2])
                    if j == 0 and not last:
                        center(n + 1, 0, (k + 1) % NX)
                steps(n, k, first, last, body)

            def end(bp, n):
                softmax_sum(NSTEP * n - 1, NSTEP - 1)

            over_strips(dve, begin, strip, end)

        @block.scalar
        def _(act):
            act.wait_ge(w_turned, 1)
            act.activation(w_cols[:, :, :].rearrange("p m c -> p (m c)"), pL[:, :], ACT.Copy).then_inc(w_ready, 1)

            def save_qk(s, j):
                act.wait_ge(qkv_ready, s + 2)
                act.wait_ge(scores_ready, s + 1)
                for g in range(2):
                    act.activation(qs[:, :, g, :], pQK[:, 0, :].rearrange("p (w q) -> p w q", q=64), ACT.Copy,
                                   scale=gmask[:, g:g + 1])
                for k in range(NH):
                    ins = act.activation(ks[:, k, :], pQK[:, 1, :], ACT.Copy, scale=hmask[:, k:k + 1])
                ins.then_inc(qk_saved, 1)

            def exponential(s, j):
                act.wait_ge(shifted, s + 1)
                e = sc[:, j % 2, :, :, :]
                act.activation(e, e, ACT.Exp).then_inc(exp_ready, 1)

            def save_probs(u):
                act.wait_ge(probs_turned, u + 3)
                act.wait_ge(pv_ready, u + NSTEP)
                act.activation(pt[:, :, :, :], pT[:, :, :, :], ACT.Copy).then_inc(pt_saved, 1)

            def save_values(u):
                act.wait_ge(pv_ready, u + NSTEP + 1)
                act.wait_ge(proj_ready, u + 1)
                act.activation(ov[:, :], pO[:, 0, :], ACT.Copy).then_inc(ov_saved, 1)

            def save_proj(u, j, n, par):
                act.wait_ge(proj_ready, u + 2)
                if j == 0:
                    act.wait_ge(x1_ready, n + NX - 1)
                cols = yr[:, par, :, 4 * 8 * j:4 * 8 * j + 32].rearrange("p r (w c) -> p w r c", c=WS)
                act.activation(cols, pO[:, 1, :].rearrange("p (w r c) -> p w r c", w=STEP, r=WS), ACT.Identity,
                               bias=pb[:, 0:1]).then_inc(yr_ready, 1)

            def square(m, half):
                rows = slice(4 * half, 4 * half + 4)
                act.wait_ge(centered, 2 * m + half + 1)
                act.activation(sq[:, rows, :], xc[:, rows, :], ACT.Square).then_inc(squared, 1)

            def log(m, half):
                rows = slice(4 * half, 4 * half + 4)
                act.wait_ge(var_ready, 2 * m + half + 1)
                act.activation(sq[:, rows, :].rearrange("p r c -> p (r c)"), pL[:, :], ACT.Ln,
                               bias=eps[:, 0:1]).then_inc(log_ready, 1)

            def root(m):
                act.wait_ge(log_ready, 2 * m + 2)
                act.activation(sq[:, :, :], sq[:, :, :], ACT.Exp, scale=-0.5).then_inc(rstd_ready, 1)

            def save_turned(q, par, half):
                act.wait_ge(x1_turned, 2 * q + half + 2)
                act.wait_ge(stored[par], 32 * (q - par) + 16)
                act.activation(xt[:, par, 4 * half:4 * half + 4, :].rearrange("p r c -> p (r c)"), pL[:, :],
                               ACT.Copy).then_inc(xt_saved, 1)

            def begin(bp, n):
                for half in range(2):
                    square(n, half)
                for half in range(2):
                    log(n, half)
                root(n)
                save_qk(NSTEP * n, 0)

            def strip(bp, i, n, k, first, last):
                def body(s, j, after, back1, back2):
                    if j == 2 and not last:
                        log(n + 1, 1)
                        root(n + 1)
                    if j == 3 and not first:
                        save_turned(n - 1, (k - 1) % 2, 0)
                    if after:
                        save_qk(*after[0:2])
                    if back2:
                        save_values(back2[0])
                    if j == 1 and not last:
                        square(n + 1, 1)
                    exponential(s, j)
                    if back1:
                        save_probs(back1[0])
                    if back2:
                        save_proj(*back2)
                    if j == 0 and not last:
                        square(n + 1, 0)
                    if j == 1 and not last:
                        log(n + 1, 0)
                    if j == 3 and not first:
                        save_turned(n - 1, (k - 1) % 2, 1)
                steps(n, k, first, last, body)

            def end(bp, n):
                s = NSTEP * n
                save_values(s - 2)
                save_probs(s - 1)
                save_proj(s - 2, NSTEP - 2, n - 1, 1)
                save_values(s - 1)
                save_proj(s - 1, NSTEP - 1, n - 1, 1)
                for half in range(2):
                    save_turned(n - 1, 1, half)

            over_strips(act, begin, strip, end)

        @block.tensor
        def _(pe):
            pe.wait_ge(const_ready, 1)
            pe.wait_ge(const_in, 16 * N_CONST)
            for m in range(4):
                ins = pe.transpose(pL[:, 128 * m:128 * m + 128], w_rows[:, m, :], ident[:, :])
            ins.then_inc(w_turned, 1)
            pe.wait_ge(w_ready, 1)

            def qkv(s, j, par, n=None):
                ht = h[:, par, STEP * j:STEP * j + STEP, :, :, :].rearrange("p w t r c -> p w t (r c)")
                if j == 0:
                    pe.wait_ge(h_ready, n + 1)
                    pe.wait_ge(h_doubled, n + 2)
                for m in range(2):
                    pe.matmul(pQK[:, m, :], w_cols[:, m, :], ht[:, :, 0, :], start=True, stop=True)
                pe.wait_ge(v_saved, s + 1)
                for w in range(STEP):
                    keys = ht[:, w, :, :].rearrange("p t q -> p (t q)")
                    ins = pe.matmul(pV[:, w, :], keys, w_cols[:, 2, :], start=True, stop=True)
                ins.then_inc(qkv_ready, 1)

            def scores(s):
                pe.wait_ge(qk_saved, s + 1)
                pe.wait_ge(scores_read, s + 1)
                for w in range(STEP):
                    ins = pe.matmul(pS[:, w, :, :], qs[:, w, :, :].rearrange("p g q -> p (g q)"), ks[:, :, 64 * w:64 * w + 64],
                                    start=True, stop=True)
                ins.then_inc(scores_ready, 1)

            def turn_probs(u, j):
                pe.wait_ge(probs_ready, u + 1)
                pe.wait_ge(pt_saved, u + 1)
                for w in range(STEP):
                    for hp in range(2):
                        ins = pe.transpose(pT[:, w, hp, :], sc[:, j % 2, w, 2 * hp:2 * hp + 2, :], ident[:, :])
                ins.then_inc(probs_turned, 1)

            def values(u, j):
                pe.wait_ge(pt_saved, u + 2)
                pe.wait_ge(yr_ready, u + 1)
                for w in range(STEP):
                    for g in range(2):
                        for hp in range(2):
                            o = 64 * g + 32 * hp
                            ins = pe.matmul(pO[o:o + 32, 0, 64 * w:64 * w + 64], vs[:, j, w, o:o + 32],
                                            pt[:, w, hp, 64 * g:64 * g + 64], start=True, stop=True)
                ins.then_inc(pv_ready, 1)

            def project(u):
                pe.wait_ge(ov_saved, u + 1)
                pe.matmul(pO[:, 1, :], w_cols[:, 3, :], ov[:, :], start=True, stop=True).then_inc(proj_ready, 1)

            def mean(m, half, k):
                pe.wait_ge(x_in[k], 8 * (m - k) + 32)
                if half == 1:
                    pe.wait_ge(centered, 2 * m + 1)
                pe.matmul(pL[:, :], mean_w[:, :], xs[:, k, 4 * half:4 * half + 4, :], start=True,
                          stop=True).then_inc(mean_ready, 1)

            def variance(m, half):
                pe.wait_ge(squared, 2 * m + half + 1)
                if half == 0:
                    pe.wait_ge(centered, 2 * m + 2)
                else:
                    pe.wait_ge(log_ready, 2 * m + 1)
                pe.matmul(pL[:, :], mean_w[:, :], sq[:, 4 * half:4 * half + 4, :], start=True,
                          stop=True).then_inc(var_ready, 1)

            def turn_out(q, half):
                pe.wait_ge(x1_ready, q + NX + 1)
                pe.wait_ge(xt_saved, 2 * q + half + 2)
                for r in range(4):
                    ins = pe.transpose(pL[:, 128 * r:128 * r + 128], x1[:, 4 * half + r, :], ident[:, :])
                ins.then_inc(x1_turned, 1)

            def begin(bp, n):
                pe.wait_ge(xt_saved, 2 * n + 2)
                for half in range(2):
                    mean(n, half, 0)
                for half in range(2):
                    variance(n, half)
                qkv(NSTEP * n, 0, 0, n)

            def strip(bp, i, n, k, first, last):
                def body(s, j, after, back1, back2):
                    scores(s)
                    if after:
                        qkv(after[0], after[1], after[3], after[2])
                    if j == 0 and not last:
                        if not first:
                            pe.wait_ge(xt_saved, 2 * n)
                        mean(n + 1, 0, (k + 1) % NX)
                    if j == 1 and not last:
                        variance(n + 1, 0)
                    if j == 3 and not first:
                        turn_out(n - 1, 1)
                    if back2:
                        values(*back2[0:2])
                    if back1:
                        turn_probs(*back1[0:2])
                    if back2:
                        project(back2[0])
                    if j == 0 and not last:
                        mean(n + 1, 1, (k + 1) % NX)
                    if j == 1 and not last:
                        variance(n + 1, 1)
                    if j == 2 and not first:
                        if not last:
                            pe.wait_ge(log_ready, 2 * n + 4)
                        turn_out(n - 1, 0)
                steps(n, k, first, last, body)

            def end(bp, n):
                s = NSTEP * n
                values(s - 2, NSTEP - 2)
                turn_probs(s - 1, NSTEP - 1)
                project(s - 2)
                values(s - 1, NSTEP - 1)
                project(s - 1)
                for half in range(2):
                    turn_out(n - 1, half)

            over_strips(pe, begin, strip, end)


def stage_choice_ffn(nc, stage, tok, gate_w, gate_b, weight1, weight2):
    E, K, HID = 32, 8, 256
    TS = 8
    TILE = 128 * TS
    NT = S // TILE
    EPS = 1e-5
    with ExitStack() as ctx:
        a = Arena(nc, ctx, stage)
        U32, I32 = mybir.dt.uint32, mybir.dt.int32
        ident = a.sb("ident", [128, 128])
        ones = a.sb("ones", [128, 128])
        tri = a.sb("tri", [128, 128])
        eps = a.sb("eps", [128, 1])
        gate_rows = a.sb("gate_rows", [E, 2, 128])
        gate_cols = a.sb("gate_cols", [128, 2, E])
        gb = a.sb("gb", [128, 1])
        w1 = a.sb("w1", [C + 1, E, HID])
        w2 = a.sb("w2", [128, 2, E, C])
        w2b = a.sb("w2b", [1, E, C])
        logits = a.sb("logits", [128, S])
        xs = a.sb("xs", [128, 2, TS, C])
        h = a.sb("h", [128, 2, TS, C])
        sq = a.sb("sq", [128, TS, C])
        st = a.sb("st", [128, 2, 2, TS])
        ht = a.sb("ht", [128, 2, 512])
        top = a.sb("top", [128, K])
        neg_max = a.sb("neg_max", [128, 1])
        at = a.sb("at", [128, K], U32)
        first = a.sb("first", [128, 1], I32)
        firstf = a.sb("firstf", [128, 1])
        idf = a.sb("idf", [128, K])
        rows_at = a.sb("rows_at", [128, K], U32)
        ex = a.sb("ex", [128, K])
        zsum = a.sb("zsum", [128, 2])
        val = a.sb("val", [128, K])
        rows = a.sb("rows", [128, K, C])
        rn = a.sb("rn", [128, K, C])
        rq = a.sb("rq", [128, K, C])
        rs = a.sb("rs", [128, 2, K])
        pooled = a.sb("pooled", [128, C + 1])
        pooled_t = a.sb("pooled_t", [C + 1, 128])
        hid = a.sb("hid", [128, 2, E, B])
        out_t = a.sb("out_t", [C, 128])
        wt = a.sb("wt", [128, K, C])
        dia = a.sb("dia", [128, K, 128])
        idr = a.sb("idr", [128, K, 128])
        same = a.sb("same", [128, 2, K, 128])
        same_before = a.sb("same_before", [128, 2, 128])
        trash = a.sb("trash", [128, K], I32)
        trashf = a.sb("trashf", [128, K])
        dup = a.sb("dup", [128, K])
        pH = [a.ps(f"pH{i}", [128, 512]) for i in range(2)]
        pG = [a.ps(f"pG{i}", [128, 512]) for i in range(2)]
        pA = a.ps("pA", [128, 512])
        pB = a.ps("pB", [128, 512])
        pC = a.ps("pC", [128, 512])
        pD = a.ps("pD", [128, 512])
        pool_done = a.sem("pool_done")
        dve_done = a.sem("dve_done")
        act_done = a.sem("act_done")
        zeros_ready = a.sem("zeros_ready")
        const_ready = a.sem("const_ready")
        gate_in = a.sem("gate_in")
        w_in = a.sem("w_in")
        gate_turned = a.sem("gate_turned")
        gate_ready = a.sem("gate_ready")
        x_in = [a.sem(f"x_in{i}") for i in range(2)]
        centered = a.sem("centered")
        squared = a.sem("squared")
        var_ready = a.sem("var_ready")
        std_ready = a.sem("std_ready")
        h_ready = a.sem("h_ready")
        h_turned = a.sem("h_turned")
        ht_saved = a.sem("ht_saved")
        gates_ready = a.sem("gates_ready")
        logits_saved = a.sem("logits_saved")
        top_ready = a.sem("top_ready")
        found = a.sem("found")
        exp_ready = a.sem("exp_ready")
        at_ready = a.sem("at_ready")
        rows_in = a.sem("rows_in")
        row_step = a.sem("row_step")
        row_act = a.sem("row_act")
        pooled_ready = a.sem("pooled_ready")
        pooled_turned = a.sem("pooled_turned")
        pooled_saved = a.sem("pooled_saved")
        hid_ready = a.sem("hid_ready")
        gelu_ready = a.sem("gelu_ready")
        out_ready = a.sem("out_ready")
        out_saved = a.sem("out_saved")
        out_turned = a.sem("out_turned")
        wt_ready = a.sem("wt_ready")
        dia_ready = a.sem("dia_ready")
        idr_ready = a.sem("idr_ready")
        same_ready = a.sem("same_ready")
        summed = a.sem("summed")
        new_rows = a.sem("new_rows")
        scattered = a.sem("scattered")
        block = ctx.enter_context(nc.Block())
        NGATE, NW = 6, 3

        @block.sync
        def _(sp):
            sp.wait_ge(zeros_ready, 1)
            for p in range(2):
                sp.dma_start(gate_rows[:, p, 64 * p:64 * p + 64], gate_w).then_inc(gate_in, 16)
            for b in range(B):
                sp.dma_start(gb[E * b:E * b + E, :], gate_b.rearrange("(e a) -> e a", a=1)).then_inc(gate_in, 16)
            with sp.Fori(0, NT) as t:
                for b in range(B):
                    sp.wait_ge(h_ready, B * t + b + 1)
                    sp.dma_start(xs[:, b % 2, :, :], tok[bass.ds(b * S + t * TILE, TILE), :].rearrange(
                        "(p j) c -> p j c", j=TS)).then_inc(x_in[b % 2], 16)
            sp.dma_start(w1[:, :, :], weight1.rearrange("e d h -> d e h")).then_inc(w_in, 16)
            for m in range(2):
                sp.dma_start(w2[:, m, :, :], weight2[:, 128 * m:128 * m + 128, :].rearrange(
                    "e h o -> h e o")).then_inc(w_in, 16)
            sp.dma_start(w2b[:, :, :], weight2[:, HID:HID + 1, :].rearrange("e a o -> a e o")).then_inc(w_in, 16)

        @block.gpsimd
        def _(pool):
            link = Link(pool, pool_done)
            for s in (var_ready, gates_ready, ht_saved, logits_saved):
                pool.sem_inc(s, 1)
            pool.memset(gate_rows[:, :, :], 0.0).then_inc(zeros_ready, 1)
            pool.memset(ones[:, :], 1.0)
            pool.memset(eps[:, :], EPS)
            pool.memset(pooled[:, C:C + 1], 1.0)
            link(pool.memset(tri[:, :], 1.0))
            link(pool.affine_select(out=tri[:, :], in_=tri[:, :], compare_op=ALU.is_gt, fill=0.0, base=0,
                                    pattern=[[1, 128]], channel_multiplier=-1))
            eye(pool, link, ident[:, :])
            link(pool.iota(trash[:, :], pattern=[[1, K]], base=B * S, channel_multiplier=K))
            pool.iota(first[:, :], pattern=[[0, 1]], base=0, channel_multiplier=1).then_inc(const_ready, 1)
            pool.sem_inc(h_ready, 2)
            pool.wait_ge(at_ready, 1)
            for k in range(K):
                pool.indirect_dma_start(rows[:, k, :], None, tok[0:B * S, :],
                                        bass.IndirectOffsetOnAxis(ap=rows_at[:, k:k + 1], axis=0)).then_inc(rows_in, 16)
            pool.wait_ge(new_rows, 1)
            for k in range(K):
                pool.indirect_dma_start(tok[:, :], bass.IndirectOffsetOnAxis(ap=rows_at[:, k:k + 1], axis=0),
                                        rows[:, k, :], None).then_inc(scattered, 16)
            pool.wait_ge(scattered, 16 * K)

        def bcast(v, n):
            return v.unsqueeze(2).to_broadcast([128, n, C])

        @block.vector
        def _(dve):
            link = Link(dve, dve_done)
            dve.wait_ge(const_ready, 1)
            link(dve.tensor_scalar(first[:, :], first[:, :], 5, 14, ALU.logical_shift_right, ALU.logical_shift_left))
            link(dve.tensor_copy(firstf[:, :], first[:, :]))
            link(dve.tensor_copy(trashf[:, :], trash[:, :]))
            dve.wait_ge(gate_turned, 1)
            dve.tensor_copy(gate_cols[:, :, :].rearrange("p m e -> p (m e)"), pA[:, 0:2 * E]).then_inc(gate_ready, 1)

            def center(t, n, b):
                par = b % 2
                dve.wait_ge(x_in[par], 16 * (2 * t + b // 2 + 1))
                s = st[:, par, 0, :]
                link(dve.tensor_reduce(s, xs[:, par, :, :], AX.X, ALU.add))
                link(dve.tensor_scalar(s, s, 1.0 / C, None, ALU.mult))
                dve.wait_ge(h_turned, n + 1)
                dve.tensor_tensor(h[:, par, :, :], xs[:, par, :, :], bcast(s, TS), ALU.subtract).then_inc(centered, 1)

            def scale(t, n, b):
                par = b % 2
                s = st[:, par, 1, :]
                dve.wait_ge(squared, n + 1)
                dve.tensor_reduce(s, sq[:, :, :], AX.X, ALU.add).then_inc(var_ready, 1)
                dve.wait_ge(std_ready, n + 1)
                link(dve.reciprocal(s, s))
                dve.tensor_tensor(h[:, par, :, :], h[:, par, :, :], bcast(s, TS), ALU.mult).then_inc(h_ready, 1)

            PER = 3 * B
            start = link.base + link.n
            with dve.Fori(0, NT) as t:
                link.base, link.n = start + t * PER, 0
                for b in range(B + 1):
                    if b < B:
                        center(t, B * t + b, b)
                    if b > 0:
                        scale(t, B * t + b - 1, b - 1)
                assert link.n == PER
            link.base, link.n = start + NT * PER, 0

            dve.wait_ge(logits_saved, 2 * NT + 1)
            link(dve.max(top[:, :], logits[:, :]))
            dve.tensor_scalar(neg_max[:, :], top[:, 0:1], -1.0, None, ALU.mult).then_inc(top_ready, 1)
            link(dve.max_index(at[:, :], top[:, :], logits[:, :]))
            dve.sem_inc(found, 1)
            link(dve.tensor_copy(idf[:, :], at[:, :]))
            link(dve.tensor_scalar(idf[:, :], idf[:, :], firstf[:, 0:1], None, ALU.add))
            dve.tensor_copy(rows_at[:, :], idf[:, :]).then_inc(at_ready, 1)
            for k in range(K):
                ins = dve.tensor_scalar(dia[:, k, :], ident[:, :], idf[:, k:k + 1], None, ALU.mult)
            ins.then_inc(dia_ready, 1)
            dve.wait_ge(exp_ready, 1)
            link(dve.reciprocal(zsum[:, 1:2], zsum[:, 0:1]))
            link(dve.tensor_scalar(val[:, :], ex[:, :], zsum[:, 1:2], None, ALU.mult))
            dve.wait_ge(idr_ready, 1)
            dve.wait_ge(rows_in, 16 * K)
            link(dve.tensor_reduce(rs[:, 0, :], rows[:, :, :], AX.X, ALU.add))
            link(dve.tensor_scalar(rs[:, 0, :], rs[:, 0, :], 1.0 / C, None, ALU.mult))
            link(dve.tensor_tensor(rn[:, :, :], rows[:, :, :], bcast(rs[:, 0, :], K), ALU.subtract))
            link(dve.tensor_tensor(rq[:, :, :], rn[:, :, :], rn[:, :, :], ALU.mult))
            dve.tensor_reduce(rs[:, 1, :], rq[:, :, :], AX.X, ALU.add).then_inc(row_step, 1)
            dve.wait_ge(row_act, 1)
            link(dve.reciprocal(rs[:, 1, :], rs[:, 1, :]))
            link(dve.tensor_tensor(rs[:, 1, :], rs[:, 1, :], val[:, :], ALU.mult))
            link(dve.tensor_tensor(rn[:, :, :], rn[:, :, :], bcast(rs[:, 1, :], K), ALU.mult))
            dve.tensor_reduce(pooled[:, 0:C], rn[:, :, :].rearrange("p k c -> p c k"), AX.X,
                              ALU.add).then_inc(pooled_ready, 1)
            dve.wait_ge(out_turned, 1)
            v = val[:, :].unsqueeze(2).to_broadcast([128, K, C])
            dve.tensor_tensor(wt[:, :, :], v, pD[:, 0:C].unsqueeze(1).to_broadcast([128, K, C]),
                              ALU.mult).then_inc(wt_ready, 1)
            for k in range(K):
                if k >= 2:
                    dve.wait_ge(summed, k - 1)
                link(dve.tensor_scalar(same[:, k % 2, :, :], idr[:, :, :], idf[:, k:k + 1], None, ALU.is_equal))
                dve.tensor_tensor(same_before[:, k % 2, :], same[:, k % 2, k, :], tri[:, :],
                                  ALU.mult).then_inc(same_ready, 1)
            dve.wait_ge(summed, K)
            link(dve.tensor_scalar(dup[:, :], pB[:, 0:K], 0.5, None, ALU.is_gt))
            link(dve.tensor_tensor(trashf[:, :], trashf[:, :], idf[:, :], ALU.subtract))
            link(dve.tensor_tensor(dup[:, :], dup[:, :], trashf[:, :], ALU.mult))
            link(dve.tensor_tensor(dup[:, :], dup[:, :], idf[:, :], ALU.add))
            dve.tensor_copy(rows_at[:, :], dup[:, :])
            dve.tensor_tensor(rows[:, :, :].rearrange("p k c -> p (k c)"), rows[:, :, :].rearrange("p k c -> p (k c)"),
                              pA[:, :], ALU.add).then_inc(new_rows, 1)

        @block.scalar
        def _(act):
            act.wait_ge(const_ready, 1)
            act.wait_ge(gate_in, 16 * NGATE)

            def square(n, b):
                act.wait_ge(centered, n + 1)
                act.wait_ge(var_ready, n + 1)
                act.activation(sq[:, :, :], h[:, b % 2, :, :], ACT.Square).then_inc(squared, 1)

            def root(n, b):
                s = st[:, b % 2, 1, :]
                act.wait_ge(var_ready, n + 2)
                act.activation(s, s, ACT.Sqrt, bias=eps[:, 0:1], scale=1.0 / C).then_inc(std_ready, 1)

            def save(n, b):
                act.wait_ge(h_turned, n + 3)
                act.wait_ge(gates_ready, n + 1)
                act.activation(ht[:, b % 2, :], pH[b % 2][:, :], ACT.Copy).then_inc(ht_saved, 1)

            with act.Fori(0, NT) as t:
                for b in range(B + 1):
                    if b < B:
                        square(B * t + b, b)
                        root(B * t + b, b)
                    if b > 0:
                        save(B * t + b - 1, b - 1)
                act.wait_ge(gates_ready, B * t + B + 2)
                out = logits[:, bass.ds(t * TILE, TILE)].rearrange("q (p j m) -> q m j p", j=TS // 2, m=2)
                for m in range(2):
                    act.activation(out[:, m, :, :], pG[m][:, :].rearrange("q (j p) -> q j p", p=128), ACT.Identity,
                                   bias=gb[:, 0:1]).then_inc(logits_saved, 1)
            act.wait_ge(top_ready, 1)
            act.activation(ex[:, :], top[:, :], ACT.Exp, bias=neg_max[:, 0:1])
            act.wait_ge(at_ready, 1)
            act.activation(logits[:, :], logits[:, :], ACT.Exp, bias=neg_max[:, 0:1],
                           accum_out=zsum[:, 0:1]).then_inc(exp_ready, 1)
            act.wait_ge(dia_ready, 2)
            act.activation(idr[:, 0:4, :].rearrange("p k i -> p (k i)"), pB[:, :], ACT.Copy)
            act.activation(idr[:, 4:8, :].rearrange("p k i -> p (k i)"), pC[:, :], ACT.Copy).then_inc(idr_ready, 1)
            act.wait_ge(row_step, 1)
            act.activation(rs[:, 1, :], rs[:, 1, :], ACT.Sqrt, bias=eps[:, 0:1], scale=1.0 / C).then_inc(row_act, 1)
            act.wait_ge(pooled_turned, 1)
            act.activation(pooled_t[:, :], pD[0:C + 1, 0:128], ACT.Copy).then_inc(pooled_saved, 1)
            act.wait_ge(hid_ready, 1)
            act.activation(hid[:, :, :, :].rearrange("p m e b -> p (m e b)"), pH[0][:, 0:2 * E * B],
                           ACT.Gelu).then_inc(gelu_ready, 1)
            act.wait_ge(out_ready, 1)
            act.activation(out_t[:, :], pH[1][0:C, 0:128], ACT.Copy).then_inc(out_saved, 1)

        @block.tensor
        def _(pe):
            pe.wait_ge(const_ready, 1)
            pe.wait_ge(gate_in, 16 * NGATE)
            for m in range(2):
                ins = pe.transpose(pA[:, E * m:E * m + E], gate_rows[:, m, :], ident[0:E, 0:E])
            ins.then_inc(gate_turned, 1)
            pe.wait_ge(gate_ready, 1)
            pe.sem_inc(h_turned, 2)
            pe.sem_inc(gates_ready, 1)
            pe.sem_inc(ht_saved, 1)

            def turn(n, b):
                pe.wait_ge(h_ready, n + 3)
                pe.wait_ge(ht_saved, n + 1)
                for j in range(TS // 2):
                    ins = pe.transpose(pH[b % 2][:, 128 * j:128 * j + 128],
                                       h[:, b % 2, 2 * j:2 * j + 2, :].rearrange("p j c -> p (j c)"), ident[:, :])
                ins.then_inc(h_turned, 1)

            def gates(n, b, t):
                pe.wait_ge(ht_saved, n + 3)
                if b == 0:
                    pe.wait_ge(logits_saved, 2 * t + 1)
                for m in range(2):
                    ins = pe.matmul(pG[m][E * b:E * b + E, :], gate_cols[:, m, :], ht[:, b % 2, :],
                                    start=True, stop=True)
                ins.then_inc(gates_ready, 1)

            with pe.Fori(0, NT) as t:
                for b in range(B):
                    turn(B * t + b, b)
                    gates(B * t + b, b, t)
            pe.wait_ge(dia_ready, 1)
            for k in range(K):
                ins = pe.matmul([pB, pC][k // 4][:, 128 * (k % 4):128 * (k % 4) + 128], ones[:, :], dia[:, k, :],
                                start=True, stop=True)
            ins.then_inc(dia_ready, 1)
            pe.wait_ge(pooled_ready, 1)
            pe.transpose(pD[0:C + 1, 0:128], pooled[:, :], ident[:, :]).then_inc(pooled_turned, 1)
            pe.wait_ge(pooled_saved, 1)
            pe.wait_ge(w_in, 16 * (NW + 1))
            for e in range(E):
                for m in range(2):
                    o = (m * E + e) * B
                    ins = pe.matmul(pH[0][:, o:o + B], w1[:, e, 128 * m:128 * m + 128],
                                    pooled_t[:, e:128:E], start=True, stop=True)
            ins.then_inc(hid_ready, 1)
            pe.wait_ge(gelu_ready, 1)
            for e in range(E):
                o = pH[1][0:C, e:128:E]
                for m in range(2):
                    pe.matmul(o, w2[:, m, e, :], hid[:, m, e, :], start=(m == 0), stop=False)
                ins = pe.matmul(o, w2b[0:1, e, :], ones[0:1, 0:B], start=False, stop=True)
            ins.then_inc(out_ready, 1)
            pe.wait_ge(out_saved, 1)
            pe.transpose(pD[:, 0:C], out_t[:, :], ident[0:C, 0:C]).then_inc(out_turned, 1)
            pe.wait_ge(wt_ready, 1)
            for j in range(K):
                pe.wait_ge(same_ready, j + 1)
                for k in range(K):
                    pe.matmul(pA[:, C * k:C * k + C], same[:, j % 2, k, :], wt[:, j, :], start=(j == 0 and k == 0),
                              stop=(j == K - 1), skip_group_check=True)
                for k in range(j, K):
                    m = same_before[:, j % 2, :] if k == j else same[:, j % 2, k, :]
                    ins = pe.matmul(pB[:, k:k + 1], m, ones[:, 0:1], start=(j == 0 and k == 0), stop=(k == j),
                                    skip_group_check=True)
                ins.then_inc(summed, 1)


def stage_conv_bn(nc, tok, gamma, beta, w_lbp, w_1x1, b_1x1):
    TS = 8
    TILE = 128 * TS
    R, P2 = TILE // W, W // 2
    NT = S // TILE
    EPS_LN, EPS_BN = 1e-6, 1e-5
    with ExitStack() as ctx:
        a = Arena(nc, ctx, "cb")
        ident = a.sb("ident", [128, 128])
        halves = a.sb("halves", [128, 128])
        ones = a.sb("ones", [1, 128])
        brow = a.sb("brow", [1, 2, C])
        bias = a.sb("bias", [128, 1, 2, C])
        eps = a.sb("eps", [128, 2])
        gam = a.sb("gam", [128, 2])
        w_in_rows = a.sb("w_in_rows", [C, C, 9])
        w_rows = a.sb("w_rows", [C, 9, 2, C])
        w_tap = a.sb("w_tap", [128, 9, C])
        wc = a.sb("wc", [128, 3, 2, 128])
        w1_rows = a.sb("w1_rows", [128, 128])
        w1 = a.sb("w1", [128, 128])
        u = a.sb("u", [128, B, H, P2])
        xs = a.sb("xs", [128, 2, TS, C])
        h = a.sb("h", [128, 2, TS, C])
        sq = a.sb("sq", [128, TS, C])
        st = a.sb("st", [128, 2, 2, TS])
        stats = a.sb("stats", [128, B * NT, 6])
        mv = a.sb("mv", [128, 8])
        zero = a.sb("zero", [128, P2 + 2])
        xn = a.sb("xn", [128, 2, R + 2, P2])
        xb = a.sb("xb", [128, 2, R + 2, P2])
        y = a.sb("y", [128, 2, R, P2])
        pH = [a.ps(f"pH{i}", [128, 512]) for i in range(2)]
        pC = [a.ps(f"pC{i}", [128, 512]) for i in range(2)]
        pY = [a.ps(f"pY{i}", [128, 512]) for i in range(2)]
        pool_done = a.sem("pool_done")
        dve_done = a.sem("dve_done")
        zeros_ready = a.sem("zeros_ready")
        const_ready = a.sem("const_ready")
        w_in = a.sem("w_in")
        w_dup = a.sem("w_dup")
        w_turned = a.sem("w_turned")
        w_ready = a.sem("w_ready")
        x_in = [a.sem(f"x_in{i}") for i in range(2)]
        centered = a.sem("centered")
        squared = a.sem("squared")
        var_ready = a.sem("var_ready")
        std_ready = a.sem("std_ready")
        h_ready = a.sem("h_ready")
        h_turned = a.sem("h_turned")
        u_saved = a.sem("u_saved")
        stats_ready = a.sem("stats_ready")
        mean_in = a.sem("mean_in")
        mean_out = a.sem("mean_out")
        bn_std = a.sem("bn_std")
        bn_ready = a.sem("bn_ready")
        r_in = [a.sem(f"r_in{i}") for i in range(2)]
        r_biased = a.sem("r_biased")
        xn_ready = a.sem("xn_ready")
        conv_ready = a.sem("conv_ready")
        y_ready = a.sem("y_ready")
        mixed = a.sem("mixed")
        sum_ready = a.sem("sum_ready")
        stored = [a.sem(f"stored{i}") for i in range(2)]
        block = ctx.enter_context(nc.Block())
        NW = 2 + 1 + 4 + 1
        BN_LINKS = 12

        def over_strips(eng, body, link=None, per=0):
            start = (link.base + link.n) if link else 0

            def strip(b, i, n, par, top, bottom):
                if link:
                    link.base, link.n = start + n * per, 0
                body(b, i, n, par, top, bottom)
                assert not link or link.n == per, link.n

            with eng.Fori(0, B) as b:
                strip(b, 0, b * NT, 0, True, False)
                with eng.Fori(0, NT // 2 - 1) as t:
                    for k in range(2):
                        strip(b, 2 * t + 1 + k, b * NT + 2 * t + 1 + k, (1 + k) % 2, False, False)
                strip(b, NT - 1, b * NT + NT - 1, 1, False, True)
            if link:
                link.base, link.n = start + B * NT * per, 0

        def tokens_by_pair(n):
            return tok[bass.ds(n * TILE, TILE), :].rearrange("(q p j) c -> p q (j c)", p=128, j=2)

        @block.sync
        def _(sp):
            sp.dma_start(w_in_rows[:, :, :], w_lbp.rearrange("o i a b -> o i (a b)")).then_inc(w_in, 16)
            sp.dma_start(brow[:, 0, :], b_1x1.rearrange("(a c) -> a c", a=1)).then_inc(w_in, 16)
            sp.wait_ge(zeros_ready, 1)
            for p in range(2):
                part = slice(64 * p, 64 * p + 64)
                sp.dma_start(w1_rows[part, part], w_1x1.rearrange("o i a b -> o (i a b)")).then_inc(w_in, 16)
                sp.dma_start(gam[part, 0:1], gamma.rearrange("(c a) -> c a", a=1)).then_inc(w_in, 16)
                sp.dma_start(gam[part, 1:2], beta.rearrange("(c a) -> c a", a=1)).then_inc(w_in, 16)
            with sp.Fori(0, NT) as t:
                for b in range(B):
                    sp.wait_ge(h_ready, B * t + b + 1)
                    sp.dma_start(xs[:, b % 2, :, :], tok[bass.ds(b * S + t * TILE, TILE), :].rearrange(
                        "(p j) c -> p j c", j=TS)).then_inc(x_in[b % 2], 16)
            sp.wait_ge(h_ready, B * NT + 2)

            def load(n, par):
                sp.wait_ge(sum_ready, n + 1)
                sp.dma_start(xs[:, par, :, :].rearrange("p (q j) c -> p q (j c)", j=2),
                             tokens_by_pair(n)).then_inc(r_in[par], 16)

            def store(n, par):
                sp.wait_ge(sum_ready, n + 3)
                sp.dma_start(tokens_by_pair(n), h[:, par, :, :].rearrange(
                    "p (q j) c -> p q (j c)", j=2)).then_inc(stored[par], 16)

            load(0, 0)
            with sp.Fori(0, B * NT // 2 - 1) as t:
                for par in range(2):
                    load(2 * t + par + 1, 1 - par)
                    store(2 * t + par, par)
            load(B * NT - 1, 1)
            for par in range(2):
                store(B * NT - 2 + par, par)
            for par in range(2):
                sp.wait_ge(stored[par], 16 * B * NT // 2 + 16)

        @block.gpsimd
        def _(pool):
            link = Link(pool, pool_done)
            for s in (var_ready, conv_ready, u_saved, y_ready):
                pool.sem_inc(s, 1)
            for s in stored:
                pool.sem_inc(s, 16)
            pool.memset(w1_rows[:, :], 0.0).then_inc(zeros_ready, 1)
            pool.memset(zero[:, :], 0.0)
            pool.memset(xb[:, :, :, :], 0.0)
            pool.memset(wc[:, :, :, :], 0.0)
            pool.memset(eps[:, 0:1], EPS_LN)
            pool.memset(eps[:, 1:2], EPS_BN)
            pool.memset(ones[:, :], 1.0)
            pool.memset(halves[:, :], 0.0)
            eye(pool, link, ident[:, :])
            for k in (0, 64, -64):
                link(pool.affine_select(out=halves[:, :], in_=halves[:, :], compare_op=ALU.not_equal, fill=0.5,
                                        base=k, pattern=[[-1, 128]], channel_multiplier=1))
            pool.sem_inc(const_ready, 1)
            pool.sem_inc(h_ready, 2)
            pool.sem_inc(sum_ready, 2)
            pool.wait_ge(bn_ready, 1)

            def add_bias(b, i, n, par, top, bottom):
                pool.wait_ge(r_in[par], 8 * (n - par) + 16)
                v = xs[:, par, :, :].rearrange("p (q j) c -> p q (j c)", j=2)
                pool.tensor_tensor(v, v, bias[:, :, :, :].rearrange("p a j c -> p a (j c)").to_broadcast([128, 4, 128]),
                                   ALU.add).then_inc(r_biased, 1)

            over_strips(pool, add_bias)

        @block.vector
        def _(dve):
            link = Link(dve, dve_done)
            dve.wait_ge(w_in, 16 * NW)
            dve.wait_ge(const_ready, 1)
            for d in range(2):
                ins = dve.tensor_copy(w_rows[:, :, d, :], w_in_rows[:, :, :].rearrange("o i k -> o k i"))
            link(dve.tensor_copy(brow[:, 1, :], brow[:, 0, :]))
            dve.sem_inc(w_dup, 1)
            dve.wait_ge(w_turned, 1)
            link(dve.tensor_copy(w_tap[:, 0:8, :].rearrange("p k o -> p (k o)"), pH[0][:, :]))
            link(dve.tensor_copy(w_tap[:, 8, :], pH[1][:, 0:64]))
            dve.tensor_copy(bias[:, 0, :, :].rearrange("p j c -> p (j c)"), pH[1][:, 64:192])
            dve.tensor_copy(w1[:, :], pC[0][:, 0:128])
            for m, pi, po, tap in parity_blocks(3, 1):
                rows, cols = slice(64 * pi, 64 * pi + 64), slice(64 * po, 64 * po + 64)
                ins = dve.tensor_copy(wc[rows, :, abs(m), cols], w_tap[rows, tap:9:3, :])
            ins.then_inc(w_ready, 1)

            def center(t, n, b):
                par = b % 2
                dve.wait_ge(x_in[par], 16 * (2 * t + b // 2 + 1))
                s = st[:, par, 0, :]
                link(dve.tensor_reduce(s, xs[:, par, :, :], AX.X, ALU.add))
                link(dve.tensor_scalar(s, s, 1.0 / C, None, ALU.mult))
                dve.wait_ge(h_turned, n + 1)
                dve.tensor_tensor(h[:, par, :, :], xs[:, par, :, :], bcast(s, TS), ALU.subtract).then_inc(centered, 1)

            def scale(t, n, b):
                par = b % 2
                s = st[:, par, 1, :]
                dve.wait_ge(squared, n + 1)
                dve.tensor_reduce(s, sq[:, :, :], AX.X, ALU.add).then_inc(var_ready, 1)
                dve.wait_ge(std_ready, n + 1)
                link(dve.reciprocal(s, s))
                dve.tensor_tensor(h[:, par, :, :], h[:, par, :, :], bcast(s, TS), ALU.mult).then_inc(h_ready, 1)

            def gather_stats(t, n, b):
                dve.wait_ge(u_saved, n + 3)
                dve.bn_stats(stats[:, n, :], u[:, b, bass.ds(t * R, R), :]).then_inc(stats_ready, 1)

            PER = 3 * B
            start = link.base + link.n
            with dve.Fori(0, NT) as t:
                link.base, link.n = start + t * PER, 0
                for b in range(B + 2):
                    if b < B:
                        center(t, B * t + b, b)
                    if 0 < b <= B:
                        scale(t, B * t + b - 1, b - 1)
                    if b > 1:
                        gather_stats(t, B * t + b - 2, b - 2)
                assert link.n == PER
            link.base, link.n = start + NT * PER, 0
            dve.wait_ge(stats_ready, B * NT)
            mean, var, avg, dev, sc, sh = (mv[:, k:k + 1] for k in range(6))
            link(dve.bn_aggr(mv[:, 0:2], stats[:, :, :].rearrange("p n s -> p (n s)")))
            dve.sem_inc(mean_in, 1)
            dve.wait_ge(mean_out, 1)
            link(dve.tensor_copy(avg, pC[0][:, 0:1]))
            link(dve.tensor_tensor(dev, mean, avg, ALU.subtract))
            link(dve.tensor_tensor(dev, dev, dev, ALU.mult))
            link(dve.tensor_tensor(var, var, dev, ALU.add))
            dve.sem_inc(mean_in, 1)
            dve.wait_ge(bn_std, 1)
            link(dve.reciprocal(sc, sc))
            link(dve.tensor_tensor(sc, sc, gam[:, 0:1], ALU.mult))
            link(dve.tensor_tensor(sh, avg, sc, ALU.mult))
            dve.tensor_tensor(sh, gam[:, 1:2], sh, ALU.subtract).then_inc(bn_ready, 1)

            def add_relu(b, i, n, par):
                dve.wait_ge(conv_ready, n + 3)
                dve.wait_ge(mixed, n + 1)
                dve.scalar_tensor_tensor(y[:, par, :, :].rearrange("p r w -> p (r w)"), pC[par][:, :], 0.0,
                                         u_flat(b, i), ALU.max, ALU.add).then_inc(y_ready, 1)

            def u_flat(b, i):
                return u[:, :, :, :].rearrange("p b r w -> p (b r w)")[:, bass.ds((b * H + i * R) * P2, R * P2)]

            def add_rest(n, par):
                dve.wait_ge(mixed, n + 3)
                dve.wait_ge(r_biased, n + 1)
                dve.wait_ge(stored[par], 8 * (n - par) + 16)
                dve.tensor_tensor(h[:, par, :, :].rearrange("p t c -> p (t c)"),
                                  xs[:, par, :, :].rearrange("p t c -> p (t c)"), pY[par][:, :], ALU.add).then_inc(sum_ready, 1)

            def strip(b, i, n, par, top, bottom):
                add_relu(b, i, n, par)
                add_rest(n, par)

            over_strips(dve, strip)

        @block.scalar
        def _(act):
            act.wait_ge(const_ready, 1)

            def square(n, b):
                act.wait_ge(centered, n + 1)
                act.wait_ge(var_ready, n + 1)
                act.activation(sq[:, :, :], h[:, b % 2, :, :], ACT.Square).then_inc(squared, 1)

            def root(n, b):
                s = st[:, b % 2, 1, :]
                act.wait_ge(var_ready, n + 2)
                act.activation(s, s, ACT.Sqrt, bias=eps[:, 0:1], scale=1.0 / C).then_inc(std_ready, 1)

            def save(t, n, b):
                act.wait_ge(h_turned, n + 3)
                dst = u[:, b, bass.ds(t * R, R), :].rearrange("q r (a j) -> q j r a", j=TS // 2)
                act.activation(dst, pH[b % 2][:, :].rearrange("q (j r a) -> q j r a", j=TS // 2, r=R),
                               ACT.Copy).then_inc(u_saved, 1)

            with act.Fori(0, NT) as t:
                for b in range(B + 1):
                    if b < B:
                        square(B * t + b, b)
                        root(B * t + b, b)
                    if b > 0:
                        save(t, B * t + b - 1, b - 1)
            act.wait_ge(mean_out, 2)
            act.activation(mv[:, 4:5], pC[1][:, 0:1], ACT.Sqrt, bias=eps[:, 1:2]).then_inc(bn_std, 1)
            act.wait_ge(bn_ready, 1)

            def normalise(b, i, n, par, top, bottom):
                act.wait_ge(conv_ready, n + 1)
                r0, r1 = int(top), R + 2 - int(bottom)
                kw = dict(bias=mv[:, 5:6], scale=mv[:, 4:5])
                if top or bottom:
                    z = 0 if top else R + 1
                    act.activation(xn[:, par, z, :], zero[:, 0:P2], ACT.Copy)
                    act.activation(xb[:, par, z, :], zero[:, 0:P2], ACT.Copy)
                src = u[:, b, bass.ds(i * R + r0 - 1, r1 - r0), :]
                act.activation(xn[:, par, r0:r1, :], src, ACT.Identity, **kw)
                for p in range(2):
                    rows = slice(64 * p, 64 * p + 64)
                    ins = act.activation(xb[rows, par, r0:r1, p:P2 - 1 + p], u[rows, b, bass.ds(i * R + r0 - 1, r1 - r0),
                                         1 - p:P2 - p], ACT.Identity, bias=mv[rows, 5:6], scale=mv[rows, 4:5])
                ins.then_inc(xn_ready, 1)

            def strip(b, i, n, par, top, bottom):
                normalise(b, i, n, par, top, bottom)

            over_strips(act, strip)

        @block.tensor
        def _(pe):
            pe.wait_ge(const_ready, 1)
            pe.wait_ge(w_dup, 1)
            for k in range(9):
                pe.transpose(pH[k // 8][:, 64 * (k % 8):64 * (k % 8) + 64],
                             w_rows[:, k, :, :].rearrange("o d i -> o (d i)"), ident[0:C, 0:C])
            pe.matmul(pH[1][:, 64:192], ones[:, :], brow[:, :, :].rearrange("a j c -> a (j c)"), start=True, stop=True)
            pe.transpose(pC[0][:, 0:128], w1_rows[:, :], ident[:, :]).then_inc(w_turned, 1)
            pe.wait_ge(w_ready, 1)
            pe.sem_inc(h_turned, 2)
            pe.sem_inc(u_saved, 1)
            pe.sem_inc(y_ready, 1)
            pe.sem_inc(mixed, 2)
            pe.sem_inc(conv_ready, 1)

            def turn(n, b):
                pe.wait_ge(h_ready, n + 3)
                pe.wait_ge(u_saved, n + 1)
                for j in range(TS // 2):
                    ins = pe.transpose(pH[b % 2][:, 128 * j:128 * j + 128],
                                       h[:, b % 2, 2 * j:2 * j + 2, :].rearrange("p j c -> p (j c)"), ident[:, :])
                ins.then_inc(h_turned, 1)

            with pe.Fori(0, NT) as t:
                for b in range(B):
                    turn(B * t + b, b)
            for k in range(2):
                pe.wait_ge(mean_in, k + 1)
                pe.matmul(pC[k][:, 0:1], halves[:, :], mv[:, k:k + 1], start=True, stop=True).then_inc(mean_out, 1)

            def strip(b, i, n, par, top, bottom):
                pe.wait_ge(xn_ready, n + 1)
                pe.wait_ge(y_ready, n + 1)
                for k in range(3):
                    for beside, src in enumerate((xn, xb)):
                        ins = pe.matmul(pC[par][:, :], wc[:, k, beside, :], src[:, par, k:k + R, :],
                                        start=(k == 0 and not beside), stop=(k == 2 and beside == 1))
                ins.then_inc(conv_ready, 1)
                pe.wait_ge(y_ready, n + 3)
                pe.wait_ge(sum_ready, n + 1)
                yt = y[:, par, :, :].rearrange("p r w -> p (r w)")
                for q in range(4):
                    ins = pe.matmul(pY[par][:, 128 * q:128 * q + 128], yt[:, 128 * q:128 * q + 128], w1[:, :],
                                    start=True, stop=True)
                ins.then_inc(mixed, 1)

            over_strips(pe, strip)


def stage_top2_ffn(nc, stage, tok, router_w, router_b, expert_w, expert_b, image=None):
    E = 8
    TS = 8
    TILE = 128 * TS
    N = B * S // TILE
    EPS = 1e-5
    BIG = 1e30
    NX = 4
    with ExitStack() as ctx:
        a = Arena(nc, ctx, stage)
        ident = a.sb("ident", [128, 128])
        eps = a.sb("eps", [128, 1])
        order = a.sb("order", [128, E])
        order_i = a.sb("order_i", [128, E], mybir.dt.int32)
        rw = a.sb("rw", [C + 1, E])
        ew = a.sb("ew", [C + 1, E, C])
        xs = a.sb("xs", [128, NX, TS, C])
        h = a.sb("h", [128, 2, TS, C + 1])
        sq = a.sb("sq", [128, TS, C])
        st = a.sb("st", [128, 2, 2, TS])
        ht = a.sb("ht", [C + 1, 2, TS, 128])
        lg = a.sb("lg", [128, TS, E])
        eq = a.sb("eq", [128, TS, E])
        one = a.sb("one", [128, 2, TS, E])
        mx = a.sb("mx", [128, 4, TS])
        ex = a.sb("ex", [128, 2, TS])
        gt = a.sb("gt", [128, 2, TS])
        gates = a.sb("gates", [128, 2, TS, E])
        prod = a.sb("prod", [128, 4, E, C])
        part = a.sb("part", [128, 2, 2, 4, C])
        y = a.sb("y", [128, 2, TS, C])
        yt = a.sb("yt", [128, 2, TS // 2, 128])
        pT = [a.ps(f"pT{i}", [128, 512]) for i in range(2)]
        pL = a.ps("pL", [128, 512])
        pE = [a.ps(f"pE{i}", [128, 512]) for i in range(4)]
        pY = a.ps("pY", [128, 512])
        pool_done = a.sem("pool_done")
        pool_step = a.sem("pool_step")
        dve_done = a.sem("dve_done")
        const_ready = a.sem("const_ready")
        w_in = a.sem("w_in")
        x_in = [a.sem(f"x_in{i}") for i in range(NX)]
        centered = a.sem("centered")
        squared = a.sem("squared")
        var_ready = a.sem("var_ready")
        std_ready = a.sem("std_ready")
        h_ready = a.sem("h_ready")
        h_turned = a.sem("h_turned")
        ht_saved = a.sem("ht_saved")
        logits_ready = a.sem("logits_ready")
        gap_ready = a.sem("gap_ready")
        gap_exp = a.sem("gap_exp")
        experts_ready = a.sem("experts_ready")
        weighted = a.sem("weighted")
        summed = a.sem("summed")
        y_ready = a.sem("y_ready")
        y_turned = a.sem("y_turned")
        yt_saved = a.sem("yt_saved")
        stored = [a.sem(f"stored{i}") for i in range(2)]
        block = ctx.enter_context(nc.Block())
        UN = 4

        def over_tiles(eng, body, link=None, per=0, tiles=N, left=()):
            loops, rest = divmod(tiles - len(left), UN)
            start = (link.base + link.n) if link else 0

            def tile(n, k):
                if link:
                    link.base, link.n = start + n * per, 0
                body(n, k)
                assert not link or link.n == per, link.n

            with eng.Fori(0, loops) as t:
                for k in range(UN):
                    tile(UN * t + k, k)
            for k in range(rest):
                tile(UN * loops + k, k)
            if link:
                link.base, link.n = start + (tiles - len(left)) * per, 0
            for k, last in enumerate(left):
                last(tiles - len(left) + k, tiles - len(left) + k)

        def over_late_tiles(eng, tile, finish):
            if image is None:
                over_tiles(eng, tile, left=[lambda n, k: tile(n, k, 1), lambda n, k: tile(n, k, 0)])
                return
            for k in range(UN):
                tile(k, k, first=(k == 0))
            with eng.Fori(1, (N - 2) // UN) as t:
                for k in range(UN):
                    tile(UN * t + k, k)
            for n in range((N - 2) // UN * UN, N):
                tile(n, n, min(2, N - 1 - n))
            finish()

        def tokens(n):
            rows = tok[bass.ds(n * TILE, TILE), :]
            return rows.rearrange("(p j) c -> p j c", j=TS) if image is None else rows.rearrange("(r w) c -> w r c", w=W)

        def image_rows(n):
            b, i = n // (H // TS), n % (H // TS)
            v = image[bass.ds(b, 1), :, bass.ds(i * TS, TS), :].rearrange("a c (q r) w -> r (a c) q w", r=2)
            return [v[r] for r in range(2)]

        @block.sync
        def _(sp):
            sp.dma_start(rw[0:C, :], router_w).then_inc(w_in, 16)
            sp.dma_start(rw[C:C + 1, :], router_b.rearrange("(a e) -> a e", a=1)).then_inc(w_in, 16)
            sp.dma_start(ew[0:C, :, :], expert_w.rearrange("e d c -> d e c")).then_inc(w_in, 16)
            sp.dma_start(ew[C:C + 1, :, :], expert_b.rearrange("(a e) c -> a e c", a=1)).then_inc(w_in, 16)

            def load(n, k):
                sp.wait_ge(y_ready, n + 1)
                sp.dma_start(xs[:, k % NX, :, :], tokens(n)).then_inc(x_in[k % NX], 16)

            def store(n, k):
                if image is None:
                    sp.wait_ge(y_ready, n + 5)
                    sp.dma_start(tokens(n), y[:, k % 2, :, :]).then_inc(stored[k % 2], 16)
                else:
                    sp.wait_ge(yt_saved, n + 2)
                    for r in range(2):
                        dst = image_rows(n)[r]
                        sp.dma_start(dst, yt[64 * r:64 * r + 64, k % 2, :, :]).then_inc(stored[k % 2], 16)

            def tile(n, k):
                load(n + 3, k + 3)
                store(n, k)

            for n in range(3):
                load(n, n)
            over_tiles(sp, tile, left=[store] * 3)
            for k in range(2):
                sp.wait_ge(stored[k], 16 * (1 if image is None else 2) * N // 2 + 16)

        @block.gpsimd
        def _(pool):
            link = Link(pool, pool_done)
            for s in (ht_saved, gap_ready, yt_saved):
                pool.sem_inc(s, 1)
            for s in stored:
                pool.sem_inc(s, 16)
            pool.memset(eps[:, :], EPS)
            pool.memset(h[:, :, :, :], 1.0)
            eye(pool, link, ident[:, :])
            pool.iota(order_i[:, :], pattern=[[-1, E]], base=E, channel_multiplier=0).then_inc(const_ready, 1)
            pool.sem_inc(y_ready, 4)
            step = Link(pool, pool_step)

            def combine(n, k):
                for q in range(4):
                    pool.wait_ge(weighted, 8 * n + 2 * q + 6)
                    pq = part[:, q % 2, :, :, :]
                    pr = prod[:, 2 * (q % 2):2 * (q % 2) + 2, :, :]
                    pool.tensor_tensor(pq, pr[:, :, 0:4, :], pr[:, :, 4:8, :], ALU.add).then_inc(summed, 1)
                    pool.wait_ge(summed, 4 * n + q + 3)
                    step(pool.tensor_tensor(pq[:, :, 0:2, :], pq[:, :, 0:2, :], pq[:, :, 2:4, :], ALU.add))
                    step(pool.tensor_tensor(pq[:, :, 0, :], pq[:, :, 0, :], pq[:, :, 1, :], ALU.add))
                    if q == 0:
                        if image is None:
                            pool.wait_ge(stored[k % 2], 8 * (n - k % 2) + 16)
                        else:
                            pool.wait_ge(y_turned, n + 1)
                    ins = pool.tensor_tensor(y[:, k % 2, 2 * q:2 * q + 2, :], pq[:, :, 0, :],
                                             xs[:, k % NX, 2 * q:2 * q + 2, :], ALU.add)
                ins.then_inc(y_ready, 1)

            over_tiles(pool, combine, step, 8)

        @block.vector
        def _(dve):
            link = Link(dve, dve_done)
            dve.wait_ge(const_ready, 1)
            link(dve.tensor_copy(order[:, :], order_i[:, :]))

            def center(n, k):
                x, s = xs[:, k % NX, :, :], st[:, k % 2, 0, :]
                dve.wait_ge(x_in[k % NX], 16 * ((n - k % NX) // NX + 1))
                link(dve.tensor_reduce(s, x, AX.X, ALU.add))
                link(dve.tensor_scalar(s, s, 1.0 / C, None, ALU.mult))
                dve.wait_ge(h_turned, n + 1)
                dve.tensor_tensor(h[:, k % 2, :, 0:C], x, bcast(s, TS), ALU.subtract).then_inc(centered, 1)

            def spread(n, k):
                dve.wait_ge(squared, n + 1)
                dve.tensor_reduce(st[:, k % 2, 1, :], sq[:, :, :], AX.X, ALU.add).then_inc(var_ready, 1)

            def scale(n, k):
                s = st[:, k % 2, 1, :]
                dve.wait_ge(std_ready, n + 1)
                link(dve.reciprocal(s, s))
                v = h[:, k % 2, :, 0:C]
                dve.tensor_tensor(v, v, bcast(s, TS), ALU.mult).then_inc(h_ready, 1)

            def pick(which, n):
                m, o = mx[:, which, :], one[:, which, :, :]
                link(dve.tensor_reduce(m, lg[:, :, :], AX.X, ALU.max))
                link(dve.tensor_tensor(eq[:, :, :], lg[:, :, :], bcast(m, TS, E), ALU.is_equal))
                link(dve.tensor_tensor(eq[:, :, :], eq[:, :, :], order[:, :].unsqueeze(1).to_broadcast([128, TS, E]),
                                       ALU.mult))
                link(dve.tensor_reduce(mx[:, 2 + which, :], eq[:, :, :], AX.X, ALU.max))
                link(dve.tensor_tensor(o, eq[:, :, :], bcast(mx[:, 2 + which, :], TS, E), ALU.is_equal))

            def route(n, k):
                dve.wait_ge(logits_ready, n + 1)
                link(dve.tensor_copy(lg[:, :, :].rearrange("p t e -> p (t e)"), pL[:, 0:TS * E]))
                pick(0, n)
                link(dve.scalar_tensor_tensor(lg[:, :, :].rearrange("p t e -> p (t e)"),
                                              one[:, 0, :, :].rearrange("p t e -> p (t e)"), -BIG,
                                              lg[:, :, :].rearrange("p t e -> p (t e)"), ALU.mult, ALU.add))
                pick(1, n)
                dve.tensor_tensor(ex[:, k % 2, :], mx[:, 1, :], mx[:, 0, :], ALU.subtract).then_inc(gap_ready, 1)

            def gate(n, k):
                dve.wait_ge(gap_exp, n + 1)
                link(dve.tensor_scalar(gt[:, 0, :], ex[:, k % 2, :], 1.0, None, ALU.add))
                link(dve.reciprocal(gt[:, 0, :], gt[:, 0, :]))
                link(dve.tensor_tensor(gt[:, 1, :], ex[:, k % 2, :], gt[:, 0, :], ALU.mult))
                link(dve.tensor_tensor(one[:, 0, :, :], one[:, 0, :, :], bcast(gt[:, 0, :], TS, E), ALU.mult))
                link(dve.tensor_tensor(one[:, 1, :, :], one[:, 1, :, :], bcast(gt[:, 1, :], TS, E), ALU.mult))
                link(dve.tensor_tensor(gates[:, k % 2, :, :], one[:, 0, :, :], one[:, 1, :, :], ALU.add))

            def weigh(n, k, j0):
                for j in (j0, j0 + 1):
                    dve.wait_ge(experts_ready, 8 * n + j + 1)
                    if j == j0:
                        dve.wait_ge(summed, 4 * n + j // 2 + 1)
                    dve.tensor_tensor(prod[:, j % 4, :, :], pE[j % 4][:, :].rearrange("p (e c) -> p e c", e=E),
                                      bcast(gates[:, k % 2, j, :], E), ALU.mult).then_inc(weighted, 1)

            def tile(n, k, ahead=2):
                if ahead > 1:
                    center(n + 2, k + 2)
                weigh(n, k, 0)
                if ahead > 1:
                    spread(n + 2, k + 2)
                weigh(n, k, 2)
                if ahead > 1:
                    scale(n + 2, k + 2)
                if ahead > 0:
                    route(n + 1, k + 1)
                weigh(n, k, 4)
                if ahead > 0:
                    gate(n + 1, k + 1)
                weigh(n, k, 6)

            for n in range(2):
                center(n, n)
                spread(n, n)
                scale(n, n)
            route(0, 0)
            gate(0, 0)
            over_tiles(dve, tile, link, 3 + 1 + 5 + 1 + 5 + 6,
                       left=[lambda n, k: tile(n, k, 1), lambda n, k: tile(n, k, 0)])

        @block.scalar
        def _(act):
            act.wait_ge(const_ready, 1)

            def spread(n, k):
                act.wait_ge(centered, n + 1)
                act.activation(sq[:, :, :], h[:, k % 2, :, 0:C], ACT.Square).then_inc(squared, 1)
                s = st[:, k % 2, 1, :]
                act.wait_ge(var_ready, n + 1)
                act.activation(s, s, ACT.Sqrt, bias=eps[:, 0:1], scale=1.0 / C).then_inc(std_ready, 1)

            def save_turned(n, k):
                for m in range(2):
                    act.wait_ge(h_turned, n + 3)
                    act.activation(ht[:, k % 2, 4 * m:4 * m + 4, :].rearrange("c t p -> c (t p)"), pT[m][0:C + 1, :],
                                   ACT.Copy).then_inc(ht_saved, 1)

            def gap(n, k):
                act.wait_ge(gap_ready, n + 2)
                act.activation(ex[:, k % 2, :], ex[:, k % 2, :], ACT.Exp).then_inc(gap_exp, 1)

            def save_out(n, k):
                act.wait_ge(y_turned, n + 3)
                act.wait_ge(stored[k % 2], 8 * 2 * (n - k % 2) + 16)
                act.activation(yt[:, k % 2, :, :].rearrange("p q w -> p (q w)"), pY[:, :],
                               ACT.Copy).then_inc(yt_saved, 1)

            def tile(n, k, ahead=2, first=False):
                if ahead > 0:
                    save_turned(n + 1, k + 1)
                if ahead > 1:
                    spread(n + 2, k + 2)
                if image is not None and not first:
                    save_out(n - 1, k - 1)
                if ahead > 0:
                    gap(n + 1, k + 1)

            for n in range(2):
                spread(n, n)
            save_turned(0, 0)
            gap(0, 0)
            over_late_tiles(act, tile, image is not None and (lambda: save_out(N - 1, N - 1)))

        @block.tensor
        def _(pe):
            pe.wait_ge(const_ready, 1)
            pe.wait_ge(w_in, 16 * 4)
            pe.sem_inc(h_turned, 2)
            pe.sem_inc(y_turned, 2)
            pe.sem_inc(summed, 2)
            pe.sem_inc(weighted, 4)

            def turn(n, k):
                pe.wait_ge(h_ready, n + 1)
                pe.wait_ge(ht_saved, 2 * n + 1)
                for j in range(TS):
                    ins = pe.transpose(pT[j // 4][0:C + 1, 128 * (j % 4):128 * (j % 4) + 128], h[:, k % 2, j, :],
                                       ident[:, :])
                ins.then_inc(h_turned, 1)

            def logits(n, k):
                pe.wait_ge(ht_saved, 2 * n + 3)
                pe.wait_ge(gap_ready, n + 1)
                for j in range(TS):
                    ins = pe.matmul(pL[:, E * j:E * j + E], ht[:, k % 2, j, :], rw[:, :], start=True, stop=True)
                ins.then_inc(logits_ready, 1)

            def experts(n, k, half):
                for j in range(4 * half, 4 * half + 4):
                    pe.wait_ge(weighted, 8 * n + j + 1)
                    pe.matmul(pE[j % 4][:, :], ht[:, k % 2, j, :], ew[:, :, :].rearrange("d e c -> d (e c)"),
                              start=True, stop=True).then_inc(experts_ready, 1)

            def turn_out(n, k):
                pe.wait_ge(y_ready, n + 5)
                pe.wait_ge(yt_saved, n + 1)
                for q in range(4):
                    ins = pe.transpose(pY[:, 128 * q:128 * q + 128],
                                       y[:, k % 2, 2 * q:2 * q + 2, :].rearrange("w r c -> w (r c)"), ident[:, :])
                ins.then_inc(y_turned, 1)

            def tile(n, k, ahead=2, first=False):
                if ahead > 0:
                    turn(n + 1, k + 1)
                experts(n, k, 0)
                if ahead > 0:
                    logits(n + 1, k + 1)
                if image is not None and not first:
                    turn_out(n - 1, k - 1)
                experts(n, k, 1)

            turn(0, 0)
            logits(0, 0)
            over_late_tiles(pe, tile, image is not None and (lambda: turn_out(N - 1, N - 1)))


def stage_sweeps(nc, tok, kernels):
    TS = 8
    TILE = 128 * TS
    R, P2 = TILE // W, W // 2
    NT = S // TILE
    KW = 9
    PAD = 2
    EPS = 1e-6
    STEPS = H - 1
    BL = 8
    NB = W // BL
    with ExitStack() as ctx:
        a = Arena(nc, ctx, "sw")
        ident = a.sb("ident", [128, 128])
        eps = a.sb("eps", [128, 1])
        k_in = a.sb("k_in", [C, 2, KW, C])
        k_dup = a.sb("k_dup", [C, KW, 2, C])
        k_tap = a.sb("k_tap", [128, KW, C])
        wc = a.sb("wc", [128, 4, 5, 128])
        xs = a.sb("xs", [128, 2, TS, C])
        h = a.sb("h", [128, 2, TS, C])
        sq = a.sb("sq", [128, TS, C])
        st = a.sb("st", [128, 2, 2, TS])
        y = a.sb("y", [128, B, H, P2])
        row = [[a.sb(f"row{p}{c}", [128, 2, P2 + 2 * PAD]) for c in range(2)] for p in range(2)]
        packed = [[a.sb(f"packed{p}{c}", [128, 2, P2]) for c in range(2)] for p in range(2)]
        swap = a.sb("swap", [64, 2, 8, P2])
        xw = a.sb("xw", [128, 2, 2, 2, BL, C])
        pH = [a.ps(f"pH{i}", [128, 512]) for i in range(2)]
        pC = [a.ps(f"pC{i}", [128, 512]) for i in range(2)]
        pT = [a.ps(f"pT{i}", [128, 512]) for i in range(2)]
        pool_done = a.sem("pool_done")
        dve_done = a.sem("dve_done")
        const_ready = a.sem("const_ready")
        k_loaded = [a.sem(f"k_loaded{i}") for i in range(2)]
        k_doubled = a.sem("k_doubled")
        k_turned = a.sem("k_turned")
        k_ready = a.sem("k_ready")
        x_in = [a.sem(f"x_in{i}") for i in range(2)]
        centered = a.sem("centered")
        squared = a.sem("squared")
        var_ready = a.sem("var_ready")
        std_ready = a.sem("std_ready")
        h_ready = a.sem("h_ready")
        h_turned = a.sem("h_turned")
        u_saved = a.sem("u_saved")
        row_ready = [a.sem(f"row_ready{c}") for c in range(2)]
        conv_ready = [a.sem(f"conv_ready{c}") for c in range(2)]
        saved = [a.sem(f"saved{c}") for c in range(2)]
        taken = a.sem("taken")
        moved = a.sem("moved")
        put_back = a.sem("put_back")
        pack_ready = [a.sem(f"pack_ready{c}") for c in range(2)]
        turned = [a.sem(f"turned{c}") for c in range(2)]
        added = [a.sem(f"added{c}") for c in range(2)]
        w_loaded = [a.sem(f"w_loaded{i}") for i in range(2)]
        stored = [a.sem(f"stored{i}") for i in range(2)]
        block = ctx.enter_context(nc.Block())
        CHUNKS = B * H // 2 // 8

        def images(c):
            return slice(2 * c, 2 * c + 2)

        def line(sweep, c, i):
            if sweep < 2:
                return y[:, images(c), bass.ds(i, 1), :].rearrange("p b a w -> p b (a w)")
            v = y[:, images(c), :, bass.ds(i[0], 1)].rearrange("p b (h m) a -> p b m (h a)", m=2)
            return v[:, :, i[1], :]

        def over_steps(eng, sweep, body):
            g0 = sweep * STEPS
            par0 = FIRST[sweep]

            def at(t, k):
                if sweep == 1:
                    return t * -2 + (H - 1 - k)
                return 2 * t + k if sweep == 0 else (t + k // 2, k % 2)

            with eng.Fori(0, (STEPS - 1) // 2) as t:
                for k in (1, 2):
                    body(at(t, k), g0 + 2 * t + k, (par0 + k) % 2)
            body(at(STEPS // 2, 1), g0 + STEPS, (par0 + STEPS) % 2)

        FIRST = [0, 1, 0, 1]

        def block_rows(c, w0):
            v = tok[2 * c * S:(2 * c + 2) * S, :].rearrange("(q m w) c -> q m w c", m=2, w=W)
            return v[:, :, bass.ds(w0, BL), :]

        def exchange(n, half, odd):
            b, q = n // (CHUNKS // B), n % (CHUNKS // B)
            v = y[64 * half:64 * half + 64, bass.ds(b, 1), bass.ds(16 * q, 16), :]
            return v.rearrange("p a (r m) w -> p m (a r) w", m=2)[:, odd, :, :]

        def over_chunks(eng, body):
            with eng.Fori(0, CHUNKS // 2) as t:
                for k in range(2):
                    body(2 * t + k, k)

        def over_blocks(eng, body):
            body(0, 0, True)
            with eng.Fori(0, NB // 2 - 1) as t:
                for k in range(2):
                    body(2 * t + 1 + k, (1 + k) % 2, False)
            body(NB - 1, 1, False)

        @block.sync
        def _(sp):
            for k in range(2):
                sp.dma_start(k_in[:, k, :, :], kernels[k].rearrange("o a k i -> o (a k) i")).then_inc(k_loaded[k], 16)
            for k in range(2, 4):
                sp.wait_ge(k_doubled, k - 1)
                sp.dma_start(k_in[:, k % 2, :, :], kernels[k].rearrange("o a k i -> o (a k) i")).then_inc(k_loaded[k % 2], 16)
            with sp.Fori(0, NT) as t:
                for b in range(B):
                    sp.wait_ge(h_ready, B * t + b + 1)
                    sp.dma_start(xs[:, b % 2, :, :], tok[bass.ds(b * S + t * TILE, TILE), :].rearrange(
                        "(p j) c -> p j c", j=TS)).then_inc(x_in[b % 2], 16)

            def load(w0, buf):
                for c in range(2):
                    for m in range(2):
                        sp.dma_start(xw[:, buf, c, m, :, :], block_rows(c, w0)[:, m, :, :]).then_inc(w_loaded[buf], 16)

            def store(i, w0, buf):
                for c in range(2):
                    sp.wait_ge(added[c], BL * (i + 1) + 1)
                    for m in range(2):
                        sp.dma_start(block_rows(c, w0)[:, m, :, :], xw[:, buf, c, m, :, :]).then_inc(stored[buf], 16)

            load(W - BL, 0)
            load(W - 2 * BL, 1)
            with sp.Fori(0, NB // 2 - 1) as t:
                for buf in range(2):
                    w0 = t * (-2 * BL) + (W - BL * (1 + buf))
                    w2 = t * (-2 * BL) + (W - BL * (3 + buf))
                    store(2 * t + buf, w0, buf)
                    sp.wait_ge(stored[buf], 64 * (t + 1))
                    load(w2, buf)
            for buf in range(2):
                store(NB - 2 + buf, BL * (1 - buf), buf)
            for buf in range(2):
                sp.wait_ge(stored[buf], 64 * NB // 2)

        @block.gpsimd
        def _(pool):
            link = Link(pool, pool_done)
            for s in (var_ready, put_back, u_saved):
                pool.sem_inc(s, 1)
            for s in pack_ready:
                pool.sem_inc(s, 1)
            for s in added:
                pool.sem_inc(s, 1)
            pool.memset(eps[:, :], EPS)
            pool.memset(wc[:, :, :, :], 0.0)
            for p in range(2):
                for c in range(2):
                    pool.memset(row[p][c][:, :, :], 0.0)
            eye(pool, link, ident[:, :])
            pool.sem_inc(const_ready, 1)
            pool.sem_inc(h_ready, 2)

        @block.vector
        def _(dve):
            link = Link(dve, dve_done)
            dve.wait_ge(const_ready, 1)
            for s in range(4):
                dve.wait_ge(k_loaded[s % 2], 16 * (s // 2 + 1))
                if s > 0:
                    dve.wait_ge(k_turned, s)
                dve.tensor_copy(k_dup[:, :, 0, :], k_in[:, s % 2, :, :])
                dve.tensor_copy(k_dup[:, :, 1, :], k_in[:, s % 2, :, :]).then_inc(k_doubled, 1)
                dve.wait_ge(k_turned, s + 1)
                link(dve.tensor_copy(k_tap[:, 0:8, :].rearrange("p k o -> p (k o)"), pH[0][:, :]))
                link(dve.tensor_copy(k_tap[:, 8, :], pH[1][:, 0:C]))
                for m, pi, po, tap in parity_blocks(KW, KW // 2):
                    rows, cols = slice(64 * pi, 64 * pi + 64), slice(64 * po, 64 * po + 64)
                    ins = dve.tensor_copy(wc[rows, s, m + 2, cols], k_tap[rows, tap, :])
                ins.then_inc(k_ready, 1)
                dve.wait_ge(k_ready, s + 1)

            def center(t, n, b):
                par = b % 2
                dve.wait_ge(x_in[par], 16 * (2 * t + b // 2 + 1))
                s = st[:, par, 0, :]
                link(dve.tensor_reduce(s, xs[:, par, :, :], AX.X, ALU.add))
                link(dve.tensor_scalar(s, s, 1.0 / C, None, ALU.mult))
                dve.wait_ge(h_turned, n + 1)
                dve.tensor_tensor(h[:, par, :, :], xs[:, par, :, :], bcast(s, TS), ALU.subtract).then_inc(centered, 1)

            def scale(t, n, b):
                par = b % 2
                s = st[:, par, 1, :]
                dve.wait_ge(squared, n + 1)
                dve.tensor_reduce(s, sq[:, :, :], AX.X, ALU.add).then_inc(var_ready, 1)
                dve.wait_ge(std_ready, n + 1)
                link(dve.reciprocal(s, s))
                dve.tensor_tensor(h[:, par, :, :], h[:, par, :, :], bcast(s, TS), ALU.mult).then_inc(h_ready, 1)

            PER = 3 * B
            start = link.base + link.n
            with dve.Fori(0, NT) as t:
                link.base, link.n = start + t * PER, 0
                for b in range(B + 1):
                    if b < B:
                        center(t, B * t + b, b)
                    if b > 0:
                        scale(t, B * t + b - 1, b - 1)
                assert link.n == PER
            link.base, link.n = start + NT * PER, 0

            def make(sweep, c, i, g, par, r=None):
                dve.wait_ge(conv_ready[c], g)
                if r is None:
                    dve.wait_ge(saved[c], g)
                else:
                    dve.wait_ge(pack_ready[c], r)
                dve.scalar_tensor_tensor(row[par][c][:, :, PAD:PAD + P2],
                                         pC[c][:, 0:2 * P2].rearrange("p (b w) -> p b w", b=2), 0.0,
                                         line(sweep, c, i), ALU.max, ALU.add).then_inc(row_ready[c], 1)

            dve.wait_ge(u_saved, B * NT + 2)
            for sweep in range(3):
                if sweep != 1:
                    for c in range(2):
                        if sweep == 2:
                            dve.wait_ge(put_back, CHUNKS + 1)
                            dve.wait_ge(moved, CHUNKS)
                        dve.tensor_copy(row[0][c][:, :, PAD:PAD + P2], line(sweep, c, 0 if sweep == 0 else (0, 0))).then_inc(row_ready[c], 1)
                over_steps(dve, sweep, lambda i, g, par: [make(sweep, c, i, g, par) for c in range(2)])
                if sweep == 1:
                    for c in range(2):
                        dve.wait_ge(saved[c], 2 * STEPS + 2)
                    def move(n, k):
                        dve.wait_ge(taken, n + 1)
                        lo = exchange(n, 0, 1)
                        dve.tensor_copy(exchange(n, 1, 0), lo).then_inc(moved, 1)
                    over_chunks(dve, move)
            for c in range(2):
                dve.wait_ge(saved[c], 3 * STEPS + 2)

            def add(c, r, s, buf):
                dve.wait_ge(turned[c], r + 1)
                dve.tensor_tensor(xw[:, buf, c, :, BL - 1 - s, :], xw[:, buf, c, :, BL - 1 - s, :],
                                  pT[c][:, 0:128].rearrange("q (m c) -> q m c", m=2), ALU.add).then_inc(added[c], 1)

            def last(i, buf, first):
                pair0 = i * (-BL // 2) + (NB - 1) * (BL // 2)
                dve.wait_ge(w_loaded[buf], 64 * ((i - buf) // 2 + 1))
                for s in range(BL + 1):
                    if s < BL and not (first and s == 0):
                        for c in range(2):
                            make(3, c, (pair0 + (BL - 1 - s) // 2, (BL - 1 - s) % 2), 3 * STEPS + BL * i + s, (FIRST[3] + s) % 2, BL * i + s)
                    if s > 0:
                        for c in range(2):
                            add(c, BL * i + s - 1, s - 1, buf)

            over_blocks(dve, last)

        @block.scalar
        def _(act):
            act.wait_ge(const_ready, 1)

            def square(n, b):
                act.wait_ge(centered, n + 1)
                act.wait_ge(var_ready, n + 1)
                act.activation(sq[:, :, :], h[:, b % 2, :, :], ACT.Square).then_inc(squared, 1)

            def root(n, b):
                s = st[:, b % 2, 1, :]
                act.wait_ge(var_ready, n + 2)
                act.activation(s, s, ACT.Sqrt, bias=eps[:, 0:1], scale=1.0 / C).then_inc(std_ready, 1)

            def save(t, n, b):
                act.wait_ge(h_turned, n + 3)
                dst = y[:, b, bass.ds(t * R, R), :].rearrange("q r (a j) -> q j r a", j=TS // 2)
                act.activation(dst, pH[b % 2][:, :].rearrange("q (j r a) -> q j r a", j=TS // 2, r=R),
                               ACT.Copy).then_inc(u_saved, 1)

            with act.Fori(0, NT) as t:
                for b in range(B + 1):
                    if b < B:
                        square(B * t + b, b)
                        root(B * t + b, b)
                    if b > 0:
                        save(t, B * t + b - 1, b - 1)

            def save_row(sweep, c, i, g, par, firsts):
                act.wait_ge(row_ready[c], g + firsts)
                act.activation(line(sweep, c, i), row[par][c][:, :, PAD:PAD + P2], ACT.Copy).then_inc(saved[c], 1)

            for sweep in range(3):
                firsts = 2 if sweep == 2 else 1
                over_steps(act, sweep, lambda i, g, par: [save_row(sweep, c, i, g, par, firsts) for c in range(2)])
                if sweep == 1:
                    for c in range(2):
                        act.wait_ge(saved[c], 2 * STEPS + 2)
                    def take(n, k):
                        act.wait_ge(put_back, n + 1)
                        act.activation(swap[:, k, :, :], exchange(n, 1, 0), ACT.Copy).then_inc(taken, 1)
                        act.wait_ge(moved, n + 1)
                        act.activation(exchange(n, 0, 1), swap[:, k, :, :], ACT.Copy).then_inc(put_back, 1)
                    over_chunks(act, take)

            def pack(i, buf, first):
                for s in range(BL):
                    r, par = BL * i + s, (FIRST[3] + s) % 2
                    for c in range(2):
                        act.wait_ge(row_ready[c], 3 * STEPS + 2 + r)
                        if not (first and s < 2):
                            act.wait_ge(turned[c], r - 1)
                        act.activation(packed[par][c][:, :, :], row[par][c][:, :, PAD:PAD + P2],
                                       ACT.Copy).then_inc(pack_ready[c], 1)

            over_blocks(act, pack)

        @block.tensor
        def _(pe):
            pe.wait_ge(const_ready, 1)
            for s in range(4):
                pe.wait_ge(k_doubled, s + 1)
                if s > 0:
                    pe.wait_ge(k_ready, s)
                for k in range(KW):
                    ins = pe.transpose(pH[k // 8][:, C * (k % 8):C * (k % 8) + C],
                                       k_dup[:, k, :, :].rearrange("o d i -> o (d i)"), ident[0:C, 0:C])
                ins.then_inc(k_turned, 1)
            pe.wait_ge(k_ready, 4)
            pe.sem_inc(h_turned, 2)
            pe.sem_inc(u_saved, 1)
            for c in range(2):
                pe.sem_inc(saved[c], 2)

            def turn(n, b):
                pe.wait_ge(h_ready, n + 3)
                pe.wait_ge(u_saved, n + 1)
                for j in range(TS // 2):
                    ins = pe.transpose(pH[b % 2][:, 128 * j:128 * j + 128],
                                       h[:, b % 2, 2 * j:2 * j + 2, :].rearrange("p j c -> p (j c)"), ident[:, :])
                ins.then_inc(h_turned, 1)

            with pe.Fori(0, NT) as t:
                for b in range(B):
                    turn(B * t + b, b)

            def conv(sweep, c, g, par, firsts):
                pe.wait_ge(row_ready[c], g - 1 + firsts)
                for m in range(5):
                    ins = pe.matmul(pC[c][:, 0:2 * P2], wc[:, sweep, m, :], row[1 - par][c][:, :, m:m + P2],
                                    start=(m == 0), stop=(m == 4))
                ins.then_inc(conv_ready[c], 1)

            for sweep in range(3):
                firsts = 2 if sweep == 2 else 1
                over_steps(pe, sweep, lambda i, g, par: [conv(sweep, c, g, par, firsts) for c in range(2)])

            def turn_out(c, r, par):
                pe.wait_ge(pack_ready[c], r + 2)
                pe.wait_ge(added[c], r + 1)
                pe.transpose(pT[c][:, 0:128], packed[par][c][:, :, :].rearrange("p b h -> p (b h)"),
                             ident[:, :]).then_inc(turned[c], 1)

            def last(i, buf, first):
                for s in range(BL + 1):
                    if s < BL and not (first and s == 0):
                        for c in range(2):
                            conv(3, c, 3 * STEPS + BL * i + s, (FIRST[3] + s) % 2, 2)
                    if s > 0:
                        for c in range(2):
                            turn_out(c, BL * i + s - 1, (FIRST[3] + s - 1) % 2)

            over_blocks(pe, last)


def stage_spread(nc, tok, w_d, w_dirs, bns):
    IT = 4
    NC = 4
    TS = 8
    NT = W // TS
    EPS_LN, EPS_BN = 1e-6, 1e-3
    SHIFTS = [H // 2 ** (IT - i) for i in range(IT)]
    UP = [(2, -s, 0) for s in SHIFTS]
    RIGHT = [(4, 0, s) for s in SHIFTS]
    LEFT = [(8, 0, -s) for s in SHIFTS]
    CONVS = UP + RIGHT + LEFT
    NP = 9 * len(CONVS) + 8 * IT
    SC, BI = 9 * len(CONVS), 9 * len(CONVS) + 4 * IT
    with ExitStack() as ctx:
        a = Arena(nc, ctx, "sp")
        eps = a.sb("eps", [128, 2])
        y = a.sb("y", [128, C, B, W])
        par = a.sb("par", [128, C, NP])
        roll = a.sb("roll", [128, IT, 128])
        diag = a.sb("diag", [128, IT + 2, 3, 128])
        cur = a.sb("cur", [128, NC, NP])
        work = a.sb("work", [128, 7168])
        st = a.sb("st", [128, 2, 2, TS])
        xs = work[:, 0:1536].rearrange("p (n t c) -> p n t c", n=3, t=TS)
        h = work[:, 2048:3072].rearrange("p (n t c) -> p n t c", n=2, t=TS)
        sq = work[:, 3072:3584].rearrange("p (t c) -> p t c", t=TS)
        x = work[:, 0:2048].rearrange("p (q n) -> p q n", q=NC)
        rel = work[:, 2048:4096].rearrange("p (q n) -> p q n", q=NC)
        band = work[:, 4096:7168].rearrange("p (q n k m) -> p q n k m", q=NC, n=2, k=3)
        raw = y[:, :, :, :].rearrange("p c b w -> p (c b w)")
        NW9 = IT * C * 9
        raw_w = [raw[:, NW9 * d:NW9 * (d + 1)] for d in range(3)]
        raw_bn = raw[:, 3 * NW9:3 * NW9 + 4 * IT * 4 * C].rearrange("p (d i k c) -> p d i k c", d=4, i=IT, k=4)
        raw_d = raw[:, 3 * NW9 + 16 * IT * C:3 * NW9 + 17 * IT * C].rearrange("p (i c) -> p i c", i=IT)
        pC = [a.ps(f"pC{i}", [128, 512]) for i in range(NC)]
        pool_done = a.sem("pool_done")
        dve_done = a.sem("dve_done")
        const_ready = a.sem("const_ready")
        p_in = a.sem("p_in")
        bn_var = a.sem("bn_var")
        bn_std = a.sem("bn_std")
        par_ready = a.sem("par_ready")
        x_in = [a.sem(f"x_in{i}") for i in range(2)]
        centered = a.sem("centered")
        squared = a.sem("squared")
        var_ready = a.sem("var_ready")
        std_ready = a.sem("std_ready")
        y_ready = a.sem("y_ready")
        cur_ready = a.sem("cur_ready")
        band_ready = [a.sem(f"band_ready{i}") for i in range(NC)]
        x_ready = [a.sem(f"x_ready{i}") for i in range(NC)]
        conv_ready = [a.sem(f"conv_ready{i}") for i in range(NC)]
        relu_ready = [a.sem(f"relu_ready{i}") for i in range(NC)]
        r_in = [a.sem(f"r_in{i}") for i in range(2)]
        sum_ready = a.sem("sum_ready")
        stored = [a.sem(f"stored{i}") for i in range(2)]
        block = ctx.enter_context(nc.Block())
        ITS = 4 * IT
        GROUPS = C // NC

        def tokens(n):
            v = tok[bass.ds(n // NT * S, S), :].rearrange("(h w) c -> h w c", h=H)
            return v[:, bass.ds(n % NT * TS, TS), :].rearrange("h t c -> h (t c)")

        def columns(n, b, t):
            v = y[:, :, bass.ds(b, 1), bass.ds(TS * t, TS)]
            return v.rearrange("p c a w -> p (a w) c")

        def channel(g, q):
            return y[:, bass.ds(NC * g + q, 1), :, :].rearrange("p a b w -> p (a b w)")

        def over_tiles(eng, body, link=None, per=0):
            start = (link.base + link.n) if link else 0
            with eng.Fori(0, B) as b:
                with eng.Fori(0, NT // 2) as t:
                    for k in range(2):
                        n = NT * b + 2 * t + k
                        if link:
                            link.base, link.n = start + n * per, 0
                        body(n, b, 2 * t + k, k)
                        assert not link or link.n == per, link.n
            if link:
                link.base, link.n = start + B * NT * per, 0

        def spans(dil, kw, roll_w):
            d, s = dil * (kw - 1), roll_w % W
            lo, hi, cut = max(0, -d), min(W, W - d), W - d - s
            return [(p, q, (p + d + s) % W) for p, q in ((lo, min(hi, cut)), (max(lo, cut), hi)) if p < q]

        @block.sync
        def _(sp):
            for d in range(3):
                sp.dma_start(raw_w[d], w_dirs[d].rearrange("i c a k m -> (i c a k m)").partition_broadcast(128)).then_inc(p_in, 16)
            for d in range(4):
                sp.dma_start(raw_bn[:, d, :, :, :].rearrange("p i k c -> p (i k c)"),
                             bns[d].rearrange("i k c -> (i k c)").partition_broadcast(128)).then_inc(p_in, 16)
            sp.dma_start(raw_d[:, :, :].rearrange("p i c -> p (i c)"),
                         w_d.rearrange("i c a k m -> (i c a k m)").partition_broadcast(128)).then_inc(p_in, 16)

            def load(n, b, t, k):
                sp.wait_ge(centered, n + 1)
                sp.dma_start(xs[:, k, :, :].rearrange("p t c -> p (t c)"), tokens(n)).then_inc(x_in[k], 16)

            over_tiles(sp, load)
            for q in range(NC):
                sp.wait_ge(x_ready[q], 17 * GROUPS + 1)

            def load_rest(n, k):
                sp.wait_ge(sum_ready, n + 1)
                sp.dma_start(xs[:, k, :, :].rearrange("p t c -> p (t c)"), tokens(n)).then_inc(r_in[k], 16)

            def store(n, k):
                sp.wait_ge(sum_ready, n + 3)
                sp.dma_start(tokens(n), h[:, k, :, :].rearrange("p t c -> p (t c)")).then_inc(stored[k], 16)

            load_rest(0, 0)
            with sp.Fori(0, B * NT // 2 - 1) as t:
                for k in range(2):
                    load_rest(2 * t + k + 1, 1 - k)
                    store(2 * t + k, k)
            load_rest(B * NT - 1, 1)
            for k in range(2):
                store(B * NT - 2 + k, k)
            for k in range(2):
                sp.wait_ge(stored[k], 16 * B * NT // 2 + 16)

        @block.gpsimd
        def _(pool):
            link = Link(pool, pool_done)
            for s in relu_ready:
                pool.sem_inc(s, 1)
            for s in stored:
                pool.sem_inc(s, 16)
            for s in x_ready:
                pool.sem_inc(s, 1)
            pool.memset(eps[:, 0:1], EPS_LN)
            pool.memset(eps[:, 1:2], EPS_BN)
            link(pool.memset(roll[:, :, :], 0.0))
            link(pool.memset(diag[:, :, :, :], 0.0))

            def set_diagonal(m, c0, c1, k):
                link(pool.affine_select(out=m[:, c0:c1], in_=m[:, c0:c1], compare_op=ALU.not_equal, fill=1.0,
                                        base=-c0 - k, pattern=[[-1, c1 - c0]], channel_multiplier=1))

            for i, s in enumerate(SHIFTS):
                for k in (s, s - H):
                    set_diagonal(roll[:, i, :], 0, H, k)
            for i, (dil, s) in enumerate([(d, s) for d, s, _ in UP] + [(RIGHT[0][0], 0), (LEFT[0][0], 0)]):
                for kh in range(3):
                    e = dil * (kh - 1)
                    for k in {e + s, e + s + H if s else e}:
                        set_diagonal(diag[:, i, kh, :], max(0, -e), min(H, H - e), k)
            pool.sem_inc(const_ready, 1)
            pool.sem_inc(centered, 2)
            pool.sem_inc(sum_ready, 2)
            with pool.Fori(0, GROUPS) as g:
                for i in range(ITS):
                    for q in range(NC):
                        pool.wait_ge(relu_ready[q], ITS * g + i + 2)
                        out = x[:, q, :] if i < ITS - 1 else channel(g, q)
                        pool.tensor_tensor(out, x[:, q, :], rel[:, q, :], ALU.add).then_inc(x_ready[q], 1)

        @block.vector
        def _(dve):
            link = Link(dve, dve_done)
            dve.wait_ge(p_in, 16 * 8)
            taps = par[:, :, 0:SC].rearrange("p c (d i k) -> p d i c k", d=3, i=IT)
            for d in range(3):
                w = raw_w[d].rearrange("p (i c k) -> p i c k", i=IT, c=C)
                for i in range(IT):
                    dve.tensor_copy(taps[:, d, i, :, :], w[:, i, :, :])
            scale_v = par[:, :, SC:BI].rearrange("p c (d i) -> p d i c", d=4)
            bias_v = par[:, :, BI:NP].rearrange("p c (d i) -> p d i c", d=4)
            gam, bet, mean, var = (raw_bn[:, :, :, k, :] for k in range(4))
            dve.wait_ge(bn_std, 1)
            link(dve.reciprocal(var, var))
            link(dve.tensor_tensor(gam, gam, var, ALU.mult))
            link(dve.tensor_tensor(mean, mean, gam, ALU.mult))
            link(dve.tensor_tensor(bet, bet, mean, ALU.subtract))
            link(dve.tensor_scalar(bias_v, bet, 2.0, None, ALU.mult))
            link(dve.tensor_scalar(scale_v, gam, 2.0, None, ALU.mult))
            link(dve.tensor_tensor(scale_v[:, 0, :, :], scale_v[:, 0, :, :], raw_d, ALU.mult))

            def normalise(n, b, t, k):
                xt, s = xs[:, k, :, :], st[:, k, :, :]
                dve.wait_ge(x_in[k], 16 * ((n - k) // 2 + 1))
                link(dve.tensor_reduce(s[:, 0, :], xt, AX.X, ALU.add))
                link(dve.tensor_scalar(s[:, 0, :], s[:, 0, :], 1.0 / C, None, ALU.mult))
                dve.tensor_tensor(h[:, k, :, :], xt, bcast(s[:, 0, :], TS), ALU.subtract).then_inc(centered, 1)
                dve.wait_ge(squared, n + 1)
                dve.tensor_reduce(s[:, 1, :], sq, AX.X, ALU.add).then_inc(var_ready, 1)
                dve.wait_ge(std_ready, n + 1)
                link(dve.reciprocal(s[:, 1, :], s[:, 1, :]))
                dve.tensor_tensor(columns(n, b, t), h[:, k, :, :], bcast(s[:, 1, :], TS), ALU.mult).then_inc(y_ready, 1)

            over_tiles(dve, normalise, link, 3)
            dve.wait_ge(y_ready, B * NT)

            def build(q, i, g):
                conv = i - IT
                d, n = (conv if conv < IT else IT + (conv - IT) // IT), i % 2
                dve.wait_ge(conv_ready[q], ITS * g + i - 1)
                for kw in range(3):
                    m = band[:, q, n, kw, :]
                    w = [cur[:, q, 9 * conv + 3 * kh + kw:9 * conv + 3 * kh + kw + 1] for kh in range(3)]
                    link(dve.tensor_scalar(m, diag[:, d, 0, :], w[0], None, ALU.mult))
                    link(dve.scalar_tensor_tensor(m, diag[:, d, 1, :], w[1], m, ALU.mult, ALU.add))
                    ins = dve.scalar_tensor_tensor(m, diag[:, d, 2, :], w[2], m, ALU.mult, ALU.add)
                ins.then_inc(band_ready[q], 1)

            PER = 6 * NC * 3 * IT
            start = link.base + link.n
            with dve.Fori(0, GROUPS) as g:
                link.base, link.n = start + g * PER, 0
                for q in range(NC):
                    dve.wait_ge(relu_ready[q], ITS * g + 1)
                    dve.tensor_copy(cur[:, q, :], par[:, bass.ds(NC * g + q, 1), :].rearrange(
                        "p a n -> p (a n)")).then_inc(cur_ready, 1)
                dve.wait_ge(cur_ready, NC * g + NC)
                for i in range(IT, ITS):
                    for q in range(NC):
                        build(q, i, g)
                assert link.n == PER
            link.base, link.n = start + GROUPS * PER, 0

            def add_rest(n, b, t, k):
                dve.wait_ge(r_in[k], 16 * ((n - k) // 2 + 1))
                dve.wait_ge(stored[k], 8 * (n - k) + 16)
                dve.tensor_tensor(h[:, k, :, :], columns(n, b, t), xs[:, k, :, :], ALU.add).then_inc(sum_ready, 1)

            over_tiles(dve, add_rest)

        @block.scalar
        def _(act):
            act.wait_ge(const_ready, 1)
            act.wait_ge(p_in, 16 * 8)
            var = raw_bn[:, :, :, 3, :]
            act.activation(var, var, ACT.Sqrt, bias=eps[:, 1:2]).then_inc(bn_std, 1)

            def spread(n, b, t, k):
                act.wait_ge(centered, n + 3)
                act.activation(sq, h[:, k, :, :], ACT.Square).then_inc(squared, 1)
                act.wait_ge(var_ready, n + 1)
                s = st[:, k, 1, :]
                act.activation(s, s, ACT.Sqrt, bias=eps[:, 0:1], scale=1.0 / C).then_inc(std_ready, 1)

            over_tiles(act, spread)
            act.wait_ge(y_ready, B * NT)
            with act.Fori(0, GROUPS) as g:
                for q in range(NC):
                    act.wait_ge(x_ready[q], 17 * g + 1)
                    act.activation(x[:, q, :], channel(g, q), ACT.Copy).then_inc(x_ready[q], 1)
                act.wait_ge(cur_ready, NC * g + NC)
                for i in range(ITS):
                    for q in range(NC):
                        act.wait_ge(conv_ready[q], ITS * g + i + 1)
                        act.activation(rel[:, q, :], pC[q][:, :], ACT.Relu, bias=cur[:, q, BI + i:BI + i + 1],
                                       scale=cur[:, q, SC + i:SC + i + 1]).then_inc(relu_ready[q], 1)

        @block.tensor
        def _(pe):
            pe.wait_ge(const_ready, 1)
            with pe.Fori(0, GROUPS) as g:
                for i in range(ITS):
                    for q in range(NC):
                        pe.wait_ge(x_ready[q], 17 * g + i + 2)
                        if i < IT:
                            pe.matmul(pC[q][:, :], roll[:, i, :], x[:, q, :], start=True,
                                      stop=True).then_inc(conv_ready[q], 1)
                            continue
                        pe.wait_ge(band_ready[q], 3 * IT * g + i - IT + 1)
                        dil, _, s = CONVS[i - IT]
                        xq = x[:, q, :].rearrange("p (b w) -> p b w", b=B)
                        out = pC[q][:, :].rearrange("p (b w) -> p b w", b=B)
                        jobs = [(kw, *piece) for kw in (1, 0, 2) for piece in spans(dil, kw, s)]
                        for n, (kw, lo, hi, at) in enumerate(jobs):
                            ins = pe.matmul(out[:, :, lo:hi], band[:, q, i % 2, kw, :], xq[:, :, at:at + hi - lo],
                                            start=(n == 0), stop=(n == len(jobs) - 1), skip_group_check=True)
                        ins.then_inc(conv_ready[q], 1)


def build_program(nc, p, out):
    PICKS = 4 * 32 * 8
    tok = nc.dram_tensor("tokens", (B * S + PICKS, C), FP32, kind="Internal").ap()
    stage_window_attention(nc, p["x"], p["L0_conv_qkv_w"], p["L0_conv_proj_w"], p["L0_conv_proj_b"],
                           p["L0_conv_bias_table"], tok)
    stage_choice_ffn(nc, "c0", tok, *(p["L0_ffn_" + n] for n in ("gate_w", "gate_b", "weight1", "weight2")))
    stage_conv_bn(nc, tok, *(p["L1_conv_" + n] for n in ("gamma", "beta", "w_lbp", "w_1x1", "b_1x1")))
    stage_top2_ffn(nc, "t1", tok, *(p["L1_ffn_" + n] for n in ("router_w", "router_b", "expert_w", "expert_b")))
    stage_sweeps(nc, tok, [p["L2_conv_kernel_" + n] for n in ("td", "dt", "lr", "rl")])
    stage_choice_ffn(nc, "c2", tok, *(p["L2_ffn_" + n] for n in ("gate_w", "gate_b", "weight1", "weight2")))
    stage_spread(nc, tok, p["L3_conv_w_d"], [p["L3_conv_w_" + n] for n in "url"],
                 [p["L3_conv_bn_" + n] for n in "durl"])
    stage_top2_ffn(nc, "t3", tok, *(p["L3_ffn_" + n] for n in ("router_w", "router_b", "expert_w", "expert_b")),
                   image=out)


def kernel(**inputs):
    import numpy as _np
    import concourse.bacc as _bacc
    from concourse import mybir as _mybir
    from concourse.bass_utils import run_bass_kernel_spmd as _run

    nc = _bacc.Bacc("TRN2", target_bir_lowering=False, num_devices=1)
    arrays, params = {}, {}
    for name, value in inputs.items():
        a = _np.ascontiguousarray(value)
        arrays[f"in_{name}"] = a
        params[name] = nc.dram_tensor(f"in_{name}", a.shape, _mybir.dt.from_np(a.dtype), kind="ExternalInput").ap()
    out = nc.dram_tensor("out", (B, C, H, W), _mybir.dt.float32, kind="ExternalOutput").ap()
    build_program(nc, params, out)
    r = _run(nc, [arrays], core_ids=[0])
    return r.results[0]["out"]
```

```python
import numpy as np
import concourse.bass as bass
from concourse import mybir
from contextlib import ExitStack

FP32 = mybir.dt.float32
ALU = mybir.AluOpType
ACT = mybir.ActivationFunctionType
AX = mybir.AxisListType
B, C, H, W = 4, 64, 128, 128
S = H * W


class Link:

    def __init__(self, eng, sem):
        self.eng, self.sem, self.base, self.n = eng, sem, 0, 0

    def __call__(self, ins):
        ins.then_inc(self.sem, 1)
        self.n += 1
        self.eng.wait_ge(self.sem, self.base + self.n)

    def mark(self, ins):
        ins.then_inc(self.sem, 1)
        self.n += 1
        return self.n

    def until(self, n):
        self.eng.wait_ge(self.sem, self.base + n)


class Arena:

    def __init__(self, nc, ctx, stage):
        self.nc, self.ctx, self.stage, self.sems = nc, ctx, stage, []
        ctx.callback(self.clear)

    def clear(self):
        self.nc.clear_and_free_semaphores(self.sems)
        self.nc.all_engine_barrier()

    def sb(self, name, shape, dt=FP32):
        return self.ctx.enter_context(self.nc.sbuf_tensor(f"{self.stage}_{name}", shape, dt))

    def ps(self, name, shape, dt=FP32):
        return self.ctx.enter_context(self.nc.psum_tensor(f"{self.stage}_{name}", shape, dt))

    def sem(self, name):
        self.sems.append(self.nc.alloc_semaphore(name=f"{self.stage}_{name}"))
        return self.sems[-1]


def eye(pool, link, m):
    link(pool.memset(m, 0.0))
    link(pool.affine_select(out=m, in_=m, compare_op=ALU.not_equal, fill=1.0, base=0,
                            pattern=[[-1, 128]], channel_multiplier=1))


def bcast(v, n, m=C):
    return v.unsqueeze(2).to_broadcast([128, n, m])


def pipelined(eng, tiles, stages):
    def step(v):
        for f, d in stages:
            if 0 <= v + d < B * tiles:
                f((v + d) // B, (v + d) % B, v + d)

    for v in range(-max(d for _, d in stages), B):
        step(v)
    with eng.Fori(1, tiles - 1) as t:
        for k in range(B):
            for f, d in stages:
                f(t + (k + d) // B, (k + d) % B, B * t + k + d)
    for v in range(B * (tiles - 1), B * tiles - min(d for _, d in stages)):
        step(v)


def parity_blocks(taps, first):
    for m in range(-2, 3):
        for pi in range(2):
            for po in range(2):
                tap = 2 * m + pi - po + first
                if 0 <= tap < taps:
                    yield m, pi, po, tap


def stage_window_attention(nc, x, qkv_w, proj_w, proj_b, bias_table, tok):
    WS, NH, SHIFT = 8, 4, 4
    STEP = 4
    NSTEP = W // WS // STEP
    T = STEP * WS * WS
    STRIPS = H // WS
    NX = 4
    SCALE = float(C // NH) ** -0.5
    EPS = 1e-6
    with ExitStack() as ctx:
        a = Arena(nc, ctx, "wa")
        ident = a.sb("ident", [128, 128])
        mean_w = a.sb("mean_w", [128, 128])
        w_rows = a.sb("w_rows", [128, 4, 128])
        w_cols = a.sb("w_cols", [128, 4, 128])
        pb = a.sb("pb", [128, 1])
        eps = a.sb("eps", [128, 1])
        iota_q = a.sb("iota_q", [128, 1], mybir.dt.int32)
        iota_k = a.sb("iota_k", [128, 64], mybir.dt.int32)
        bits_q = a.sb("bits_q", [128, 4], mybir.dt.int32)
        bits_k = a.sb("bits_k", [128, 2, 64], mybir.dt.int32)
        bits_qf = a.sb("bits_qf", [128, 4])
        bits_kf = a.sb("bits_kf", [128, 2, 64])
        gmask = a.sb("gmask", [128, 2])
        hmask = a.sb("hmask", [128, NH])
        half_mask = a.sb("half_mask", [128, 2, 16])
        table = a.sb("table", [128, 64, NH])
        bias = a.sb("bias", [128, 2, 2, NH, 64])
        cut = a.sb("cut", [128, 3, 64])
        xs = a.sb("xs", [128, NX, 8, 128])
        xc = a.sb("xc", [128, 8, 128])
        sq = a.sb("sq", [128, 8, 128])
        h = a.sb("h", [128, 2, W // WS, 2, WS, WS])
        qs = a.sb("qs", [128, STEP, 2, 64])
        ks = a.sb("ks", [128, NH, T])
        vs = a.sb("vs", [128, NSTEP, STEP, 128])
        sc = a.sb("sc", [128, 2, STEP, NH, 64])
        mx = a.sb("mx", [128, STEP, NH])
        sm = a.sb("sm", [128, 2, 2, STEP, NH])
        pt = a.sb("pt", [128, STEP, 2, 128])
        ov = a.sb("ov", [128, T])
        yr = a.sb("yr", [128, 2, WS, W])
        x1 = a.sb("x1", [128, WS, W])
        xt = a.sb("xt", [128, 2, WS, 128])
        pL = a.ps("pL", [128, 512])
        pQK = a.ps("pQK", [128, 2, T])
        pV = a.ps("pV", [128, STEP, 128])
        pS = a.ps("pS", [128, STEP, NH, 64])
        pT = a.ps("pT", [128, STEP, 2, 128])
        pO = a.ps("pO", [128, 2, T])
        const_in = a.sem("const_in")
        pool_done = a.sem("pool_done")
        dve_done = a.sem("dve_done")
        const_ready = a.sem("const_ready")
        zeros_ready = a.sem("zeros_ready")
        w_turned = a.sem("w_turned")
        w_ready = a.sem("w_ready")
        x_in = [a.sem(f"x_in{i}") for i in range(NX)]
        mean_ready = a.sem("mean_ready")
        centered = a.sem("centered")
        squared = a.sem("squared")
        var_ready = a.sem("var_ready")
        log_ready = a.sem("log_ready")
        rstd_ready = a.sem("rstd_ready")
        h_ready = a.sem("h_ready")
        h_doubled = a.sem("h_doubled")
        qkv_ready = a.sem("qkv_ready")
        qk_saved = a.sem("qk_saved")
        v_saved = a.sem("v_saved")
        scores_ready = a.sem("scores_ready")
        bias_ready = a.sem("bias_ready")
        scores_read = a.sem("scores_read")
        max_ready = a.sem("max_ready")
        shifted = a.sem("shifted")
        exp_ready = a.sem("exp_ready")
        row_sums = a.sem("row_sums")
        sum_ready = a.sem("sum_ready")
        probs_ready = a.sem("probs_ready")
        probs_turned = a.sem("probs_turned")
        pt_saved = a.sem("pt_saved")
        pv_ready = a.sem("pv_ready")
        ov_saved = a.sem("ov_saved")
        proj_ready = a.sem("proj_ready")
        yr_ready = a.sem("yr_ready")
        x1_ready = a.sem("x1_ready")
        x1_turned = a.sem("x1_turned")
        xt_saved = a.sem("xt_saved")
        stored = [a.sem(f"stored{i}") for i in range(2)]
        block = ctx.enter_context(nc.Block())

        N_CONST = 8 + 2 + 16

        def over_strips(eng, begin, strip, end):
            with eng.Fori(0, 2) as bp:
                n0 = bp * STRIPS
                begin(bp, n0)
                strip(bp, 0, n0, 0, True, False)
                with eng.Fori(0, STRIPS // NX - 1) as t:
                    for k in range(1, NX + 1):
                        strip(bp, NX * t + k, bp * STRIPS + NX * t + k, k % NX, False, False)
                for i in range(STRIPS - NX + 1, STRIPS):
                    strip(bp, i, bp * STRIPS + i, i % NX, False, i == STRIPS - 1)
                end(bp, bp * STRIPS + STRIPS)

        def normalised(eng, par, copy):
            for w0, w1, c0, c1, col in ((0, 15, 0, WS, SHIFT), (15, 16, 0, 4, W - 4), (15, 16, 4, 8, 0)):
                def part(t):
                    return t[:, :, col:col + (w1 - w0) * (c1 - c0)].rearrange("p r (w c) -> p w r c", c=c1 - c0)
                ins = eng.tensor_tensor(h[:, par, w0:w1, copy, :, c0:c1], part(xc), part(sq), ALU.mult)
            return ins

        def steps(n, k, first, last, body):
            for j in range(NSTEP):
                s = NSTEP * n + j
                def at(d):
                    up = (j + d) // NSTEP
                    return s + d, (j + d) % NSTEP, n + up, (k + up) % 2
                body(s, j, None if last and j == NSTEP - 1 else at(1),
                     None if first and j < 1 else at(-1), None if first and j < 2 else at(-2))

        @block.sync
        def _(sp):
            sp.wait_ge(zeros_ready, 1)
            for g in range(2):
                part = slice(64 * g, 64 * g + 64)
                for m in range(4):
                    w = proj_w if m == 3 else qkv_w[64 * m:64 * m + 64, :]
                    sp.dma_start(w_rows[part, m, part], w).then_inc(const_in, 16)
                sp.dma_start(pb[part, :], proj_b.rearrange("(c a) -> c a", a=1)).then_inc(const_in, 16)
                for qr in range(WS):
                    src = bass.AP(bias_table.tensor, qr * 15 * NH, [[NH, 8], [15 * NH, 8], [1, 8 * NH]])
                    sp.dma_start(table[64 * g + 8 * qr:64 * g + 8 * qr + 8, :, :].rearrange(
                        "p (i j) h -> p i (j h)", i=8), src).then_inc(const_in, 16)

            def halves(i):
                return [(WS * i + SHIFT + 4 * half) % H if isinstance(i, int) else WS * i + SHIFT + 4 * half
                        for half in range(2)]

            def load(bp, i, n, k):
                sp.wait_ge(x1_ready, n + 1)
                for half, r in enumerate(halves(i)):
                    src = x[bass.ds(2 * bp, 2), :, bass.ds(r, 4), :].rearrange("g c h w -> (g c) h w")
                    sp.dma_start(xs[:, k, 4 * half:4 * half + 4, :], src).then_inc(x_in[k], 16)

            def store(bp, i, n, par):
                sp.wait_ge(xt_saved, 2 * n + 4)
                for half, r in enumerate(halves(i)):
                    for g in range(2):
                        rows = tok[bass.ds((2 * bp + g) * S + r * W, 4 * W), :]
                        sp.dma_start(rows.rearrange("(r w) c -> w r c", r=4),
                                     xt[:, par, 4 * half:4 * half + 4, 64 * g:64 * g + 64]).then_inc(stored[par], 16)

            with sp.Fori(0, 2) as bp:
                for i in range(NX):
                    load(bp, i, bp * STRIPS + i, i)
                with sp.Fori(1, STRIPS // NX - 1) as t:
                    for k in range(NX):
                        load(bp, NX * t + k, bp * STRIPS + NX * t + k, k)
                        store(bp, NX * t + (k - NX), bp * STRIPS + NX * t + (k - NX), k % 2)
                for i in range(STRIPS - NX, STRIPS):
                    load(bp, i, bp * STRIPS + i, i % NX)
                    store(bp, i - NX, bp * STRIPS + (i - NX), i % 2)
                for i in range(STRIPS - NX, STRIPS):
                    store(bp, i, bp * STRIPS + i, i % 2)
            for par in range(2):
                sp.wait_ge(stored[par], 64 * STRIPS + 16)

        @block.gpsimd
        def _(pool):
            link = Link(pool, pool_done)
            for s, k in ((x1_turned, 1), (yr_ready, 1), (qkv_ready, 1), (scores_ready, 1), (v_saved, 1), (pt_saved, 1),
                         (proj_ready, 1), (scores_read, 1), (h_doubled, 1), (probs_turned, 2), (xt_saved, 2),
                         (pv_ready, NSTEP), (x1_ready, NX), (stored[0], 16), (stored[1], 16)):
                pool.sem_inc(s, k)
            pool.memset(w_rows[:, :, :], 0.0).then_inc(zeros_ready, 1)
            pool.memset(eps[:, :], EPS)
            link(pool.memset(mean_w[:, :], 0.0))
            for g in range(2):
                link(pool.memset(mean_w[64 * g:64 * g + 64, 64 * g:64 * g + 64], 1.0 / C))
            eye(pool, link, ident[:, :])
            link(pool.iota(iota_q[:, :], pattern=[[0, 1]], base=0, channel_multiplier=1))
            pool.iota(iota_k[:, :], pattern=[[1, 64]], base=0, channel_multiplier=0).then_inc(const_ready, 1)

            def normalise(u, j):
                pool.wait_ge(sum_ready, u + 1)
                p = sc[:, j % 2, :, :, :]
                r = sm[:, j % 2, 1, :, :].unsqueeze(3).to_broadcast([128, STEP, NH, 64])
                pool.tensor_tensor(p, p, r, ALU.mult).then_inc(probs_ready, 1)

            def write_h(m, par, done):
                pool.wait_ge(rstd_ready, m + 1)
                pool.wait_ge(qkv_ready, done + 1)
                normalised(pool, par, 1).then_inc(h_doubled, 1)

            def residual(q, k):
                pool.wait_ge(yr_ready, NSTEP * q + NSTEP + 1)
                pool.wait_ge(x1_turned, 2 * q + 1)
                o, p = x1[:, :, :], yr[:, k % 2, :, :]
                pool.tensor_tensor(o[:, :, SHIFT:W], xs[:, k, :, SHIFT:W], p[:, :, 0:W - SHIFT], ALU.add)
                pool.tensor_tensor(o[:, :, 0:SHIFT], xs[:, k, :, 0:SHIFT], p[:, :, W - SHIFT:W],
                                   ALU.add).then_inc(x1_ready, 1)

            def begin(bp, n):
                write_h(n, 0, NSTEP * n)

            def strip(bp, i, n, k, first, last):
                def body(s, j, after, back1, back2):
                    if back1:
                        normalise(*back1[0:2])
                    if j == 2 and not last:
                        write_h(n + 1, (k + 1) % 2, NSTEP * n)
                    if j == 2 and not first:
                        residual(n - 1, (k - 1) % NX)
                steps(n, k, first, last, body)

            def end(bp, n):
                normalise(NSTEP * n - 1, NSTEP - 1)
                residual(n - 1, NX - 1)

            over_strips(pool, begin, strip, end)

        @block.vector
        def _(dve):
            link = Link(dve, dve_done)
            SHR, AND = ALU.logical_shift_right, ALU.bitwise_and
            dve.wait_ge(const_ready, 1)
            for k, (bit, m) in enumerate([(5, 1), (2, 1), (4, 3), (6, 1)]):
                link(dve.tensor_scalar(bits_q[:, k:k + 1], iota_q[:, :], bit, m, SHR, AND))
                if k < 2:
                    link(dve.tensor_scalar(bits_k[:, k, :], iota_k[:, :], bit, m, SHR, AND))
            link(dve.tensor_copy(bits_qf[:, :], bits_q[:, :]))
            link(dve.tensor_copy(bits_kf[:, :, :], bits_k[:, :, :]))
            for g in range(2):
                link(dve.tensor_scalar(gmask[:, g:g + 1], bits_qf[:, 3:4], float(g), SCALE, ALU.is_equal, ALU.mult))
                link(dve.memset(half_mask[:, g, :], 0.0))
                link(dve.tensor_scalar(half_mask[:, g, :], half_mask[:, g, :], bits_qf[:, 3:4], float(g),
                                       ALU.add, ALU.is_equal))
            for k in range(NH):
                link(dve.tensor_scalar(hmask[:, k:k + 1], bits_qf[:, 2:3], float(k), None, ALU.is_equal))
            for k in range(2):
                link(dve.tensor_scalar(cut[:, k, :], bits_kf[:, k, :], bits_qf[:, k:k + 1], -100.0,
                                       ALU.not_equal, ALU.mult))
            link(dve.tensor_tensor(cut[:, 2, :], cut[:, 0, :], cut[:, 1, :], ALU.min))
            dve.wait_ge(const_in, 16 * N_CONST)
            link(dve.tensor_copy(bias[:, 0, 0, :, :], table[:, ::-1, :].rearrange("p k h -> p h k")))
            for row, col, which in ((0, 1, 1), (1, 0, 0), (1, 1, 2)):
                link(dve.tensor_tensor(bias[:, row, col, :, :], bias[:, 0, 0, :, :],
                                       cut[:, which, :].unsqueeze(1).to_broadcast([128, NH, 64]), ALU.add))
            dve.sem_inc(bias_ready, 1)

            dve.wait_ge(bias_ready, 1)

            def save_v(s, j):
                dve.wait_ge(qkv_ready, s + 2)
                dve.wait_ge(pv_ready, s + 1)
                m = half_mask[:, :, :].rearrange("p a d -> p (a d)").unsqueeze(1).to_broadcast([128, STEP * 4, 32])
                dve.tensor_tensor(vs[:, j, :, :].rearrange("p w (a d) -> p (w a) d", d=32),
                                  pV[:, :, :].rearrange("p w (a d) -> p (w a) d", d=32), m,
                                  ALU.mult).then_inc(v_saved, 1)

            def softmax_shift(s, j, last):
                dve.wait_ge(scores_ready, s + 2)
                dve.wait_ge(probs_turned, s + 1)
                e, f = sc[:, j % 2, :, :, :], pS[:, :, :, :]
                n = STEP - 1 if j == NSTEP - 1 else STEP
                if n < STEP:
                    dve.tensor_tensor(e[:, n, :, :], f[:, n, :, :], bias[:, int(last), 1, :, :], ALU.add)
                r = bias[:, int(last), 0, :, :].rearrange("p h k -> p (h k)").unsqueeze(1).to_broadcast([128, n, NH * 64])
                dve.tensor_tensor(e[:, 0:n, :, :].rearrange("p w h k -> p w (h k)"),
                                  f[:, 0:n, :, :].rearrange("p w h k -> p w (h k)"), r,
                                  ALU.add).then_inc(scores_read, 1)
                dve.wait_ge(scores_read, s + 2)
                dve.tensor_reduce(mx[:, :, :], e, AX.X, ALU.max).then_inc(max_ready, 1)
                dve.wait_ge(max_ready, s + 1)
                dve.tensor_tensor(e, e, mx[:, :, :].unsqueeze(3).to_broadcast([128, STEP, NH, 64]),
                                  ALU.subtract).then_inc(shifted, 1)

            def softmax_sum(u, j):
                dve.wait_ge(exp_ready, u + 1)
                dve.tensor_reduce(sm[:, j % 2, 0, :, :], sc[:, j % 2, :, :, :], AX.X, ALU.add).then_inc(row_sums, 1)
                dve.wait_ge(row_sums, u + 1)
                dve.reciprocal(sm[:, j % 2, 1, :, :], sm[:, j % 2, 0, :, :]).then_inc(sum_ready, 1)

            def center(m, half, k):
                rows = slice(4 * half, 4 * half + 4)
                dve.wait_ge(mean_ready, 2 * m + half + 1)
                dve.wait_ge(h_doubled, m + 1)
                dve.tensor_tensor(xc[:, rows, :], xs[:, k, rows, :],
                                  pL[:, :].rearrange("p (r c) -> p r c", c=W), ALU.subtract).then_inc(centered, 1)

            def write_h(m, par, done):
                dve.wait_ge(rstd_ready, m + 1)
                dve.wait_ge(qkv_ready, done + 1)
                normalised(dve, par, 0).then_inc(h_ready, 1)

            def begin(bp, n):
                for half in range(2):
                    center(n, half, 0)
                write_h(n, 0, NSTEP * n)
                save_v(NSTEP * n, 0)

            def strip(bp, i, n, k, first, last):
                def body(s, j, after, back1, back2):
                    if back1:
                        softmax_sum(*back1[0:2])
                    if j == 1 and not last:
                        center(n + 1, 1, (k + 1) % NX)
                    softmax_shift(s, j, last)
                    if j == 2 and not last:
                        write_h(n + 1, (k + 1) % 2, NSTEP * n)
                    if after:
                        save_v(*after[0:2])
                    if j == 0 and not last:
                        center(n + 1, 0, (k + 1) % NX)
                steps(n, k, first, last, body)

            def end(bp, n):
                softmax_sum(NSTEP * n - 1, NSTEP - 1)

            over_strips(dve, begin, strip, end)

        @block.scalar
        def _(act):
            act.wait_ge(w_turned, 1)
            act.activation(w_cols[:, :, :].rearrange("p m c -> p (m c)"), pL[:, :], ACT.Copy).then_inc(w_ready, 1)

            def save_qk(s, j):
                act.wait_ge(qkv_ready, s + 2)
                act.wait_ge(scores_ready, s + 1)
                for g in range(2):
                    act.activation(qs[:, :, g, :], pQK[:, 0, :].rearrange("p (w q) -> p w q", q=64), ACT.Copy,
                                   scale=gmask[:, g:g + 1])
                for k in range(NH):
                    ins = act.activation(ks[:, k, :], pQK[:, 1, :], ACT.Copy, scale=hmask[:, k:k + 1])
                ins.then_inc(qk_saved, 1)

            def exponential(s, j):
                act.wait_ge(shifted, s + 1)
                e = sc[:, j % 2, :, :, :]
                act.activation(e, e, ACT.Exp).then_inc(exp_ready, 1)

            def save_probs(u):
                act.wait_ge(probs_turned, u + 3)
                act.wait_ge(pv_ready, u + NSTEP)
                act.activation(pt[:, :, :, :], pT[:, :, :, :], ACT.Copy).then_inc(pt_saved, 1)

            def save_values(u):
                act.wait_ge(pv_ready, u + NSTEP + 1)
                act.wait_ge(proj_ready, u + 1)
                act.activation(ov[:, :], pO[:, 0, :], ACT.Copy).then_inc(ov_saved, 1)

            def save_proj(u, j, n, par):
                act.wait_ge(proj_ready, u + 2)
                if j == 0:
                    act.wait_ge(x1_ready, n + NX - 1)
                cols = yr[:, par, :, 4 * 8 * j:4 * 8 * j + 32].rearrange("p r (w c) -> p w r c", c=WS)
                act.activation(cols, pO[:, 1, :].rearrange("p (w r c) -> p w r c", w=STEP, r=WS), ACT.Identity,
                               bias=pb[:, 0:1]).then_inc(yr_ready, 1)

            def square(m, half):
                rows = slice(4 * half, 4 * half + 4)
                act.wait_ge(centered, 2 * m + half + 1)
                act.activation(sq[:, rows, :], xc[:, rows, :], ACT.Square).then_inc(squared, 1)

            def log(m, half):
                rows = slice(4 * half, 4 * half + 4)
                act.wait_ge(var_ready, 2 * m + half + 1)
                act.activation(sq[:, rows, :].rearrange("p r c -> p (r c)"), pL[:, :], ACT.Ln,
                               bias=eps[:, 0:1]).then_inc(log_ready, 1)

            def root(m):
                act.wait_ge(log_ready, 2 * m + 2)
                act.activation(sq[:, :, :], sq[:, :, :], ACT.Exp, scale=-0.5).then_inc(rstd_ready, 1)

            def save_turned(q, par, half):
                act.wait_ge(x1_turned, 2 * q + half + 2)
                act.wait_ge(stored[par], 32 * (q - par) + 16)
                act.activation(xt[:, par, 4 * half:4 * half + 4, :].rearrange("p r c -> p (r c)"), pL[:, :],
                               ACT.Copy).then_inc(xt_saved, 1)

            def begin(bp, n):
                for half in range(2):
                    square(n, half)
                for half in range(2):
                    log(n, half)
                root(n)
                save_qk(NSTEP * n, 0)

            def strip(bp, i, n, k, first, last):
                def body(s, j, after, back1, back2):
                    if j == 2 and not last:
                        log(n + 1, 1)
                        root(n + 1)
                    if j == 3 and not first:
                        save_turned(n - 1, (k - 1) % 2, 0)
                    if after:
                        save_qk(*after[0:2])
                    if back2:
                        save_values(back2[0])
                    if j == 1 and not last:
                        square(n + 1, 1)
                    exponential(s, j)
                    if back1:
                        save_probs(back1[0])
                    if back2:
                        save_proj(*back2)
                    if j == 0 and not last:
                        square(n + 1, 0)
                    if j == 1 and not last:
                        log(n + 1, 0)
                    if j == 3 and not first:
                        save_turned(n - 1, (k - 1) % 2, 1)
                steps(n, k, first, last, body)

            def end(bp, n):
                s = NSTEP * n
                save_values(s - 2)
                save_probs(s - 1)
                save_proj(s - 2, NSTEP - 2, n - 1, 1)
                save_values(s - 1)
                save_proj(s - 1, NSTEP - 1, n - 1, 1)
                for half in range(2):
                    save_turned(n - 1, 1, half)

            over_strips(act, begin, strip, end)

        @block.tensor
        def _(pe):
            pe.wait_ge(const_ready, 1)
            pe.wait_ge(const_in, 16 * N_CONST)
            for m in range(4):
                ins = pe.transpose(pL[:, 128 * m:128 * m + 128], w_rows[:, m, :], ident[:, :])
            ins.then_inc(w_turned, 1)
            pe.wait_ge(w_ready, 1)

            def qkv(s, j, par, n=None):
                ht = h[:, par, STEP * j:STEP * j + STEP, :, :, :].rearrange("p w t r c -> p w t (r c)")
                if j == 0:
                    pe.wait_ge(h_ready, n + 1)
                    pe.wait_ge(h_doubled, n + 2)
                for m in range(2):
                    pe.matmul(pQK[:, m, :], w_cols[:, m, :], ht[:, :, 0, :], start=True, stop=True)
                pe.wait_ge(v_saved, s + 1)
                for w in range(STEP):
                    keys = ht[:, w, :, :].rearrange("p t q -> p (t q)")
                    ins = pe.matmul(pV[:, w, :], keys, w_cols[:, 2, :], start=True, stop=True)
                ins.then_inc(qkv_ready, 1)

            def scores(s):
                pe.wait_ge(qk_saved, s + 1)
                pe.wait_ge(scores_read, s + 1)
                for w in range(STEP):
                    ins = pe.matmul(pS[:, w, :, :], qs[:, w, :, :].rearrange("p g q -> p (g q)"), ks[:, :, 64 * w:64 * w + 64],
                                    start=True, stop=True)
                ins.then_inc(scores_ready, 1)

            def turn_probs(u, j):
                pe.wait_ge(probs_ready, u + 1)
                pe.wait_ge(pt_saved, u + 1)
                for w in range(STEP):
                    for hp in range(2):
                        ins = pe.transpose(pT[:, w, hp, :], sc[:, j % 2, w, 2 * hp:2 * hp + 2, :], ident[:, :])
                ins.then_inc(probs_turned, 1)

            def values(u, j):
                pe.wait_ge(pt_saved, u + 2)
                pe.wait_ge(yr_ready, u + 1)
                for w in range(STEP):
                    for g in range(2):
                        for hp in range(2):
                            o = 64 * g + 32 * hp
                            ins = pe.matmul(pO[o:o + 32, 0, 64 * w:64 * w + 64], vs[:, j, w, o:o + 32],
                                            pt[:, w, hp, 64 * g:64 * g + 64], start=True, stop=True)
                ins.then_inc(pv_ready, 1)

            def project(u):
                pe.wait_ge(ov_saved, u + 1)
                pe.matmul(pO[:, 1, :], w_cols[:, 3, :], ov[:, :], start=True, stop=True).then_inc(proj_ready, 1)

            def mean(m, half, k):
                pe.wait_ge(x_in[k], 8 * (m - k) + 32)
                if half == 1:
                    pe.wait_ge(centered, 2 * m + 1)
                pe.matmul(pL[:, :], mean_w[:, :], xs[:, k, 4 * half:4 * half + 4, :], start=True,
                          stop=True).then_inc(mean_ready, 1)

            def variance(m, half):
                pe.wait_ge(squared, 2 * m + half + 1)
                if half == 0:
                    pe.wait_ge(centered, 2 * m + 2)
                else:
                    pe.wait_ge(log_ready, 2 * m + 1)
                pe.matmul(pL[:, :], mean_w[:, :], sq[:, 4 * half:4 * half + 4, :], start=True,
                          stop=True).then_inc(var_ready, 1)

            def turn_out(q, half):
                pe.wait_ge(x1_ready, q + NX + 1)
                pe.wait_ge(xt_saved, 2 * q + half + 2)
                for r in range(4):
                    ins = pe.transpose(pL[:, 128 * r:128 * r + 128], x1[:, 4 * half + r, :], ident[:, :])
                ins.then_inc(x1_turned, 1)

            def begin(bp, n):
                pe.wait_ge(xt_saved, 2 * n + 2)
                for half in range(2):
                    mean(n, half, 0)
                for half in range(2):
                    variance(n, half)
                qkv(NSTEP * n, 0, 0, n)

            def strip(bp, i, n, k, first, last):
                def body(s, j, after, back1, back2):
                    scores(s)
                    if after:
                        qkv(after[0], after[1], after[3], after[2])
                    if j == 0 and not last:
                        if not first:
                            pe.wait_ge(xt_saved, 2 * n)
                        mean(n + 1, 0, (k + 1) % NX)
                    if j == 1 and not last:
                        variance(n + 1, 0)
                    if j == 3 and not first:
                        turn_out(n - 1, 1)
                    if back2:
                        values(*back2[0:2])
                    if back1:
                        turn_probs(*back1[0:2])
                    if back2:
                        project(back2[0])
                    if j == 0 and not last:
                        mean(n + 1, 1, (k + 1) % NX)
                    if j == 1 and not last:
                        variance(n + 1, 1)
                    if j == 2 and not first:
                        if not last:
                            pe.wait_ge(log_ready, 2 * n + 4)
                        turn_out(n - 1, 0)
                steps(n, k, first, last, body)

            def end(bp, n):
                s = NSTEP * n
                values(s - 2, NSTEP - 2)
                turn_probs(s - 1, NSTEP - 1)
                project(s - 2)
                values(s - 1, NSTEP - 1)
                project(s - 1)
                for half in range(2):
                    turn_out(n - 1, half)

            over_strips(pe, begin, strip, end)


def stage_choice_ffn(nc, stage, tok, gate_w, gate_b, weight1, weight2):
    E, K, HID = 32, 8, 256
    TS = 8
    TILE = 128 * TS
    NT = S // TILE
    EPS = 1e-5
    POOL_SCALES = (1, 3)
    with ExitStack() as ctx:
        a = Arena(nc, ctx, stage)
        U32, I32 = mybir.dt.uint32, mybir.dt.int32
        ident = a.sb("ident", [128, 128])
        ones = a.sb("ones", [128, 128])
        tri = a.sb("tri", [128, 128])
        eps = a.sb("eps", [128, 1])
        gate_rows = a.sb("gate_rows", [E, 2, 128])
        gate_cols = a.sb("gate_cols", [128, 2, E])
        gb = a.sb("gb", [128, 1])
        w1 = a.sb("w1", [C + 1, E, HID])
        w2 = a.sb("w2", [128, 2, E, C])
        w2b = a.sb("w2b", [1, E, C])
        logits = a.sb("logits", [128, S])
        xs = a.sb("xs", [128, B, TS, C])
        h = a.sb("h", [128, B, TS, C])
        sq = a.sb("sq", [128, 2, TS, C])
        st = a.sb("st", [128, B, 2, TS])
        ht = a.sb("ht", [128, 2, 512])
        top = a.sb("top", [128, K])
        neg_max = a.sb("neg_max", [128, 1])
        at = a.sb("at", [128, K], U32)
        first = a.sb("first", [128, 1], I32)
        firstf = a.sb("firstf", [128, 1])
        idf = a.sb("idf", [128, K])
        rows_at = a.sb("rows_at", [128, K], U32)
        ex = a.sb("ex", [128, K])
        zsum = a.sb("zsum", [128, 2])
        val = a.sb("val", [128, K])
        rows = a.sb("rows", [128, K, C])
        rn = a.sb("rn", [128, K, C])
        rq = a.sb("rq", [128, K, C])
        rs = a.sb("rs", [128, 2, K])
        pooled = a.sb("pooled", [128, C + 1])
        pooled_t = a.sb("pooled_t", [C + 1, 128])
        hid = a.sb("hid", [128, 2, E, B])
        out_t = a.sb("out_t", [C, 128])
        wt = a.sb("wt", [128, K, C])
        dia = a.sb("dia", [128, K, 128])
        idr = a.sb("idr", [128, K, 128])
        same = a.sb("same", [128, 2, K, 128])
        same_before = a.sb("same_before", [128, 2, 128])
        trash = a.sb("trash", [128, K], I32)
        trashf = a.sb("trashf", [128, K])
        dup = a.sb("dup", [128, K])
        pH = [a.ps(f"pH{i}", [128, 512]) for i in range(2)]
        pG = [a.ps(f"pG{i}", [128, 512]) for i in range(2)]
        pA = a.ps("pA", [128, 512])
        pB = a.ps("pB", [128, 512])
        pC = a.ps("pC", [128, 512])
        pD = a.ps("pD", [128, 512])
        pool_done = a.sem("pool_done")
        dve_done = a.sem("dve_done")
        zeros_ready = a.sem("zeros_ready")
        const_ready = a.sem("const_ready")
        gate_in = a.sem("gate_in")
        w_in = a.sem("w_in")
        gate_turned = a.sem("gate_turned")
        gate_ready = a.sem("gate_ready")
        x_in = [a.sem(f"x_in{i}") for i in range(B)]
        total_ready = a.sem("total_ready")
        mean_ready = a.sem("mean_ready")
        inverted = a.sem("inverted")
        centered = a.sem("centered")
        squared = a.sem("squared")
        var_ready = a.sem("var_ready")
        std_ready = a.sem("std_ready")
        h_ready = [a.sem(f"h_ready{i}") for i in range(B)]
        h_turned = a.sem("h_turned")
        ht_saved = a.sem("ht_saved")
        gates_ready = a.sem("gates_ready")
        logits_saved = a.sem("logits_saved")
        top_ready = a.sem("top_ready")
        found = a.sem("found")
        exp_ready = a.sem("exp_ready")
        at_ready = a.sem("at_ready")
        rows_in = a.sem("rows_in")
        row_step = a.sem("row_step")
        row_act = a.sem("row_act")
        pooled_ready = a.sem("pooled_ready")
        pooled_turned = a.sem("pooled_turned")
        pooled_saved = a.sem("pooled_saved")
        hid_ready = a.sem("hid_ready")
        gelu_ready = a.sem("gelu_ready")
        out_ready = a.sem("out_ready")
        out_saved = a.sem("out_saved")
        out_turned = a.sem("out_turned")
        wt_ready = a.sem("wt_ready")
        dia_ready = a.sem("dia_ready")
        idr_ready = a.sem("idr_ready")
        same_ready = a.sem("same_ready")
        summed = a.sem("summed")
        new_rows = a.sem("new_rows")
        scattered = a.sem("scattered")
        block = ctx.enter_context(nc.Block())
        NGATE, NW = 6, 3

        @block.sync
        def _(sp):
            sp.wait_ge(zeros_ready, 1)
            for p in range(2):
                sp.dma_start(gate_rows[:, p, 64 * p:64 * p + 64], gate_w).then_inc(gate_in, 16)
            for b in range(B):
                sp.dma_start(gb[E * b:E * b + E, :], gate_b.rearrange("(e a) -> e a", a=1)).then_inc(gate_in, 16)
            with sp.Fori(0, NT) as t:
                for b in range(B):
                    sp.wait_ge(centered, B * t + b + 1)
                    sp.dma_start(xs[:, b, :, :], tok[bass.ds(b * S + t * TILE, TILE), :].rearrange(
                        "(p j) c -> p j c", j=TS)).then_inc(x_in[b], 16)
            sp.dma_start(w1[:, :, :], weight1.rearrange("e d h -> d e h")).then_inc(w_in, 16)
            for m in range(2):
                sp.dma_start(w2[:, m, :, :], weight2[:, 128 * m:128 * m + 128, :].rearrange(
                    "e h o -> h e o")).then_inc(w_in, 16)
            sp.dma_start(w2b[:, :, :], weight2[:, HID:HID + 1, :].rearrange("e a o -> a e o")).then_inc(w_in, 16)

        @block.gpsimd
        def _(pool):
            link = Link(pool, pool_done)
            for s in (var_ready, gates_ready, ht_saved, logits_saved):
                pool.sem_inc(s, 1)
            pool.sem_inc(var_ready, 1)
            pool.memset(gate_rows[:, :, :], 0.0).then_inc(zeros_ready, 1)
            pool.memset(ones[:, :], 1.0)
            pool.memset(eps[:, :], EPS)
            pool.memset(pooled[:, C:C + 1], 1.0)
            link(pool.memset(tri[:, :], 1.0))
            link(pool.affine_select(out=tri[:, :], in_=tri[:, :], compare_op=ALU.is_gt, fill=0.0, base=0,
                                    pattern=[[1, 128]], channel_multiplier=-1))
            eye(pool, link, ident[:, :])
            link(pool.iota(trash[:, :], pattern=[[1, K]], base=B * S, channel_multiplier=K))
            pool.iota(first[:, :], pattern=[[0, 1]], base=0, channel_multiplier=1).then_inc(const_ready, 1)
            pool.sem_inc(centered, 4)
            pool.sem_inc(h_turned, 2)

            def center(t, b, n):
                pool.wait_ge(mean_ready, n + 1)
                pool.wait_ge(h_turned, n + 1)
                pool.tensor_tensor(h[:, b, :, :], xs[:, b, :, :], bcast(st[:, b, 0, :], TS), ALU.subtract).then_inc(centered, 1)

            def pool_scale(t, b, n):
                if b in POOL_SCALES:
                    pool.wait_ge(inverted, n + 1)
                    pool.tensor_tensor(h[:, b, :, :], h[:, b, :, :], bcast(st[:, b, 1, :], TS),
                                       ALU.mult).then_inc(h_ready[b], 1)

            pipelined(pool, NT, [(pool_scale, 0), (center, 3)])
            pool.wait_ge(at_ready, 1)
            for k in range(K):
                pool.indirect_dma_start(rows[:, k, :], None, tok[0:B * S, :],
                                        bass.IndirectOffsetOnAxis(ap=rows_at[:, k:k + 1], axis=0)).then_inc(rows_in, 16)
            pool.wait_ge(new_rows, 1)
            for k in range(K):
                pool.indirect_dma_start(tok[:, :], bass.IndirectOffsetOnAxis(ap=rows_at[:, k:k + 1], axis=0),
                                        rows[:, k, :], None).then_inc(scattered, 16)
            pool.wait_ge(scattered, 16 * K)

        @block.vector
        def _(dve):
            link = Link(dve, dve_done)
            dve.wait_ge(const_ready, 1)
            link(dve.tensor_scalar(first[:, :], first[:, :], 5, 14, ALU.logical_shift_right, ALU.logical_shift_left))
            link(dve.tensor_copy(firstf[:, :], first[:, :]))
            link(dve.tensor_copy(trashf[:, :], trash[:, :]))
            dve.wait_ge(gate_turned, 1)
            dve.tensor_copy(gate_cols[:, :, :].rearrange("p m e -> p (m e)"), pA[:, 0:2 * E]).then_inc(gate_ready, 1)

            def total(t, b, n):
                dve.wait_ge(x_in[b], 16 * (t + 1))
                dve.tensor_reduce(st[:, b, 0, :], xs[:, b, :, :], AX.X, ALU.add).then_inc(total_ready, 1)

            def mean(t, b, n):
                dve.wait_ge(total_ready, n + 1)
                dve.tensor_scalar(st[:, b, 0, :], st[:, b, 0, :], 1.0 / C, None, ALU.mult).then_inc(mean_ready, 1)

            def variance(t, b, n):
                dve.wait_ge(squared, n + 1)
                dve.tensor_reduce(st[:, b, 1, :], sq[:, b % 2, :, :], AX.X, ALU.add).then_inc(var_ready, 1)

            def scale(t, b, n):
                s = st[:, b, 1, :]
                dve.wait_ge(std_ready, n + 1)
                dve.reciprocal(s, s).then_inc(inverted, 1)
                if b not in POOL_SCALES:
                    dve.wait_ge(inverted, n + 1)
                    dve.tensor_tensor(h[:, b, :, :], h[:, b, :, :], bcast(s, TS), ALU.mult).then_inc(h_ready[b], 1)

            pipelined(dve, NT, [(total, 3), (variance, 1), (mean, 3), (scale, 0)])

            dve.wait_ge(logits_saved, 2 * NT + 1)
            link(dve.max(top[:, :], logits[:, :]))
            dve.tensor_scalar(neg_max[:, :], top[:, 0:1], -1.0, None, ALU.mult).then_inc(top_ready, 1)
            link(dve.max_index(at[:, :], top[:, :], logits[:, :]))
            dve.sem_inc(found, 1)
            link(dve.tensor_copy(idf[:, :], at[:, :]))
            link(dve.tensor_scalar(idf[:, :], idf[:, :], firstf[:, 0:1], None, ALU.add))
            dve.tensor_copy(rows_at[:, :], idf[:, :]).then_inc(at_ready, 1)
            for k in range(K):
                ins = dve.tensor_scalar(dia[:, k, :], ident[:, :], idf[:, k:k + 1], None, ALU.mult)
            ins.then_inc(dia_ready, 1)
            dve.wait_ge(exp_ready, 1)
            link(dve.reciprocal(zsum[:, 1:2], zsum[:, 0:1]))
            link(dve.tensor_scalar(val[:, :], ex[:, :], zsum[:, 1:2], None, ALU.mult))
            dve.wait_ge(idr_ready, 1)
            dve.wait_ge(rows_in, 16 * K)
            link(dve.tensor_reduce(rs[:, 0, :], rows[:, :, :], AX.X, ALU.add))
            link(dve.tensor_scalar(rs[:, 0, :], rs[:, 0, :], 1.0 / C, None, ALU.mult))
            link(dve.tensor_tensor(rn[:, :, :], rows[:, :, :], bcast(rs[:, 0, :], K), ALU.subtract))
            link(dve.tensor_tensor(rq[:, :, :], rn[:, :, :], rn[:, :, :], ALU.mult))
            dve.tensor_reduce(rs[:, 1, :], rq[:, :, :], AX.X, ALU.add).then_inc(row_step, 1)
            dve.wait_ge(row_act, 1)
            link(dve.reciprocal(rs[:, 1, :], rs[:, 1, :]))
            link(dve.tensor_tensor(rs[:, 1, :], rs[:, 1, :], val[:, :], ALU.mult))
            link(dve.tensor_tensor(rn[:, :, :], rn[:, :, :], bcast(rs[:, 1, :], K), ALU.mult))
            dve.tensor_reduce(pooled[:, 0:C], rn[:, :, :].rearrange("p k c -> p c k"), AX.X,
                              ALU.add).then_inc(pooled_ready, 1)
            dve.wait_ge(out_turned, 1)
            v = val[:, :].unsqueeze(2).to_broadcast([128, K, C])
            dve.tensor_tensor(wt[:, :, :], v, pD[:, 0:C].unsqueeze(1).to_broadcast([128, K, C]),
                              ALU.mult).then_inc(wt_ready, 1)
            for k in range(K):
                if k >= 2:
                    dve.wait_ge(summed, k - 1)
                link(dve.tensor_scalar(same[:, k % 2, :, :], idr[:, :, :], idf[:, k:k + 1], None, ALU.is_equal))
                dve.tensor_tensor(same_before[:, k % 2, :], same[:, k % 2, k, :], tri[:, :],
                                  ALU.mult).then_inc(same_ready, 1)
            dve.wait_ge(summed, K)
            link(dve.tensor_scalar(dup[:, :], pB[:, 0:K], 0.5, None, ALU.is_gt))
            link(dve.tensor_tensor(trashf[:, :], trashf[:, :], idf[:, :], ALU.subtract))
            link(dve.tensor_tensor(dup[:, :], dup[:, :], trashf[:, :], ALU.mult))
            link(dve.tensor_tensor(dup[:, :], dup[:, :], idf[:, :], ALU.add))
            dve.tensor_copy(rows_at[:, :], dup[:, :])
            dve.tensor_tensor(rows[:, :, :].rearrange("p k c -> p (k c)"), rows[:, :, :].rearrange("p k c -> p (k c)"),
                              pA[:, :], ALU.add).then_inc(new_rows, 1)

        @block.scalar
        def _(act):
            act.wait_ge(const_ready, 1)
            act.wait_ge(gate_in, 16 * NGATE)

            def square(t, b, n):
                act.wait_ge(centered, n + 5)
                act.wait_ge(var_ready, n + 1)
                act.activation(sq[:, b % 2, :, :], h[:, b, :, :], ACT.Square).then_inc(squared, 1)

            def root(t, b, n):
                s = st[:, b, 1, :]
                act.wait_ge(var_ready, n + 3)
                act.activation(s, s, ACT.Sqrt, bias=eps[:, 0:1], scale=1.0 / C).then_inc(std_ready, 1)

            def save(t, b, n):
                act.wait_ge(h_turned, n + 5)
                act.wait_ge(gates_ready, n + 1)
                act.activation(ht[:, b % 2, :], pH[b % 2][:, :], ACT.Copy).then_inc(ht_saved, 1)

            def save_logits(t, b, n):
                if b < B - 1:
                    return
                act.wait_ge(gates_ready, n + 3)
                out = logits[:, bass.ds(t * TILE, TILE)].rearrange("q (p j m) -> q m j p", j=TS // 2, m=2)
                for m in range(2):
                    act.activation(out[:, m, :, :], pG[m][:, :].rearrange("q (j p) -> q j p", p=128), ACT.Identity,
                                   bias=gb[:, 0:1]).then_inc(logits_saved, 1)

            pipelined(act, NT, [(root, 1), (save_logits, -2), (square, 2), (save, -1)])
            act.wait_ge(top_ready, 1)
            act.activation(ex[:, :], top[:, :], ACT.Exp, bias=neg_max[:, 0:1])
            act.wait_ge(at_ready, 1)
            act.activation(logits[:, :], logits[:, :], ACT.Exp, bias=neg_max[:, 0:1],
                           accum_out=zsum[:, 0:1]).then_inc(exp_ready, 1)
            act.wait_ge(dia_ready, 2)
            act.activation(idr[:, 0:4, :].rearrange("p k i -> p (k i)"), pB[:, :], ACT.Copy)
            act.activation(idr[:, 4:8, :].rearrange("p k i -> p (k i)"), pC[:, :], ACT.Copy).then_inc(idr_ready, 1)
            act.wait_ge(row_step, 1)
            act.activation(rs[:, 1, :], rs[:, 1, :], ACT.Sqrt, bias=eps[:, 0:1], scale=1.0 / C).then_inc(row_act, 1)
            act.wait_ge(pooled_turned, 1)
            act.activation(pooled_t[:, :], pD[0:C + 1, 0:128], ACT.Copy).then_inc(pooled_saved, 1)
            act.wait_ge(hid_ready, 1)
            act.activation(hid[:, :, :, :].rearrange("p m e b -> p (m e b)"), pH[0][:, 0:2 * E * B],
                           ACT.Gelu).then_inc(gelu_ready, 1)
            act.wait_ge(out_ready, 1)
            act.activation(out_t[:, :], pH[1][0:C, 0:128], ACT.Copy).then_inc(out_saved, 1)

        @block.tensor
        def _(pe):
            pe.wait_ge(const_ready, 1)
            pe.wait_ge(gate_in, 16 * NGATE)
            for m in range(2):
                ins = pe.transpose(pA[:, E * m:E * m + E], gate_rows[:, m, :], ident[0:E, 0:E])
            ins.then_inc(gate_turned, 1)
            pe.wait_ge(gate_ready, 1)
            pe.sem_inc(h_turned, 2)
            pe.sem_inc(gates_ready, 1)
            pe.sem_inc(ht_saved, 1)

            def turn(t, b, n):
                pe.wait_ge(h_ready[b], t + 1)
                pe.wait_ge(ht_saved, n + 1)
                for j in range(TS // 2):
                    ins = pe.transpose(pH[b % 2][:, 128 * j:128 * j + 128],
                                       h[:, b, 2 * j:2 * j + 2, :].rearrange("p j c -> p (j c)"), ident[:, :])
                ins.then_inc(h_turned, 1)

            def gates(t, b, n):
                pe.wait_ge(ht_saved, n + 3)
                if b == 0:
                    pe.wait_ge(logits_saved, 2 * t + 1)
                for m in range(2):
                    ins = pe.matmul(pG[m][E * b:E * b + E, :], gate_cols[:, m, :], ht[:, b % 2, :],
                                    start=True, stop=True)
                ins.then_inc(gates_ready, 1)

            pipelined(pe, NT, [(turn, 0), (gates, -1)])
            pe.wait_ge(dia_ready, 1)
            for k in range(K):
                ins = pe.matmul([pB, pC][k // 4][:, 128 * (k % 4):128 * (k % 4) + 128], ones[:, :], dia[:, k, :],
                                start=True, stop=True)
            ins.then_inc(dia_ready, 1)
            pe.wait_ge(pooled_ready, 1)
            pe.transpose(pD[0:C + 1, 0:128], pooled[:, :], ident[:, :]).then_inc(pooled_turned, 1)
            pe.wait_ge(pooled_saved, 1)
            pe.wait_ge(w_in, 16 * (NW + 1))
            for e in range(E):
                for m in range(2):
                    o = (m * E + e) * B
                    ins = pe.matmul(pH[0][:, o:o + B], w1[:, e, 128 * m:128 * m + 128],
                                    pooled_t[:, e:128:E], start=True, stop=True)
            ins.then_inc(hid_ready, 1)
            pe.wait_ge(gelu_ready, 1)
            for e in range(E):
                o = pH[1][0:C, e:128:E]
                for m in range(2):
                    pe.matmul(o, w2[:, m, e, :], hid[:, m, e, :], start=(m == 0), stop=False)
                ins = pe.matmul(o, w2b[0:1, e, :], ones[0:1, 0:B], start=False, stop=True)
            ins.then_inc(out_ready, 1)
            pe.wait_ge(out_saved, 1)
            pe.transpose(pD[:, 0:C], out_t[:, :], ident[0:C, 0:C]).then_inc(out_turned, 1)
            pe.wait_ge(wt_ready, 1)
            for j in range(K):
                pe.wait_ge(same_ready, j + 1)
                for k in range(K):
                    pe.matmul(pA[:, C * k:C * k + C], same[:, j % 2, k, :], wt[:, j, :], start=(j == 0 and k == 0),
                              stop=(j == K - 1), skip_group_check=True)
                for k in range(j, K):
                    m = same_before[:, j % 2, :] if k == j else same[:, j % 2, k, :]
                    ins = pe.matmul(pB[:, k:k + 1], m, ones[:, 0:1], start=(j == 0 and k == 0), stop=(k == j),
                                    skip_group_check=True)
                ins.then_inc(summed, 1)


def stage_conv_bn(nc, tok, gamma, beta, w_lbp, w_1x1, b_1x1):
    TS = 8
    TILE = 128 * TS
    R, P2 = TILE // W, W // 2
    NT = S // TILE
    EPS_LN, EPS_BN = 1e-6, 1e-5
    POOL_SCALES = (1, 3)
    with ExitStack() as ctx:
        a = Arena(nc, ctx, "cb")
        ident = a.sb("ident", [128, 128])
        halves = a.sb("halves", [128, 128])
        ones = a.sb("ones", [1, 128])
        brow = a.sb("brow", [1, 2, C])
        bias = a.sb("bias", [128, 1, 2, C])
        eps = a.sb("eps", [128, 2])
        gam = a.sb("gam", [128, 2])
        w_in_rows = a.sb("w_in_rows", [C, C, 9])
        w_rows = a.sb("w_rows", [C, 9, 2, C])
        w_tap = a.sb("w_tap", [128, 9, C])
        wc = a.sb("wc", [128, 3, 2, 128])
        w1_rows = a.sb("w1_rows", [128, 128])
        w1 = a.sb("w1", [128, 128])
        u = a.sb("u", [128, B, H, P2])
        xs = a.sb("xs", [128, B, TS, C])
        h = a.sb("h", [128, B, TS, C])
        sq = a.sb("sq", [128, 2, TS, C])
        st = a.sb("st", [128, B, 2, TS])
        stats = a.sb("stats", [128, B * NT, 6])
        mv = a.sb("mv", [128, 8])
        zero = a.sb("zero", [128, P2 + 2])
        xn = a.sb("xn", [128, 2, R + 2, P2])
        xb = a.sb("xb", [128, 2, R + 2, P2])
        y = a.sb("y", [128, 2, R, P2])
        pH = [a.ps(f"pH{i}", [128, 512]) for i in range(2)]
        pC = [a.ps(f"pC{i}", [128, 512]) for i in range(2)]
        pY = [a.ps(f"pY{i}", [128, 512]) for i in range(2)]
        pool_done = a.sem("pool_done")
        dve_done = a.sem("dve_done")
        zeros_ready = a.sem("zeros_ready")
        const_ready = a.sem("const_ready")
        w_in = a.sem("w_in")
        w_dup = a.sem("w_dup")
        w_turned = a.sem("w_turned")
        w_ready = a.sem("w_ready")
        x_in = [a.sem(f"x_in{i}") for i in range(B)]
        total_ready = a.sem("total_ready")
        mean_ready = a.sem("mean_ready")
        inverted = a.sem("inverted")
        centered = a.sem("centered")
        squared = a.sem("squared")
        var_ready = a.sem("var_ready")
        std_ready = a.sem("std_ready")
        h_ready = [a.sem(f"h_ready{i}") for i in range(B)]
        h_turned = a.sem("h_turned")
        u_saved = a.sem("u_saved")
        stats_ready = a.sem("stats_ready")
        mean_in = a.sem("mean_in")
        mean_out = a.sem("mean_out")
        bn_std = a.sem("bn_std")
        bn_ready = a.sem("bn_ready")
        r_in = [a.sem(f"r_in{i}") for i in range(2)]
        r_biased = a.sem("r_biased")
        xn_ready = a.sem("xn_ready")
        conv_ready = a.sem("conv_ready")
        y_ready = a.sem("y_ready")
        mixed = a.sem("mixed")
        sum_ready = a.sem("sum_ready")
        stored = [a.sem(f"stored{i}") for i in range(2)]
        block = ctx.enter_context(nc.Block())
        NW = 2 + 1 + 4 + 1
        BN_LINKS = 12

        def over_strips(eng, body, link=None, per=0):
            start = (link.base + link.n) if link else 0

            def strip(b, i, n, par, top, bottom):
                if link:
                    link.base, link.n = start + n * per, 0
                body(b, i, n, par, top, bottom)
                assert not link or link.n == per, link.n

            with eng.Fori(0, B) as b:
                strip(b, 0, b * NT, 0, True, False)
                with eng.Fori(0, NT // 2 - 1) as t:
                    for k in range(2):
                        strip(b, 2 * t + 1 + k, b * NT + 2 * t + 1 + k, (1 + k) % 2, False, False)
                strip(b, NT - 1, b * NT + NT - 1, 1, False, True)
            if link:
                link.base, link.n = start + B * NT * per, 0

        def tokens_by_pair(n):
            return tok[bass.ds(n * TILE, TILE), :].rearrange("(q p j) c -> p q (j c)", p=128, j=2)

        @block.sync
        def _(sp):
            sp.dma_start(w_in_rows[:, :, :], w_lbp.rearrange("o i a b -> o i (a b)")).then_inc(w_in, 16)
            sp.dma_start(brow[:, 0, :], b_1x1.rearrange("(a c) -> a c", a=1)).then_inc(w_in, 16)
            sp.wait_ge(zeros_ready, 1)
            for p in range(2):
                part = slice(64 * p, 64 * p + 64)
                sp.dma_start(w1_rows[part, part], w_1x1.rearrange("o i a b -> o (i a b)")).then_inc(w_in, 16)
                sp.dma_start(gam[part, 0:1], gamma.rearrange("(c a) -> c a", a=1)).then_inc(w_in, 16)
                sp.dma_start(gam[part, 1:2], beta.rearrange("(c a) -> c a", a=1)).then_inc(w_in, 16)
            with sp.Fori(0, NT) as t:
                for b in range(B):
                    sp.wait_ge(centered, B * t + b + 1)
                    sp.dma_start(xs[:, b, :, :], tok[bass.ds(b * S + t * TILE, TILE), :].rearrange(
                        "(p j) c -> p j c", j=TS)).then_inc(x_in[b], 16)
            for b in range(B):
                sp.wait_ge(h_ready[b], NT)

            def load(n, par):
                sp.wait_ge(sum_ready, n + 1)
                sp.dma_start(xs[:, par, :, :].rearrange("p (q j) c -> p q (j c)", j=2),
                             tokens_by_pair(n)).then_inc(r_in[par], 16)

            def store(n, par):
                sp.wait_ge(sum_ready, n + 3)
                sp.dma_start(tokens_by_pair(n), h[:, par, :, :].rearrange(
                    "p (q j) c -> p q (j c)", j=2)).then_inc(stored[par], 16)

            load(0, 0)
            with sp.Fori(0, B * NT // 2 - 1) as t:
                for par in range(2):
                    load(2 * t + par + 1, 1 - par)
                    store(2 * t + par, par)
            load(B * NT - 1, 1)
            for par in range(2):
                store(B * NT - 2 + par, par)
            for par in range(2):
                sp.wait_ge(stored[par], 16 * B * NT // 2 + 16)

        @block.gpsimd
        def _(pool):
            link = Link(pool, pool_done)
            for s in (var_ready, conv_ready, u_saved, y_ready):
                pool.sem_inc(s, 1)
            pool.sem_inc(var_ready, 1)
            for s in stored:
                pool.sem_inc(s, 16)
            pool.memset(w1_rows[:, :], 0.0).then_inc(zeros_ready, 1)
            pool.memset(zero[:, :], 0.0)
            pool.memset(xb[:, :, :, :], 0.0)
            pool.memset(wc[:, :, :, :], 0.0)
            pool.memset(eps[:, 0:1], EPS_LN)
            pool.memset(eps[:, 1:2], EPS_BN)
            pool.memset(ones[:, :], 1.0)
            pool.memset(halves[:, :], 0.0)
            eye(pool, link, ident[:, :])
            for k in (0, 64, -64):
                link(pool.affine_select(out=halves[:, :], in_=halves[:, :], compare_op=ALU.not_equal, fill=0.5,
                                        base=k, pattern=[[-1, 128]], channel_multiplier=1))
            pool.sem_inc(const_ready, 1)
            pool.sem_inc(centered, 4)
            pool.sem_inc(h_turned, 2)

            def center(t, b, n):
                pool.wait_ge(mean_ready, n + 1)
                pool.wait_ge(h_turned, n + 1)
                pool.tensor_tensor(h[:, b, :, :], xs[:, b, :, :], bcast(st[:, b, 0, :], TS), ALU.subtract).then_inc(centered, 1)

            def pool_scale(t, b, n):
                if b in POOL_SCALES:
                    pool.wait_ge(inverted, n + 1)
                    pool.tensor_tensor(h[:, b, :, :], h[:, b, :, :], bcast(st[:, b, 1, :], TS),
                                       ALU.mult).then_inc(h_ready[b], 1)

            pipelined(pool, NT, [(pool_scale, 0), (center, 3)])
            pool.sem_inc(sum_ready, 2)
            pool.wait_ge(bn_ready, 1)

            def add_bias(b, i, n, par, top, bottom):
                pool.wait_ge(r_in[par], 8 * (n - par) + 16)
                v = xs[:, par, :, :].rearrange("p (q j) c -> p q (j c)", j=2)
                pool.tensor_tensor(v, v, bias[:, :, :, :].rearrange("p a j c -> p a (j c)").to_broadcast([128, 4, 128]),
                                   ALU.add).then_inc(r_biased, 1)

            over_strips(pool, add_bias)

        @block.vector
        def _(dve):
            link = Link(dve, dve_done)
            dve.wait_ge(w_in, 16 * NW)
            dve.wait_ge(const_ready, 1)
            for d in range(2):
                ins = dve.tensor_copy(w_rows[:, :, d, :], w_in_rows[:, :, :].rearrange("o i k -> o k i"))
            link(dve.tensor_copy(brow[:, 1, :], brow[:, 0, :]))
            dve.sem_inc(w_dup, 1)
            dve.wait_ge(w_turned, 1)
            link(dve.tensor_copy(w_tap[:, 0:8, :].rearrange("p k o -> p (k o)"), pH[0][:, :]))
            link(dve.tensor_copy(w_tap[:, 8, :], pH[1][:, 0:64]))
            dve.tensor_copy(bias[:, 0, :, :].rearrange("p j c -> p (j c)"), pH[1][:, 64:192])
            dve.tensor_copy(w1[:, :], pC[0][:, 0:128])
            for m, pi, po, tap in parity_blocks(3, 1):
                rows, cols = slice(64 * pi, 64 * pi + 64), slice(64 * po, 64 * po + 64)
                ins = dve.tensor_copy(wc[rows, :, abs(m), cols], w_tap[rows, tap:9:3, :])
            ins.then_inc(w_ready, 1)

            def total(t, b, n):
                dve.wait_ge(x_in[b], 16 * (t + 1))
                dve.tensor_reduce(st[:, b, 0, :], xs[:, b, :, :], AX.X, ALU.add).then_inc(total_ready, 1)

            def mean(t, b, n):
                dve.wait_ge(total_ready, n + 1)
                dve.tensor_scalar(st[:, b, 0, :], st[:, b, 0, :], 1.0 / C, None, ALU.mult).then_inc(mean_ready, 1)

            def variance(t, b, n):
                dve.wait_ge(squared, n + 1)
                dve.tensor_reduce(st[:, b, 1, :], sq[:, b % 2, :, :], AX.X, ALU.add).then_inc(var_ready, 1)

            def scale(t, b, n):
                s = st[:, b, 1, :]
                dve.wait_ge(std_ready, n + 1)
                dve.reciprocal(s, s).then_inc(inverted, 1)
                if b not in POOL_SCALES:
                    dve.wait_ge(inverted, n + 1)
                    dve.tensor_tensor(h[:, b, :, :], h[:, b, :, :], bcast(s, TS), ALU.mult).then_inc(h_ready[b], 1)

            def gather_stats(t, b, n):
                dve.wait_ge(u_saved, n + 3)
                dve.bn_stats(stats[:, n, :], u[:, b, bass.ds(t * R, R), :]).then_inc(stats_ready, 1)

            pipelined(dve, NT, [(total, 3), (variance, 1), (mean, 3), (gather_stats, -2), (scale, 0)])
            dve.wait_ge(stats_ready, B * NT)
            mean, var, avg, dev, sc, sh = (mv[:, k:k + 1] for k in range(6))
            link(dve.bn_aggr(mv[:, 0:2], stats[:, :, :].rearrange("p n s -> p (n s)")))
            dve.sem_inc(mean_in, 1)
            dve.wait_ge(mean_out, 1)
            link(dve.tensor_copy(avg, pC[0][:, 0:1]))
            link(dve.tensor_tensor(dev, mean, avg, ALU.subtract))
            link(dve.tensor_tensor(dev, dev, dev, ALU.mult))
            link(dve.tensor_tensor(var, var, dev, ALU.add))
            dve.sem_inc(mean_in, 1)
            dve.wait_ge(bn_std, 1)
            link(dve.reciprocal(sc, sc))
            link(dve.tensor_tensor(sc, sc, gam[:, 0:1], ALU.mult))
            link(dve.tensor_tensor(sh, avg, sc, ALU.mult))
            dve.tensor_tensor(sh, gam[:, 1:2], sh, ALU.subtract).then_inc(bn_ready, 1)

            def add_relu(b, i, n, par):
                dve.wait_ge(conv_ready, n + 3)
                dve.wait_ge(mixed, n + 1)
                dve.scalar_tensor_tensor(y[:, par, :, :].rearrange("p r w -> p (r w)"), pC[par][:, :], 0.0,
                                         u_flat(b, i), ALU.max, ALU.add).then_inc(y_ready, 1)

            def u_flat(b, i):
                return u[:, :, :, :].rearrange("p b r w -> p (b r w)")[:, bass.ds((b * H + i * R) * P2, R * P2)]

            def add_rest(n, par):
                dve.wait_ge(mixed, n + 3)
                dve.wait_ge(r_biased, n + 1)
                dve.wait_ge(stored[par], 8 * (n - par) + 16)
                dve.tensor_tensor(h[:, par, :, :].rearrange("p t c -> p (t c)"),
                                  xs[:, par, :, :].rearrange("p t c -> p (t c)"), pY[par][:, :], ALU.add).then_inc(sum_ready, 1)

            def strip(b, i, n, par, top, bottom):
                add_relu(b, i, n, par)
                add_rest(n, par)

            over_strips(dve, strip)

        @block.scalar
        def _(act):
            act.wait_ge(const_ready, 1)

            def square(t, b, n):
                act.wait_ge(centered, n + 5)
                act.wait_ge(var_ready, n + 1)
                act.activation(sq[:, b % 2, :, :], h[:, b, :, :], ACT.Square).then_inc(squared, 1)

            def root(t, b, n):
                s = st[:, b, 1, :]
                act.wait_ge(var_ready, n + 3)
                act.activation(s, s, ACT.Sqrt, bias=eps[:, 0:1], scale=1.0 / C).then_inc(std_ready, 1)

            def save(t, b, n):
                act.wait_ge(h_turned, n + 5)
                dst = u[:, b, bass.ds(t * R, R), :].rearrange("q r (a j) -> q j r a", j=TS // 2)
                act.activation(dst, pH[b % 2][:, :].rearrange("q (j r a) -> q j r a", j=TS // 2, r=R),
                               ACT.Copy).then_inc(u_saved, 1)

            pipelined(act, NT, [(root, 1), (square, 2), (save, -1)])
            act.wait_ge(mean_out, 2)
            act.activation(mv[:, 4:5], pC[1][:, 0:1], ACT.Sqrt, bias=eps[:, 1:2]).then_inc(bn_std, 1)
            act.wait_ge(bn_ready, 1)

            def normalise(b, i, n, par, top, bottom):
                act.wait_ge(conv_ready, n + 1)
                r0, r1 = int(top), R + 2 - int(bottom)
                kw = dict(bias=mv[:, 5:6], scale=mv[:, 4:5])
                if top or bottom:
                    z = 0 if top else R + 1
                    act.activation(xn[:, par, z, :], zero[:, 0:P2], ACT.Copy)
                    act.activation(xb[:, par, z, :], zero[:, 0:P2], ACT.Copy)
                src = u[:, b, bass.ds(i * R + r0 - 1, r1 - r0), :]
                act.activation(xn[:, par, r0:r1, :], src, ACT.Identity, **kw)
                for p in range(2):
                    rows = slice(64 * p, 64 * p + 64)
                    ins = act.activation(xb[rows, par, r0:r1, p:P2 - 1 + p], u[rows, b, bass.ds(i * R + r0 - 1, r1 - r0),
                                         1 - p:P2 - p], ACT.Identity, bias=mv[rows, 5:6], scale=mv[rows, 4:5])
                ins.then_inc(xn_ready, 1)

            def strip(b, i, n, par, top, bottom):
                normalise(b, i, n, par, top, bottom)

            over_strips(act, strip)

        @block.tensor
        def _(pe):
            pe.wait_ge(const_ready, 1)
            pe.wait_ge(w_dup, 1)
            for k in range(9):
                pe.transpose(pH[k // 8][:, 64 * (k % 8):64 * (k % 8) + 64],
                             w_rows[:, k, :, :].rearrange("o d i -> o (d i)"), ident[0:C, 0:C])
            pe.matmul(pH[1][:, 64:192], ones[:, :], brow[:, :, :].rearrange("a j c -> a (j c)"), start=True, stop=True)
            pe.transpose(pC[0][:, 0:128], w1_rows[:, :], ident[:, :]).then_inc(w_turned, 1)
            pe.wait_ge(w_ready, 1)
            pe.sem_inc(h_turned, 2)
            pe.sem_inc(u_saved, 1)
            pe.sem_inc(y_ready, 1)
            pe.sem_inc(mixed, 2)
            pe.sem_inc(conv_ready, 1)

            def turn(t, b, n):
                pe.wait_ge(h_ready[b], t + 1)
                pe.wait_ge(u_saved, n + 1)
                for j in range(TS // 2):
                    ins = pe.transpose(pH[b % 2][:, 128 * j:128 * j + 128],
                                       h[:, b, 2 * j:2 * j + 2, :].rearrange("p j c -> p (j c)"), ident[:, :])
                ins.then_inc(h_turned, 1)

            pipelined(pe, NT, [(turn, 0)])
            for k in range(2):
                pe.wait_ge(mean_in, k + 1)
                pe.matmul(pC[k][:, 0:1], halves[:, :], mv[:, k:k + 1], start=True, stop=True).then_inc(mean_out, 1)

            def strip(b, i, n, par, top, bottom):
                pe.wait_ge(xn_ready, n + 1)
                pe.wait_ge(y_ready, n + 1)
                for k in range(3):
                    for beside, src in enumerate((xn, xb)):
                        ins = pe.matmul(pC[par][:, :], wc[:, k, beside, :], src[:, par, k:k + R, :],
                                        start=(k == 0 and not beside), stop=(k == 2 and beside == 1))
                ins.then_inc(conv_ready, 1)
                pe.wait_ge(y_ready, n + 3)
                pe.wait_ge(sum_ready, n + 1)
                yt = y[:, par, :, :].rearrange("p r w -> p (r w)")
                for q in range(4):
                    ins = pe.matmul(pY[par][:, 128 * q:128 * q + 128], yt[:, 128 * q:128 * q + 128], w1[:, :],
                                    start=True, stop=True)
                ins.then_inc(mixed, 1)

            over_strips(pe, strip)


def stage_top2_ffn(nc, stage, tok, router_w, router_b, expert_w, expert_b, rows=None, image=None):
    E = 8
    TS = 8
    TILE = 128 * TS
    N = B * S // TILE
    EPS = 1e-5
    BIG = 1e30
    NX = 4
    with ExitStack() as ctx:
        a = Arena(nc, ctx, stage)
        ident = a.sb("ident", [128, 128])
        eps = a.sb("eps", [128, 1])
        order = a.sb("order", [128, E])
        order_i = a.sb("order_i", [128, E], mybir.dt.int32)
        rw = a.sb("rw", [C + 1, E])
        ew = a.sb("ew", [C + 1, E, C])
        xs = a.sb("xs", [128, NX, TS, C])
        h = a.sb("h", [128, 2, TS, C + 1])
        sq = a.sb("sq", [128, TS, C])
        st = a.sb("st", [128, 2, 2, TS])
        ht = a.sb("ht", [C + 1, 2, TS, 128])
        lg = a.sb("lg", [128, TS, E])
        eq = a.sb("eq", [128, TS, E])
        one = a.sb("one", [128, 2, TS, E])
        mx = a.sb("mx", [128, 4, TS])
        ex = a.sb("ex", [128, 2, TS])
        gt = a.sb("gt", [128, 2, TS])
        gates = a.sb("gates", [128, 2, TS, E])
        prod = a.sb("prod", [128, 4, E, C])
        part = a.sb("part", [128, 2, 2, 4, C])
        y = a.sb("y", [128, 2, TS, C]) if rows is None else None
        pT = [a.ps(f"pT{i}", [128, 512]) for i in range(2)]
        pL = a.ps("pL", [128, 512])
        pE = [a.ps(f"pE{i}", [128, 512]) for i in range(4)]
        pool_done = a.sem("pool_done")
        pool_step = a.sem("pool_step")
        dve_done = a.sem("dve_done")
        const_ready = a.sem("const_ready")
        w_in = a.sem("w_in")
        x_in = [a.sem(f"x_in{i}") for i in range(NX)]
        centered = a.sem("centered")
        squared = a.sem("squared")
        var_ready = a.sem("var_ready")
        std_ready = a.sem("std_ready")
        h_ready = a.sem("h_ready")
        h_turned = a.sem("h_turned")
        ht_saved = a.sem("ht_saved")
        logits_ready = a.sem("logits_ready")
        gap_ready = a.sem("gap_ready")
        gap_exp = a.sem("gap_exp")
        experts_ready = a.sem("experts_ready")
        weighted = a.sem("weighted")
        summed = a.sem("summed")
        y_ready = a.sem("y_ready")
        joined = a.sem("joined")
        stored = [a.sem(f"stored{i}") for i in range(2)]
        block = ctx.enter_context(nc.Block())
        UN = 4

        def over_tiles(eng, body, link=None, per=0, tiles=N, left=()):
            loops, rest = divmod(tiles - len(left), UN)
            start = (link.base + link.n) if link else 0

            def tile(n, k):
                if link:
                    link.base, link.n = start + n * per, 0
                body(n, k)
                assert not link or link.n == per, link.n

            with eng.Fori(0, loops) as t:
                for k in range(UN):
                    tile(UN * t + k, k)
            for k in range(rest):
                tile(UN * loops + k, k)
            if link:
                link.base, link.n = start + (tiles - len(left)) * per, 0
            for k, last in enumerate(left):
                last(tiles - len(left) + k, tiles - len(left) + k)

        def columns(n, j, js):
            return rows.rearrange("p c b w -> p (b w) c")[:, bass.ds(TS * n + j, js), :]

        def tokens(n):
            return tok[bass.ds(n * TILE, TILE), :].rearrange("(p j) c -> p j c", j=TS)

        def tokens_of_columns(b, t):
            return tok[bass.ds(b * S, S), :].rearrange("(h w) c -> h w c", h=H)[:, bass.ds(TS * t, TS), :]

        @block.sync
        def _(sp):
            sp.dma_start(rw[0:C, :], router_w).then_inc(w_in, 16)
            sp.dma_start(rw[C:C + 1, :], router_b.rearrange("(a e) -> a e", a=1)).then_inc(w_in, 16)
            sp.dma_start(ew[0:C, :, :], expert_w.rearrange("e d c -> d e c")).then_inc(w_in, 16)
            sp.dma_start(ew[C:C + 1, :, :], expert_b.rearrange("(a e) c -> a e c", a=1)).then_inc(w_in, 16)

            def load(n, k, src):
                sp.wait_ge(y_ready, n + 1)
                sp.dma_start(xs[:, k % NX, :, :], src).then_inc(x_in[k % NX], 16)

            if rows is None:
                def store(n, k):
                    sp.wait_ge(y_ready, n + 5)
                    sp.dma_start(tokens(n), y[:, k % 2, :, :]).then_inc(stored[k % 2], 16)

                def tile(n, k):
                    load(n + 3, k + 3, tokens(n + 3))
                    store(n, k)

                for n in range(3):
                    load(n, n, tokens(n))
                over_tiles(sp, tile, left=[store] * 3)
                for k in range(2):
                    sp.wait_ge(stored[k], 16 * N // 2 + 16)
            else:
                PARTS = 4

                def load_columns(b, t, k):
                    load(N // B * b + NX * t + k, k, tokens_of_columns(b, NX * t + k))

                def store_image(b):
                    sp.wait_ge(y_ready, N // B * b + N // B + NX)
                    for m in range(PARTS):
                        cs = slice(C // PARTS * m, C // PARTS * (m + 1))
                        dst = image[bass.ds(b, 1), cs, :, :].rearrange("a c h w -> h (a c) w")
                        src = rows[:, cs, bass.ds(b, 1), :].rearrange("p c a w -> p c (a w)")
                        sp.dma_start(dst, src).then_inc(stored[0], 16)

                with sp.Fori(0, N // B // NX) as t:
                    for k in range(NX):
                        load_columns(0, t, k)
                with sp.Fori(1, B) as b:
                    for t in range(2):
                        for k in range(NX):
                            load_columns(b, t, k)
                    store_image(b - 1)
                    with sp.Fori(2, N // B // NX) as t:
                        for k in range(NX):
                            load_columns(b, t, k)
                store_image(B - 1)
                sp.wait_ge(stored[0], 16 * B * PARTS + 16)

        @block.gpsimd
        def _(pool):
            link = Link(pool, pool_done)
            for s in (ht_saved, gap_ready):
                pool.sem_inc(s, 1)
            for s in stored:
                pool.sem_inc(s, 16)
            pool.memset(eps[:, :], EPS)
            pool.memset(h[:, :, :, :], 1.0)
            eye(pool, link, ident[:, :])
            pool.iota(order_i[:, :], pattern=[[-1, E]], base=E, channel_multiplier=0).then_inc(const_ready, 1)
            pool.sem_inc(y_ready, 4)
            step = Link(pool, pool_step)

            def combine(n, k):
                for q in range(4):
                    pool.wait_ge(weighted, 8 * n + 2 * q + 6)
                    pq = part[:, q % 2, :, :, :]
                    pr = prod[:, 2 * (q % 2):2 * (q % 2) + 2, :, :]
                    pool.tensor_tensor(pq, pr[:, :, 0:4, :], pr[:, :, 4:8, :], ALU.add).then_inc(summed, 1)
                    pool.wait_ge(summed, 4 * n + q + 3)
                    step(pool.tensor_tensor(pq[:, :, 0:2, :], pq[:, :, 0:2, :], pq[:, :, 2:4, :], ALU.add))
                    step(pool.tensor_tensor(pq[:, :, 0, :], pq[:, :, 0, :], pq[:, :, 1, :], ALU.add))
                    if rows is None and q == 0:
                        pool.wait_ge(stored[k % 2], 8 * (n - k % 2) + 16)
                    dst = y[:, k % 2, 2 * q:2 * q + 2, :] if rows is None else columns(n, 2 * q, 2)
                    ins = pool.tensor_tensor(dst, pq[:, :, 0, :], xs[:, k % NX, 2 * q:2 * q + 2, :], ALU.add)
                ins.then_inc(y_ready, 1)

            over_tiles(pool, combine, step, 8)

        @block.vector
        def _(dve):
            link = Link(dve, dve_done)
            dve.wait_ge(const_ready, 1)
            link(dve.tensor_copy(order[:, :], order_i[:, :]))

            def center(n, k):
                x, s = xs[:, k % NX, :, :], st[:, k % 2, 0, :]
                dve.wait_ge(x_in[k % NX], 16 * ((n - k % NX) // NX + 1))
                if rows is not None:
                    dve.tensor_tensor(x, columns(n, 0, TS), x, ALU.add).then_inc(joined, 1)
                    dve.wait_ge(joined, n + 1)
                link(dve.tensor_reduce(s, x, AX.X, ALU.add))
                link(dve.tensor_scalar(s, s, 1.0 / C, None, ALU.mult))
                dve.wait_ge(h_turned, n + 1)
                dve.tensor_tensor(h[:, k % 2, :, 0:C], x, bcast(s, TS), ALU.subtract).then_inc(centered, 1)

            def spread(n, k):
                dve.wait_ge(squared, n + 1)
                dve.tensor_reduce(st[:, k % 2, 1, :], sq[:, :, :], AX.X, ALU.add).then_inc(var_ready, 1)

            def scale(n, k):
                s = st[:, k % 2, 1, :]
                dve.wait_ge(std_ready, n + 1)
                link(dve.reciprocal(s, s))
                v = h[:, k % 2, :, 0:C]
                dve.tensor_tensor(v, v, bcast(s, TS), ALU.mult).then_inc(h_ready, 1)

            def pick(which, n):
                m, o = mx[:, which, :], one[:, which, :, :]
                link(dve.tensor_reduce(m, lg[:, :, :], AX.X, ALU.max))
                link(dve.tensor_tensor(eq[:, :, :], lg[:, :, :], bcast(m, TS, E), ALU.is_equal))
                link(dve.tensor_tensor(eq[:, :, :], eq[:, :, :], order[:, :].unsqueeze(1).to_broadcast([128, TS, E]),
                                       ALU.mult))
                link(dve.tensor_reduce(mx[:, 2 + which, :], eq[:, :, :], AX.X, ALU.max))
                link(dve.tensor_tensor(o, eq[:, :, :], bcast(mx[:, 2 + which, :], TS, E), ALU.is_equal))

            def route(n, k):
                dve.wait_ge(logits_ready, n + 1)
                link(dve.tensor_copy(lg[:, :, :].rearrange("p t e -> p (t e)"), pL[:, 0:TS * E]))
                pick(0, n)
                link(dve.scalar_tensor_tensor(lg[:, :, :].rearrange("p t e -> p (t e)"),
                                              one[:, 0, :, :].rearrange("p t e -> p (t e)"), -BIG,
                                              lg[:, :, :].rearrange("p t e -> p (t e)"), ALU.mult, ALU.add))
                pick(1, n)
                dve.tensor_tensor(ex[:, k % 2, :], mx[:, 1, :], mx[:, 0, :], ALU.subtract).then_inc(gap_ready, 1)

            def gate(n, k):
                dve.wait_ge(gap_exp, n + 1)
                link(dve.tensor_scalar(gt[:, 0, :], ex[:, k % 2, :], 1.0, None, ALU.add))
                link(dve.reciprocal(gt[:, 0, :], gt[:, 0, :]))
                link(dve.tensor_tensor(gt[:, 1, :], ex[:, k % 2, :], gt[:, 0, :], ALU.mult))
                link(dve.tensor_tensor(one[:, 0, :, :], one[:, 0, :, :], bcast(gt[:, 0, :], TS, E), ALU.mult))
                link(dve.tensor_tensor(one[:, 1, :, :], one[:, 1, :, :], bcast(gt[:, 1, :], TS, E), ALU.mult))
                link(dve.tensor_tensor(gates[:, k % 2, :, :], one[:, 0, :, :], one[:, 1, :, :], ALU.add))

            def weigh(n, k, j0):
                for j in (j0, j0 + 1):
                    dve.wait_ge(experts_ready, 8 * n + j + 1)
                    if j == j0:
                        dve.wait_ge(summed, 4 * n + j // 2 + 1)
                    dve.tensor_tensor(prod[:, j % 4, :, :], pE[j % 4][:, :].rearrange("p (e c) -> p e c", e=E),
                                      bcast(gates[:, k % 2, j, :], E), ALU.mult).then_inc(weighted, 1)

            def tile(n, k, ahead=2):
                if ahead > 1:
                    center(n + 2, k + 2)
                weigh(n, k, 0)
                if ahead > 1:
                    spread(n + 2, k + 2)
                weigh(n, k, 2)
                if ahead > 1:
                    scale(n + 2, k + 2)
                if ahead > 0:
                    route(n + 1, k + 1)
                weigh(n, k, 4)
                if ahead > 0:
                    gate(n + 1, k + 1)
                weigh(n, k, 6)

            for n in range(2):
                center(n, n)
                spread(n, n)
                scale(n, n)
            route(0, 0)
            gate(0, 0)
            over_tiles(dve, tile, link, 3 + 1 + 5 + 1 + 5 + 6,
                       left=[lambda n, k: tile(n, k, 1), lambda n, k: tile(n, k, 0)])

        @block.scalar
        def _(act):
            act.wait_ge(const_ready, 1)

            def spread(n, k):
                act.wait_ge(centered, n + 1)
                act.activation(sq[:, :, :], h[:, k % 2, :, 0:C], ACT.Square).then_inc(squared, 1)
                s = st[:, k % 2, 1, :]
                act.wait_ge(var_ready, n + 1)
                act.activation(s, s, ACT.Sqrt, bias=eps[:, 0:1], scale=1.0 / C).then_inc(std_ready, 1)

            def save_turned(n, k):
                for m in range(2):
                    act.wait_ge(h_turned, n + 3)
                    act.activation(ht[:, k % 2, 4 * m:4 * m + 4, :].rearrange("c t p -> c (t p)"), pT[m][0:C + 1, :],
                                   ACT.Copy).then_inc(ht_saved, 1)

            def gap(n, k):
                act.wait_ge(gap_ready, n + 2)
                act.activation(ex[:, k % 2, :], ex[:, k % 2, :], ACT.Exp).then_inc(gap_exp, 1)

            def tile(n, k, ahead=2):
                if ahead > 0:
                    save_turned(n + 1, k + 1)
                if ahead > 1:
                    spread(n + 2, k + 2)
                if ahead > 0:
                    gap(n + 1, k + 1)

            for n in range(2):
                spread(n, n)
            save_turned(0, 0)
            gap(0, 0)
            over_tiles(act, tile, left=[lambda n, k: tile(n, k, 1), lambda n, k: tile(n, k, 0)])

        @block.tensor
        def _(pe):
            pe.wait_ge(const_ready, 1)
            pe.wait_ge(w_in, 16 * 4)
            pe.sem_inc(h_turned, 2)
            pe.sem_inc(summed, 2)
            pe.sem_inc(weighted, 4)

            def turn(n, k):
                pe.wait_ge(h_ready, n + 1)
                pe.wait_ge(ht_saved, 2 * n + 1)
                for j in range(TS):
                    ins = pe.transpose(pT[j // 4][0:C + 1, 128 * (j % 4):128 * (j % 4) + 128], h[:, k % 2, j, :],
                                       ident[:, :])
                ins.then_inc(h_turned, 1)

            def logits(n, k):
                pe.wait_ge(ht_saved, 2 * n + 3)
                pe.wait_ge(gap_ready, n + 1)
                for j in range(TS):
                    ins = pe.matmul(pL[:, E * j:E * j + E], ht[:, k % 2, j, :], rw[:, :], start=True, stop=True)
                ins.then_inc(logits_ready, 1)

            def experts(n, k, half):
                for j in range(4 * half, 4 * half + 4):
                    pe.wait_ge(weighted, 8 * n + j + 1)
                    pe.matmul(pE[j % 4][:, :], ht[:, k % 2, j, :], ew[:, :, :].rearrange("d e c -> d (e c)"),
                              start=True, stop=True).then_inc(experts_ready, 1)

            def tile(n, k, ahead=2):
                if ahead > 0:
                    turn(n + 1, k + 1)
                experts(n, k, 0)
                if ahead > 0:
                    logits(n + 1, k + 1)
                experts(n, k, 1)

            turn(0, 0)
            logits(0, 0)
            over_tiles(pe, tile, left=[lambda n, k: tile(n, k, 1), lambda n, k: tile(n, k, 0)])


def stage_sweeps(nc, tok, kernels):
    TS = 8
    TILE = 128 * TS
    R, P2 = TILE // W, W // 2
    NT = S // TILE
    KW = 9
    PAD = 2
    EPS = 1e-6
    STEPS = H - 1
    BL = 8
    NB = W // BL
    POOL_SCALES = (1, 3)
    with ExitStack() as ctx:
        a = Arena(nc, ctx, "sw")
        ident = a.sb("ident", [128, 128])
        eps = a.sb("eps", [128, 1])
        k_in = a.sb("k_in", [C, 2, KW, C])
        k_dup = a.sb("k_dup", [C, KW, 2, C])
        k_tap = a.sb("k_tap", [128, KW, C])
        wc = a.sb("wc", [128, 4, 5, 128])
        xs = a.sb("xs", [128, B, TS, C])
        h = a.sb("h", [128, B, TS, C])
        sq = a.sb("sq", [128, 2, TS, C])
        st = a.sb("st", [128, B, 2, TS])
        y = a.sb("y", [128, B, H, P2])
        row = [[a.sb(f"row{p}{c}", [128, 2, P2 + 2 * PAD]) for c in range(2)] for p in range(2)]
        packed = [[a.sb(f"packed{p}{c}", [128, 2, P2]) for c in range(2)] for p in range(2)]
        swap = a.sb("swap", [64, 2, 8, P2])
        xw = a.sb("xw", [128, 2, 2, 2, BL, C])
        pH = [a.ps(f"pH{i}", [128, 512]) for i in range(2)]
        pC = [a.ps(f"pC{i}", [128, 512]) for i in range(2)]
        pT = [a.ps(f"pT{i}", [128, 512]) for i in range(2)]
        pool_done = a.sem("pool_done")
        dve_done = a.sem("dve_done")
        const_ready = a.sem("const_ready")
        k_loaded = [a.sem(f"k_loaded{i}") for i in range(2)]
        k_doubled = a.sem("k_doubled")
        k_turned = a.sem("k_turned")
        k_ready = a.sem("k_ready")
        x_in = [a.sem(f"x_in{i}") for i in range(B)]
        total_ready = a.sem("total_ready")
        mean_ready = a.sem("mean_ready")
        inverted = a.sem("inverted")
        centered = a.sem("centered")
        squared = a.sem("squared")
        var_ready = a.sem("var_ready")
        std_ready = a.sem("std_ready")
        h_ready = [a.sem(f"h_ready{i}") for i in range(B)]
        h_turned = a.sem("h_turned")
        u_saved = a.sem("u_saved")
        row_ready = [a.sem(f"row_ready{c}") for c in range(2)]
        conv_ready = [a.sem(f"conv_ready{c}") for c in range(2)]
        saved = [a.sem(f"saved{c}") for c in range(2)]
        taken = a.sem("taken")
        moved = a.sem("moved")
        put_back = a.sem("put_back")
        pack_ready = [a.sem(f"pack_ready{c}") for c in range(2)]
        turned = [a.sem(f"turned{c}") for c in range(2)]
        added = [a.sem(f"added{c}") for c in range(2)]
        w_loaded = [a.sem(f"w_loaded{i}") for i in range(2)]
        stored = [a.sem(f"stored{i}") for i in range(2)]
        block = ctx.enter_context(nc.Block())
        CHUNKS = B * H // 2 // 8

        def images(c):
            return slice(2 * c, 2 * c + 2)

        def line(sweep, c, i):
            if sweep < 2:
                return y[:, images(c), bass.ds(i, 1), :].rearrange("p b a w -> p b (a w)")
            v = y[:, images(c), :, bass.ds(i[0], 1)].rearrange("p b (h m) a -> p b m (h a)", m=2)
            return v[:, :, i[1], :]

        def over_steps(eng, sweep, body):
            g0 = sweep * STEPS
            par0 = FIRST[sweep]

            def at(t, k):
                if sweep == 1:
                    return t * -2 + (H - 1 - k)
                return 2 * t + k if sweep == 0 else (t + k // 2, k % 2)

            with eng.Fori(0, (STEPS - 1) // 2) as t:
                for k in (1, 2):
                    body(at(t, k), g0 + 2 * t + k, (par0 + k) % 2)
            body(at(STEPS // 2, 1), g0 + STEPS, (par0 + STEPS) % 2)

        FIRST = [0, 1, 0, 1]

        def block_rows(c, w0):
            v = tok[2 * c * S:(2 * c + 2) * S, :].rearrange("(q m w) c -> q m w c", m=2, w=W)
            return v[:, :, bass.ds(w0, BL), :]

        def exchange(n, half, odd):
            b, q = n // (CHUNKS // B), n % (CHUNKS // B)
            v = y[64 * half:64 * half + 64, bass.ds(b, 1), bass.ds(16 * q, 16), :]
            return v.rearrange("p a (r m) w -> p m (a r) w", m=2)[:, odd, :, :]

        def over_chunks(eng, body):
            with eng.Fori(0, CHUNKS // 2) as t:
                for k in range(2):
                    body(2 * t + k, k)

        def over_blocks(eng, body):
            body(0, 0, True)
            with eng.Fori(0, NB // 2 - 1) as t:
                for k in range(2):
                    body(2 * t + 1 + k, (1 + k) % 2, False)
            body(NB - 1, 1, False)

        @block.sync
        def _(sp):
            for k in range(2):
                sp.dma_start(k_in[:, k, :, :], kernels[k].rearrange("o a k i -> o (a k) i")).then_inc(k_loaded[k], 16)
            for k in range(2, 4):
                sp.wait_ge(k_doubled, k - 1)
                sp.dma_start(k_in[:, k % 2, :, :], kernels[k].rearrange("o a k i -> o (a k) i")).then_inc(k_loaded[k % 2], 16)
            with sp.Fori(0, NT) as t:
                for b in range(B):
                    sp.wait_ge(centered, B * t + b + 1)
                    sp.dma_start(xs[:, b, :, :], tok[bass.ds(b * S + t * TILE, TILE), :].rearrange(
                        "(p j) c -> p j c", j=TS)).then_inc(x_in[b], 16)

            def load(w0, buf):
                for c in range(2):
                    for m in range(2):
                        sp.dma_start(xw[:, buf, c, m, :, :], block_rows(c, w0)[:, m, :, :]).then_inc(w_loaded[buf], 16)

            def store(i, w0, buf):
                for c in range(2):
                    sp.wait_ge(added[c], BL * (i + 1) + 1)
                    for m in range(2):
                        sp.dma_start(block_rows(c, w0)[:, m, :, :], xw[:, buf, c, m, :, :]).then_inc(stored[buf], 16)

            load(W - BL, 0)
            load(W - 2 * BL, 1)
            with sp.Fori(0, NB // 2 - 1) as t:
                for buf in range(2):
                    w0 = t * (-2 * BL) + (W - BL * (1 + buf))
                    w2 = t * (-2 * BL) + (W - BL * (3 + buf))
                    store(2 * t + buf, w0, buf)
                    sp.wait_ge(stored[buf], 64 * (t + 1))
                    load(w2, buf)
            for buf in range(2):
                store(NB - 2 + buf, BL * (1 - buf), buf)
            for buf in range(2):
                sp.wait_ge(stored[buf], 64 * NB // 2)

        @block.gpsimd
        def _(pool):
            link = Link(pool, pool_done)
            for s in (var_ready, put_back, u_saved):
                pool.sem_inc(s, 1)
            pool.sem_inc(var_ready, 1)
            for s in pack_ready:
                pool.sem_inc(s, 1)
            for s in added:
                pool.sem_inc(s, 1)
            pool.memset(eps[:, :], EPS)
            pool.memset(wc[:, :, :, :], 0.0)
            for p in range(2):
                for c in range(2):
                    pool.memset(row[p][c][:, :, :], 0.0)
            eye(pool, link, ident[:, :])
            pool.sem_inc(const_ready, 1)
            pool.sem_inc(centered, 4)
            pool.sem_inc(h_turned, 2)

            def center(t, b, n):
                pool.wait_ge(mean_ready, n + 1)
                pool.wait_ge(h_turned, n + 1)
                pool.tensor_tensor(h[:, b, :, :], xs[:, b, :, :], bcast(st[:, b, 0, :], TS), ALU.subtract).then_inc(centered, 1)

            def pool_scale(t, b, n):
                if b in POOL_SCALES:
                    pool.wait_ge(inverted, n + 1)
                    pool.tensor_tensor(h[:, b, :, :], h[:, b, :, :], bcast(st[:, b, 1, :], TS),
                                       ALU.mult).then_inc(h_ready[b], 1)

            pipelined(pool, NT, [(pool_scale, 0), (center, 3)])

        @block.vector
        def _(dve):
            link = Link(dve, dve_done)
            dve.wait_ge(const_ready, 1)
            for s in range(4):
                dve.wait_ge(k_loaded[s % 2], 16 * (s // 2 + 1))
                if s > 0:
                    dve.wait_ge(k_turned, s)
                dve.tensor_copy(k_dup[:, :, 0, :], k_in[:, s % 2, :, :])
                dve.tensor_copy(k_dup[:, :, 1, :], k_in[:, s % 2, :, :]).then_inc(k_doubled, 1)
                dve.wait_ge(k_turned, s + 1)
                link(dve.tensor_copy(k_tap[:, 0:8, :].rearrange("p k o -> p (k o)"), pH[0][:, :]))
                link(dve.tensor_copy(k_tap[:, 8, :], pH[1][:, 0:C]))
                for m, pi, po, tap in parity_blocks(KW, KW // 2):
                    rows, cols = slice(64 * pi, 64 * pi + 64), slice(64 * po, 64 * po + 64)
                    ins = dve.tensor_copy(wc[rows, s, m + 2, cols], k_tap[rows, tap, :])
                ins.then_inc(k_ready, 1)
                dve.wait_ge(k_ready, s + 1)

            def total(t, b, n):
                dve.wait_ge(x_in[b], 16 * (t + 1))
                dve.tensor_reduce(st[:, b, 0, :], xs[:, b, :, :], AX.X, ALU.add).then_inc(total_ready, 1)

            def mean(t, b, n):
                dve.wait_ge(total_ready, n + 1)
                dve.tensor_scalar(st[:, b, 0, :], st[:, b, 0, :], 1.0 / C, None, ALU.mult).then_inc(mean_ready, 1)

            def variance(t, b, n):
                dve.wait_ge(squared, n + 1)
                dve.tensor_reduce(st[:, b, 1, :], sq[:, b % 2, :, :], AX.X, ALU.add).then_inc(var_ready, 1)

            def scale(t, b, n):
                s = st[:, b, 1, :]
                dve.wait_ge(std_ready, n + 1)
                dve.reciprocal(s, s).then_inc(inverted, 1)
                if b not in POOL_SCALES:
                    dve.wait_ge(inverted, n + 1)
                    dve.tensor_tensor(h[:, b, :, :], h[:, b, :, :], bcast(s, TS), ALU.mult).then_inc(h_ready[b], 1)

            pipelined(dve, NT, [(total, 3), (variance, 1), (mean, 3), (scale, 0)])

            def make(sweep, c, i, g, par, r=None):
                dve.wait_ge(conv_ready[c], g)
                if r is None:
                    dve.wait_ge(saved[c], g)
                else:
                    dve.wait_ge(pack_ready[c], r)
                dve.scalar_tensor_tensor(row[par][c][:, :, PAD:PAD + P2],
                                         pC[c][:, 0:2 * P2].rearrange("p (b w) -> p b w", b=2), 0.0,
                                         line(sweep, c, i), ALU.max, ALU.add).then_inc(row_ready[c], 1)

            dve.wait_ge(u_saved, B * NT + 2)
            for sweep in range(3):
                if sweep != 1:
                    for c in range(2):
                        if sweep == 2:
                            dve.wait_ge(put_back, CHUNKS + 1)
                            dve.wait_ge(moved, CHUNKS)
                        dve.tensor_copy(row[0][c][:, :, PAD:PAD + P2], line(sweep, c, 0 if sweep == 0 else (0, 0))).then_inc(row_ready[c], 1)
                over_steps(dve, sweep, lambda i, g, par: [make(sweep, c, i, g, par) for c in range(2)])
                if sweep == 1:
                    for c in range(2):
                        dve.wait_ge(saved[c], 2 * STEPS + 2)
                    def move(n, k):
                        dve.wait_ge(taken, n + 1)
                        lo = exchange(n, 0, 1)
                        dve.tensor_copy(exchange(n, 1, 0), lo).then_inc(moved, 1)
                    over_chunks(dve, move)
            for c in range(2):
                dve.wait_ge(saved[c], 3 * STEPS + 2)

            def add(c, r, s, buf):
                dve.wait_ge(turned[c], r + 1)
                dve.tensor_tensor(xw[:, buf, c, :, BL - 1 - s, :], xw[:, buf, c, :, BL - 1 - s, :],
                                  pT[c][:, 0:128].rearrange("q (m c) -> q m c", m=2), ALU.add).then_inc(added[c], 1)

            def last(i, buf, first):
                pair0 = i * (-BL // 2) + (NB - 1) * (BL // 2)
                dve.wait_ge(w_loaded[buf], 64 * ((i - buf) // 2 + 1))
                for s in range(BL + 1):
                    if s < BL and not (first and s == 0):
                        for c in range(2):
                            make(3, c, (pair0 + (BL - 1 - s) // 2, (BL - 1 - s) % 2), 3 * STEPS + BL * i + s, (FIRST[3] + s) % 2, BL * i + s)
                    if s > 0:
                        for c in range(2):
                            add(c, BL * i + s - 1, s - 1, buf)

            over_blocks(dve, last)

        @block.scalar
        def _(act):
            act.wait_ge(const_ready, 1)

            def square(t, b, n):
                act.wait_ge(centered, n + 5)
                act.wait_ge(var_ready, n + 1)
                act.activation(sq[:, b % 2, :, :], h[:, b, :, :], ACT.Square).then_inc(squared, 1)

            def root(t, b, n):
                s = st[:, b, 1, :]
                act.wait_ge(var_ready, n + 3)
                act.activation(s, s, ACT.Sqrt, bias=eps[:, 0:1], scale=1.0 / C).then_inc(std_ready, 1)

            def save(t, b, n):
                act.wait_ge(h_turned, n + 5)
                dst = y[:, b, bass.ds(t * R, R), :].rearrange("q r (a j) -> q j r a", j=TS // 2)
                act.activation(dst, pH[b % 2][:, :].rearrange("q (j r a) -> q j r a", j=TS // 2, r=R),
                               ACT.Copy).then_inc(u_saved, 1)

            pipelined(act, NT, [(root, 1), (square, 2), (save, -1)])

            def save_row(sweep, c, i, g, par, firsts):
                act.wait_ge(row_ready[c], g + firsts)
                act.activation(line(sweep, c, i), row[par][c][:, :, PAD:PAD + P2], ACT.Copy).then_inc(saved[c], 1)

            for sweep in range(3):
                firsts = 2 if sweep == 2 else 1
                over_steps(act, sweep, lambda i, g, par: [save_row(sweep, c, i, g, par, firsts) for c in range(2)])
                if sweep == 1:
                    for c in range(2):
                        act.wait_ge(saved[c], 2 * STEPS + 2)

                    def take(n, k):
                        act.wait_ge(put_back, n)
                        act.activation(swap[:, k, :, :], exchange(n, 1, 0), ACT.Copy).then_inc(taken, 1)

                    def put(n, k):
                        act.wait_ge(moved, n + 1)
                        act.activation(exchange(n, 0, 1), swap[:, k, :, :], ACT.Copy).then_inc(put_back, 1)

                    act.activation(swap[:, 0, :, :], exchange(0, 1, 0), ACT.Copy).then_inc(taken, 1)
                    with act.Fori(0, CHUNKS // 2 - 1) as t:
                        for k in range(2):
                            take(2 * t + k + 1, 1 - k)
                            put(2 * t + k, k)
                    take(CHUNKS - 1, 1)
                    for k in range(2):
                        put(CHUNKS - 2 + k, k)

            def pack(i, buf, first):
                for s in range(BL):
                    r, par = BL * i + s, (FIRST[3] + s) % 2
                    for c in range(2):
                        act.wait_ge(row_ready[c], 3 * STEPS + 2 + r)
                        if not (first and s < 2):
                            act.wait_ge(turned[c], r - 1)
                        act.activation(packed[par][c][:, :, :], row[par][c][:, :, PAD:PAD + P2],
                                       ACT.Copy).then_inc(pack_ready[c], 1)

            over_blocks(act, pack)

        @block.tensor
        def _(pe):
            pe.wait_ge(const_ready, 1)
            for s in range(4):
                pe.wait_ge(k_doubled, s + 1)
                if s > 0:
                    pe.wait_ge(k_ready, s)
                for k in range(KW):
                    ins = pe.transpose(pH[k // 8][:, C * (k % 8):C * (k % 8) + C],
                                       k_dup[:, k, :, :].rearrange("o d i -> o (d i)"), ident[0:C, 0:C])
                ins.then_inc(k_turned, 1)
            pe.wait_ge(k_ready, 4)
            pe.sem_inc(h_turned, 2)
            pe.sem_inc(u_saved, 1)
            for c in range(2):
                pe.sem_inc(saved[c], 2)

            def turn(t, b, n):
                pe.wait_ge(h_ready[b], t + 1)
                pe.wait_ge(u_saved, n + 1)
                for j in range(TS // 2):
                    ins = pe.transpose(pH[b % 2][:, 128 * j:128 * j + 128],
                                       h[:, b, 2 * j:2 * j + 2, :].rearrange("p j c -> p (j c)"), ident[:, :])
                ins.then_inc(h_turned, 1)

            pipelined(pe, NT, [(turn, 0)])

            def conv(sweep, c, g, par, firsts):
                pe.wait_ge(row_ready[c], g - 1 + firsts)
                for m in range(5):
                    ins = pe.matmul(pC[c][:, 0:2 * P2], wc[:, sweep, m, :], row[1 - par][c][:, :, m:m + P2],
                                    start=(m == 0), stop=(m == 4))
                ins.then_inc(conv_ready[c], 1)

            for sweep in range(3):
                firsts = 2 if sweep == 2 else 1
                over_steps(pe, sweep, lambda i, g, par: [conv(sweep, c, g, par, firsts) for c in range(2)])

            def turn_out(c, r, par):
                pe.wait_ge(pack_ready[c], r + 2)
                pe.wait_ge(added[c], r + 1)
                pe.transpose(pT[c][:, 0:128], packed[par][c][:, :, :].rearrange("p b h -> p (b h)"),
                             ident[:, :]).then_inc(turned[c], 1)

            def last(i, buf, first):
                for s in range(BL + 1):
                    if s < BL and not (first and s == 0):
                        for c in range(2):
                            conv(3, c, 3 * STEPS + BL * i + s, (FIRST[3] + s) % 2, 2)
                    if s > 0:
                        for c in range(2):
                            turn_out(c, BL * i + s - 1, (FIRST[3] + s - 1) % 2)

            over_blocks(pe, last)


def stage_spread(nc, tok, w_d, w_dirs, bns, y):
    IT = 4
    NC = 4
    TS = 8
    NT = W // TS
    EPS_LN, EPS_BN = 1e-6, 1e-3
    SHIFTS = [H // 2 ** (IT - i) for i in range(IT)]
    UP = [(2, -s, 0) for s in SHIFTS]
    RIGHT = [(4, 0, s) for s in SHIFTS]
    LEFT = [(8, 0, -s) for s in SHIFTS]
    CONVS = UP + RIGHT + LEFT
    NP = 9 * len(CONVS) + 8 * IT
    SC, BI = 9 * len(CONVS), 9 * len(CONVS) + 4 * IT
    with ExitStack() as ctx:
        a = Arena(nc, ctx, "sp")
        eps = a.sb("eps", [128, 2])
        par = a.sb("par", [128, C, NP])
        roll = a.sb("roll", [128, IT, 128])
        diag = a.sb("diag", [128, IT + 2, 3, 128])
        cur = a.sb("cur", [128, NC, NP])
        work = a.sb("work", [128, 7168])
        st = a.sb("st", [128, B, 2, TS])
        xs = work[:, 0:2048].rearrange("p (n t c) -> p n t c", n=B, t=TS)
        h = work[:, 2048:4096].rearrange("p (n t c) -> p n t c", n=B, t=TS)
        sq = work[:, 4096:5120].rearrange("p (n t c) -> p n t c", n=2, t=TS)
        x = work[:, 0:2048].rearrange("p (q n) -> p q n", q=NC)
        rel = work[:, 2048:4096].rearrange("p (q n) -> p q n", q=NC)
        band = work[:, 4096:7168].rearrange("p (q n k m) -> p q n k m", q=NC, n=2, k=3)
        raw = y[:, :, :, :].rearrange("p c b w -> p (c b w)")
        NW9 = IT * C * 9
        raw_w = [raw[:, NW9 * d:NW9 * (d + 1)] for d in range(3)]
        raw_bn = raw[:, 3 * NW9:3 * NW9 + 4 * IT * 4 * C].rearrange("p (d i k c) -> p d i k c", d=4, i=IT, k=4)
        raw_d = raw[:, 3 * NW9 + 16 * IT * C:3 * NW9 + 17 * IT * C].rearrange("p (i c) -> p i c", i=IT)
        pC = [a.ps(f"pC{i}", [128, 512]) for i in range(NC)]
        pool_done = a.sem("pool_done")
        dve_done = a.sem("dve_done")
        const_ready = a.sem("const_ready")
        p_in = a.sem("p_in")
        bn_std = a.sem("bn_std")
        x_in = [a.sem(f"x_in{i}") for i in range(B)]
        total_ready = a.sem("total_ready")
        mean_ready = a.sem("mean_ready")
        inverted = a.sem("inverted")
        centered = a.sem("centered")
        squared = a.sem("squared")
        var_ready = a.sem("var_ready")
        std_ready = a.sem("std_ready")
        y_ready = a.sem("y_ready")
        cur_ready = a.sem("cur_ready")
        band_ready = [a.sem(f"band_ready{i}") for i in range(NC)]
        x_ready = [a.sem(f"x_ready{i}") for i in range(NC)]
        conv_ready = [a.sem(f"conv_ready{i}") for i in range(NC)]
        relu_ready = [a.sem(f"relu_ready{i}") for i in range(NC)]
        block = ctx.enter_context(nc.Block())
        ITS = 4 * IT
        GROUPS = C // NC

        def tokens(b, t):
            v = tok[b * S:b * S + S, :].rearrange("(h w) c -> h w c", h=H)
            return v[:, bass.ds(t * TS, TS), :].rearrange("h t c -> h (t c)")

        def columns(n, b, t):
            v = y[:, :, bass.ds(b, 1), bass.ds(TS * t, TS)]
            return v.rearrange("p c a w -> p (a w) c")

        def channel(g, q):
            return y[:, bass.ds(NC * g + q, 1), :, :].rearrange("p a b w -> p (a b w)")

        def spans(dil, kw, roll_w):
            d, s = dil * (kw - 1), roll_w % W
            lo, hi, cut = max(0, -d), min(W, W - d), W - d - s
            return [(p, q, (p + d + s) % W) for p, q in ((lo, min(hi, cut)), (max(lo, cut), hi)) if p < q]

        def dve_adds(i):
            return 0 if i >= IT else 2 if i > 0 else NC

        def add(eng, g, i, q):
            src = x[:, q, :] if i > 0 else channel(g, q)
            out = x[:, q, :] if i < ITS - 1 else channel(g, q)
            return eng.tensor_tensor(out, src, rel[:, q, :], ALU.add)

        @block.sync
        def _(sp):
            for d in range(3):
                sp.dma_start(raw_w[d], w_dirs[d].rearrange("i c a k m -> (i c a k m)").partition_broadcast(128)).then_inc(p_in, 16)
            for d in range(4):
                sp.dma_start(raw_bn[:, d, :, :, :].rearrange("p i k c -> p (i k c)"),
                             bns[d].rearrange("i k c -> (i k c)").partition_broadcast(128)).then_inc(p_in, 16)
            sp.dma_start(raw_d[:, :, :].rearrange("p i c -> p (i c)"),
                         w_d.rearrange("i c a k m -> (i c a k m)").partition_broadcast(128)).then_inc(p_in, 16)

            with sp.Fori(0, NT) as t:
                for b in range(B):
                    sp.wait_ge(centered, B * t + b + 1)
                    sp.dma_start(xs[:, b, :, :].rearrange("p t c -> p (t c)"), tokens(b, t)).then_inc(x_in[b], 16)

        @block.gpsimd
        def _(pool):
            link = Link(pool, pool_done)
            for s in relu_ready:
                pool.sem_inc(s, 1)
            for s in x_ready:
                pool.sem_inc(s, 1)
            pool.memset(eps[:, 0:1], EPS_LN)
            pool.memset(eps[:, 1:2], EPS_BN)
            link(pool.memset(roll[:, :, :], 0.0))
            link(pool.memset(diag[:, :, :, :], 0.0))

            def set_diagonal(m, c0, c1, k):
                link(pool.affine_select(out=m[:, c0:c1], in_=m[:, c0:c1], compare_op=ALU.not_equal, fill=1.0,
                                        base=-c0 - k, pattern=[[-1, c1 - c0]], channel_multiplier=1))

            for i, s in enumerate(SHIFTS):
                for k in (s, s - H):
                    set_diagonal(roll[:, i, :], 0, H, k)
            for i, (dil, s) in enumerate([(d, s) for d, s, _ in UP] + [(RIGHT[0][0], 0), (LEFT[0][0], 0)]):
                for kh in range(3):
                    e = dil * (kh - 1)
                    for k in {e + s, e + s + H if s else e}:
                        set_diagonal(diag[:, i, kh, :], max(0, -e), min(H, H - e), k)
            pool.sem_inc(const_ready, 1)
            pool.sem_inc(centered, 4)
            pool.sem_inc(y_ready, 4)
            pool.sem_inc(var_ready, 2)

            def center(t, b, n):
                pool.wait_ge(mean_ready, n + 1)
                pool.wait_ge(y_ready, n + 1)
                pool.tensor_tensor(h[:, b, :, :], xs[:, b, :, :], bcast(st[:, b, 0, :], TS),
                                   ALU.subtract).then_inc(centered, 1)

            pipelined(pool, NT, [(center, 3)])
            pool.wait_ge(y_ready, B * NT + 4)
            with pool.Fori(0, GROUPS) as g:
                for i in range(ITS):
                    for q in range(dve_adds(i), NC):
                        pool.wait_ge(relu_ready[q], ITS * g + i + 2)
                        add(pool, g, i, q).then_inc(x_ready[q], 1)

        @block.vector
        def _(dve):
            link = Link(dve, dve_done)
            dve.wait_ge(p_in, 16 * 8)
            taps = par[:, :, 0:SC].rearrange("p c (d i k) -> p d i c k", d=3, i=IT)
            for d in range(3):
                w = raw_w[d].rearrange("p (i c k) -> p i c k", i=IT, c=C)
                for i in range(IT):
                    dve.tensor_copy(taps[:, d, i, :, :], w[:, i, :, :])
            scale_v = par[:, :, SC:BI].rearrange("p c (d i) -> p d i c", d=4)
            bias_v = par[:, :, BI:NP].rearrange("p c (d i) -> p d i c", d=4)
            gam, bet, mean, var = (raw_bn[:, :, :, k, :] for k in range(4))
            dve.wait_ge(bn_std, 1)
            link(dve.reciprocal(var, var))
            link(dve.tensor_tensor(gam, gam, var, ALU.mult))
            link(dve.tensor_tensor(mean, mean, gam, ALU.mult))
            link(dve.tensor_tensor(bet, bet, mean, ALU.subtract))
            link(dve.tensor_scalar(bias_v, bet, 2.0, None, ALU.mult))
            link(dve.tensor_scalar(scale_v, gam, 2.0, None, ALU.mult))
            link(dve.tensor_tensor(scale_v[:, 0, :, :], scale_v[:, 0, :, :], raw_d, ALU.mult))

            def total(t, b, n):
                dve.wait_ge(x_in[b], 16 * (t + 1))
                dve.tensor_reduce(st[:, b, 0, :], xs[:, b, :, :], AX.X, ALU.add).then_inc(total_ready, 1)

            def mean(t, b, n):
                dve.wait_ge(total_ready, n + 1)
                dve.tensor_scalar(st[:, b, 0, :], st[:, b, 0, :], 1.0 / C, None, ALU.mult).then_inc(mean_ready, 1)

            def variance(t, b, n):
                dve.wait_ge(squared, n + 1)
                dve.tensor_reduce(st[:, b, 1, :], sq[:, b % 2, :, :], AX.X, ALU.add).then_inc(var_ready, 1)

            def scale(t, b, n):
                s = st[:, b, 1, :]
                dve.wait_ge(std_ready, n + 1)
                dve.reciprocal(s, s).then_inc(inverted, 1)
                dve.wait_ge(inverted, n + 1)
                dve.tensor_tensor(columns(n, b, t), h[:, b, :, :], bcast(s, TS), ALU.mult).then_inc(y_ready, 1)

            pipelined(dve, NT, [(total, 3), (variance, 1), (mean, 3), (scale, 0)])
            dve.wait_ge(y_ready, B * NT + 4)

            def build(q, i, g):
                conv = i - IT
                d, n = (conv if conv < IT else IT + (conv - IT) // IT), i % 2
                if i > IT + 1:
                    dve.wait_ge(conv_ready[q], ITS * g + i - 1)
                written = []
                for kh in range(3):
                    for kw in range(3):
                        m = band[:, q, n, kw, :]
                        tap = 9 * conv + 3 * kh + kw
                        w = cur[:, q, tap:tap + 1]
                        if kh > 0:
                            link.until(written[3 * kh - 3 + kw])
                            ins = dve.scalar_tensor_tensor(m, diag[:, d, kh, :], w, m, ALU.mult, ALU.add)
                        else:
                            ins = dve.tensor_scalar(m, diag[:, d, kh, :], w, None, ALU.mult)
                        if kh < 2:
                            written.append(link.mark(ins))
                ins.then_inc(band_ready[q], 1)

            PER = 6 * NC * 3 * IT
            start = link.base + link.n
            with dve.Fori(0, GROUPS) as g:
                link.base, link.n = start + g * PER, 0
                for q in range(NC):
                    dve.wait_ge(relu_ready[q], ITS * g + 1)
                    dve.tensor_copy(cur[:, q, :], par[:, bass.ds(NC * g + q, 1), :].rearrange(
                        "p a n -> p (a n)")).then_inc(cur_ready, 1)
                dve.wait_ge(cur_ready, NC * g + NC)
                for i in range(IT):
                    for q in range(dve_adds(i)):
                        dve.wait_ge(relu_ready[q], ITS * g + i + 2)
                        add(dve, g, i, q).then_inc(x_ready[q], 1)
                    build(i, IT, g)
                for i in range(IT + 1, ITS):
                    for q in range(NC):
                        build(q, i, g)
                assert link.n == PER
            link.base, link.n = start + GROUPS * PER, 0

        @block.scalar
        def _(act):
            act.wait_ge(const_ready, 1)
            act.wait_ge(p_in, 16 * 8)
            var = raw_bn[:, :, :, 3, :]
            act.activation(var, var, ACT.Sqrt, bias=eps[:, 1:2]).then_inc(bn_std, 1)

            def square(t, b, n):
                act.wait_ge(centered, n + 5)
                act.wait_ge(var_ready, n + 1)
                act.activation(sq[:, b % 2, :, :], h[:, b, :, :], ACT.Square).then_inc(squared, 1)

            def root(t, b, n):
                s = st[:, b, 1, :]
                act.wait_ge(var_ready, n + 3)
                act.activation(s, s, ACT.Sqrt, bias=eps[:, 0:1], scale=1.0 / C).then_inc(std_ready, 1)

            pipelined(act, NT, [(root, 1), (square, 2)])
            act.wait_ge(y_ready, B * NT + 4)
            with act.Fori(0, GROUPS) as g:
                act.wait_ge(cur_ready, NC * g + NC)
                for i in range(ITS):
                    for q in range(NC):
                        act.wait_ge(conv_ready[q], ITS * g + i + 1)
                        if i == 0:
                            act.wait_ge(x_ready[q], ITS * g + 1)
                        act.activation(rel[:, q, :], pC[q][:, :], ACT.Relu, bias=cur[:, q, BI + i:BI + i + 1],
                                       scale=cur[:, q, SC + i:SC + i + 1]).then_inc(relu_ready[q], 1)

        @block.tensor
        def _(pe):
            pe.wait_ge(const_ready, 1)
            pe.wait_ge(y_ready, B * NT + 4)
            with pe.Fori(0, GROUPS) as g:
                for i in range(ITS):
                    for q in range(NC):
                        if i == 0:
                            pe.wait_ge(relu_ready[q], ITS * g + 1)
                        else:
                            pe.wait_ge(x_ready[q], ITS * g + i + 1)
                        if i < IT:
                            pe.matmul(pC[q][:, :], roll[:, i, :], x[:, q, :] if i > 0 else channel(g, q), start=True,
                                      stop=True).then_inc(conv_ready[q], 1)
                            continue
                        pe.wait_ge(band_ready[q], 3 * IT * g + i - IT + 1)
                        dil, _, s = CONVS[i - IT]
                        xq = x[:, q, :].rearrange("p (b w) -> p b w", b=B)
                        out = pC[q][:, :].rearrange("p (b w) -> p b w", b=B)
                        jobs = [(kw, *piece) for kw in (1, 0, 2) for piece in spans(dil, kw, s)]
                        for n, (kw, lo, hi, at) in enumerate(jobs):
                            ins = pe.matmul(out[:, :, lo:hi], band[:, q, i % 2, kw, :], xq[:, :, at:at + hi - lo],
                                            start=(n == 0), stop=(n == len(jobs) - 1), skip_group_check=True)
                        ins.then_inc(conv_ready[q], 1)


def build_program(nc, p, out):
    PICKS = 4 * 32 * 8
    tok = nc.dram_tensor("tokens", (B * S + PICKS, C), FP32, kind="Internal").ap()
    stage_window_attention(nc, p["x"], p["L0_conv_qkv_w"], p["L0_conv_proj_w"], p["L0_conv_proj_b"],
                           p["L0_conv_bias_table"], tok)
    stage_choice_ffn(nc, "c0", tok, *(p["L0_ffn_" + n] for n in ("gate_w", "gate_b", "weight1", "weight2")))
    stage_conv_bn(nc, tok, *(p["L1_conv_" + n] for n in ("gamma", "beta", "w_lbp", "w_1x1", "b_1x1")))
    stage_top2_ffn(nc, "t1", tok, *(p["L1_ffn_" + n] for n in ("router_w", "router_b", "expert_w", "expert_b")))
    stage_sweeps(nc, tok, [p["L2_conv_kernel_" + n] for n in ("td", "dt", "lr", "rl")])
    stage_choice_ffn(nc, "c2", tok, *(p["L2_ffn_" + n] for n in ("gate_w", "gate_b", "weight1", "weight2")))
    with nc.sbuf_tensor("passes", [128, C, B, W], FP32) as passes:
        stage_spread(nc, tok, p["L3_conv_w_d"], [p["L3_conv_w_" + n] for n in "url"],
                     [p["L3_conv_bn_" + n] for n in "durl"], passes)
        stage_top2_ffn(nc, "t3", tok, *(p["L3_ffn_" + n] for n in ("router_w", "router_b", "expert_w", "expert_b")),
                       rows=passes[:, :, :, :], image=out)


def kernel(**inputs):
    import numpy as _np
    import concourse.bacc as _bacc
    from concourse import mybir as _mybir
    from concourse.bass_utils import run_bass_kernel_spmd as _run

    nc = _bacc.Bacc("TRN2", target_bir_lowering=False, num_devices=1)
    arrays, params = {}, {}
    for name, value in inputs.items():
        a = _np.ascontiguousarray(value)
        arrays[f"in_{name}"] = a
        params[name] = nc.dram_tensor(f"in_{name}", a.shape, _mybir.dt.from_np(a.dtype), kind="ExternalInput").ap()
    out = nc.dram_tensor("out", (B, C, H, W), _mybir.dt.float32, kind="ExternalOutput").ap()
    build_program(nc, params, out)
    r = _run(nc, [arrays], core_ids=[0])
    return r.results[0]["out"]
```
